# Optimizing a Trainium2 kernel written in Bass

```python
import numpy as np
import jax
import jax.numpy as jnp

def _softmax(x, axis=-1):
    return jax.nn.softmax(x, axis=axis)

def _gelu(x):
    return jax.nn.gelu(x, approximate=True)

def _silu(x):
    return jax.nn.silu(x)

def _sigmoid(x):
    return jax.nn.sigmoid(x)

def _layernorm(x, axis=-1, eps=1e-05):
    m = jnp.mean(x, axis=axis, keepdims=True)
    v = jnp.var(x, axis=axis, keepdims=True)
    return (x - m) / jnp.sqrt(v + eps)

def _scatter_add(tgt, idx, src, axis=0):
    return tgt.at[idx].add(src)

def _segment_sum(src, seg, n):
    return jax.ops.segment_sum(src, seg, n)
kernel_name = 'mk_xattn_ffn_d2_seqx_r8_bab166'

def setup_inputs(seed: int=0):
    np.random.seed(seed)
    _w = jnp.asarray

    def _rec_inputs():
        import jax
        import jax.numpy as jnp
        _rk = jax.random.key(seed)
        x = 7.22e-05 + 1 * jax.random.normal(jax.random.fold_in(_rk, 1), (16, 128, 256), jnp.float32)
        _lenS = 128 - jax.random.randint(jax.random.fold_in(_rk, 7), (16,), 0, max(1, 128 // 4) + 1, jnp.int32)
        _lenS2 = 128 - jax.random.randint(jax.random.fold_in(_rk, 8), (16,), 0, max(1, 128 // 4) + 1, jnp.int32)
        _ctx_2048P = jax.random.normal(jax.random.fold_in(_rk, 11), (16, 16, 256), jnp.float32)
        _ctx_2048c = jax.random.dirichlet(jax.random.fold_in(_rk, 511), 0.3 * jnp.ones((16,), jnp.float32), (16, 128))
        _ctx_2048t = jnp.einsum('bsk,bkd->bsd', _ctx_2048c, _ctx_2048P)
        _ctx_2048t = _ctx_2048t * jax.lax.rsqrt(jnp.mean(jnp.square(_ctx_2048t)) + 1e-12) * 0.953939
        ctx_2048 = 4.13588e-05 + 0.999923 * (_ctx_2048t + 0.3 * jax.random.normal(jax.random.fold_in(_rk, 611), (16, 128, 256), jnp.float32))
        return (x, ctx_2048)
    x, ctx_2048 = _rec_inputs()

    def _L0_xattn_setup():
        import jax, jax.numpy as jnp
        import numpy as np
        B, S, DIM, HD = (4, 128, 256, 128)
        H = DIM // HD
        GN_EPS = 0.001

        def _decay_masks(n_heads, seq_len):
            gam = 1.0 - 2.0 ** (-5.0 - jnp.arange(n_heads, dtype=jnp.float32))
            idx = jnp.arange(seq_len, dtype=jnp.float32)
            expo = idx[None, :] - idx[:, None]
            D = jnp.where(expo[None, :, :] <= 0, gam[:, None, None] ** expo[None, :, :], 0.0)
            return D / jnp.sqrt(D.sum(axis=-1))[:, None, :]
        key = jax.random.key(seed)
        ks = jax.random.split(key, 8)
        x = jax.random.normal(ks[0], (B, S, DIM), dtype=jnp.float32)
        k = jax.random.normal(ks[1], (B, S, DIM), dtype=jnp.float32)
        v = jax.random.normal(ks[2], (B, S, DIM), dtype=jnp.float32)
        Wh = jax.random.normal(ks[3], (H, HD, HD), dtype=jnp.float32) / np.sqrt(HD)
        wg_w = jax.random.normal(ks[4], (DIM, DIM), dtype=jnp.float32) / np.sqrt(DIM)
        wo_w = jax.random.normal(ks[5], (DIM, DIM), dtype=jnp.float32) / np.sqrt(DIM)
        gn_gamma = jnp.ones((DIM,), dtype=jnp.float32)
        gn_beta = jnp.zeros((DIM,), dtype=jnp.float32)
        return {'x': x, 'k': k, 'v': v, 'Wh': Wh, 'wg_w': wg_w, 'wo_w': wo_w, 'gn_gamma': gn_gamma, 'gn_beta': gn_beta}
    _L0_xattn_all = _L0_xattn_setup()
    _L0_xattn_in = {k: v for k, v in _L0_xattn_all.items() if k in ('Wh', 'wg_w', 'wo_w', 'gn_gamma', 'gn_beta')}
    del _L0_xattn_all

    def _L0_ffn_setup():
        import jax, jax.numpy as jnp
        import numpy as np
        B, L, D = (2, 128, 256)
        E, K = (8, 2)
        H, HS = (176, 352)
        key = jax.random.key(seed)
        ks = jax.random.split(key, 9)
        s = 0.02
        return {'x': jax.random.normal(ks[0], (B, L, D), dtype=jnp.float32), 'gate_w': jax.random.normal(ks[1], (E, D), dtype=jnp.float32) * s, 'w_gate': jax.random.normal(ks[2], (E, D, H), dtype=jnp.float32) * s, 'w_up': jax.random.normal(ks[3], (E, D, H), dtype=jnp.float32) * s, 'w_down': jax.random.normal(ks[4], (E, H, D), dtype=jnp.float32) * s, 'shgate_w': jax.random.normal(ks[5], (D,), dtype=jnp.float32) * s, 'shw_gate': jax.random.normal(ks[6], (D, HS), dtype=jnp.float32) * s, 'shw_up': jax.random.normal(ks[7], (D, HS), dtype=jnp.float32) * s, 'shw_down': jax.random.normal(ks[8], (HS, D), dtype=jnp.float32) * s}
    _L0_ffn_all = _L0_ffn_setup()
    _L0_ffn_in = {k: v for k, v in _L0_ffn_all.items() if k in ('gate_w', 'w_gate', 'w_up', 'w_down', 'shgate_w', 'shw_gate', 'shw_up', 'shw_down')}
    del _L0_ffn_all

    def _L1_xattn_setup():
        import jax, jax.numpy as jnp
        import numpy as np
        B, DIM1, DIM2, LATENT, T = (16, 128, 128, 64, 256)
        LN_EPS = 1e-05
        key = jax.random.key(seed)
        ks = jax.random.split(key, 8)

        def xavier(k, shape):
            fan_out, fan_in = shape
            std = float(np.sqrt(2.0 / (fan_in + fan_out)))
            return jax.random.normal(k, shape, dtype=jnp.float32) * std
        return {'input1': jax.random.normal(ks[0], (B, DIM1, T), dtype=jnp.float32), 'input2': jax.random.normal(ks[1], (B, DIM2, T), dtype=jnp.float32), 'theta_w': xavier(ks[2], (LATENT, DIM2)), 'theta_b': jnp.zeros((LATENT,), jnp.float32), 'phi_w': xavier(ks[3], (LATENT, DIM1)), 'phi_b': jnp.zeros((LATENT,), jnp.float32), 'g_w': xavier(ks[4], (LATENT, DIM1)), 'g_b': jnp.zeros((LATENT,), jnp.float32), 'ln_gamma': jnp.ones((LATENT, T), jnp.float32), 'ln_beta': jnp.zeros((LATENT, T), jnp.float32), 'out_w': xavier(ks[5], (DIM2, LATENT)), 'out_b': jnp.zeros((DIM2,), jnp.float32)}
    _L1_xattn_all = _L1_xattn_setup()
    _L1_xattn_in = {k: v for k, v in _L1_xattn_all.items() if k in ('theta_w', 'theta_b', 'phi_w', 'phi_b', 'g_w', 'g_b', 'ln_gamma', 'ln_beta', 'out_w', 'out_b')}
    del _L1_xattn_all

    def _L1_ffn_setup():
        import jax, jax.numpy as jnp
        import numpy as np
        EPS = 1e-05

        def _quant_weight(w):
            scale = jnp.mean(jnp.abs(w)) + EPS
            wq = jnp.clip(jnp.round(w / scale), -1.0, 1.0)
            return (wq, scale)

        def _quant_act(x):
            s = jnp.max(jnp.abs(x), axis=-1, keepdims=True) / 127.0 + EPS
            xq = jnp.clip(jnp.round(x / s), -128.0, 127.0)
            return (xq, s)

        def _qlinear(x, w):
            wq, ws = _quant_weight(w)
            xq, xs = _quant_act(x)
            y = jnp.einsum('bsi,oi->bso', xq, wq)
            return y * xs * ws
        key = jax.random.key(seed)
        k1, k2, k3, k4 = jax.random.split(key, 4)
        H, I = (256, 1024)
        x = jax.random.normal(k1, (4, 512, H), dtype=jnp.float32)
        w_gate = jax.random.normal(k2, (I, H), dtype=jnp.float32) * (1.0 / np.sqrt(H))
        w_up = jax.random.normal(k3, (I, H), dtype=jnp.float32) * (1.0 / np.sqrt(H))
        w_down = jax.random.normal(k4, (H, I), dtype=jnp.float32) * (1.0 / np.sqrt(I))
        return {'x': x, 'w_gate': w_gate, 'w_up': w_up, 'w_down': w_down}
    _L1_ffn_all = _L1_ffn_setup()
    _L1_ffn_in = {k: v for k, v in _L1_ffn_all.items() if k in ('w_gate', 'w_up', 'w_down')}
    del _L1_ffn_all
    return {'x': x, 'ctx_2048': ctx_2048, 'L0_xattn_Wh': _L0_xattn_in['Wh'], 'L0_xattn_wg_w': _L0_xattn_in['wg_w'], 'L0_xattn_wo_w': _L0_xattn_in['wo_w'], 'L0_xattn_gn_gamma': _L0_xattn_in['gn_gamma'], 'L0_xattn_gn_beta': _L0_xattn_in['gn_beta'], 'L0_ffn_gate_w': _L0_ffn_in['gate_w'], 'L0_ffn_w_gate': _L0_ffn_in['w_gate'], 'L0_ffn_w_up': _L0_ffn_in['w_up'], 'L0_ffn_w_down': _L0_ffn_in['w_down'], 'L0_ffn_shgate_w': _L0_ffn_in['shgate_w'], 'L0_ffn_shw_gate': _L0_ffn_in['shw_gate'], 'L0_ffn_shw_up': _L0_ffn_in['shw_up'], 'L0_ffn_shw_down': _L0_ffn_in['shw_down'], 'L1_xattn_theta_w': _L1_xattn_in['theta_w'], 'L1_xattn_theta_b': _L1_xattn_in['theta_b'], 'L1_xattn_phi_w': _L1_xattn_in['phi_w'], 'L1_xattn_phi_b': _L1_xattn_in['phi_b'], 'L1_xattn_g_w': _L1_xattn_in['g_w'], 'L1_xattn_g_b': _L1_xattn_in['g_b'], 'L1_xattn_ln_gamma': _L1_xattn_in['ln_gamma'], 'L1_xattn_ln_beta': _L1_xattn_in['ln_beta'], 'L1_xattn_out_w': _L1_xattn_in['out_w'], 'L1_xattn_out_b': _L1_xattn_in['out_b'], 'L1_ffn_w_gate': _L1_ffn_in['w_gate'], 'L1_ffn_w_up': _L1_ffn_in['w_up'], 'L1_ffn_w_down': _L1_ffn_in['w_down']}

def reference(x, ctx_2048, L0_xattn_Wh, L0_xattn_wg_w, L0_xattn_wo_w, L0_xattn_gn_gamma, L0_xattn_gn_beta, L0_ffn_gate_w, L0_ffn_w_gate, L0_ffn_w_up, L0_ffn_w_down, L0_ffn_shgate_w, L0_ffn_shw_gate, L0_ffn_shw_up, L0_ffn_shw_down, L1_xattn_theta_w, L1_xattn_theta_b, L1_xattn_phi_w, L1_xattn_phi_b, L1_xattn_g_w, L1_xattn_g_b, L1_xattn_ln_gamma, L1_xattn_ln_beta, L1_xattn_out_w, L1_xattn_out_b, L1_ffn_w_gate, L1_ffn_w_up, L1_ffn_w_down):
    import jax
    import jax.numpy as jnp

    def _L0_xattn_ref(x, k, v, Wh, wg_w, wo_w, gn_gamma, gn_beta):
        import jax, jax.numpy as jnp
        import numpy as np
        B, S, DIM, HD = (4, 128, 256, 128)
        H = DIM // HD
        GN_EPS = 0.001

        def _decay_masks(n_heads, seq_len):
            gam = 1.0 - 2.0 ** (-5.0 - jnp.arange(n_heads, dtype=jnp.float32))
            idx = jnp.arange(seq_len, dtype=jnp.float32)
            expo = idx[None, :] - idx[:, None]
            D = jnp.where(expo[None, :, :] <= 0, gam[:, None, None] ** expo[None, :, :], 0.0)
            return D / jnp.sqrt(D.sum(axis=-1))[:, None, :]
        b, s, dim = x.shape
        h, hd, _ = Wh.shape
        xh = x.reshape(b, s, h, hd)
        kh = k.reshape(b, s, h, hd)
        vh = v.reshape(b, s, h, hd)
        Q = jnp.einsum('bshd,hde->bshe', xh, Wh)
        K = jnp.einsum('bshd,hde->bshe', kh, Wh)
        V = jnp.einsum('bshd,hde->bshe', vh, Wh)
        scores = jnp.einsum('bshe,bthe->bhst', Q, K) / jnp.sqrt(jnp.float32(hd))
        Dn = _decay_masks(h, s)
        masked = scores * Dn[None, :, :, :]
        A = jnp.maximum(jnp.abs(masked.sum(axis=0)), 1.0)
        O = jnp.einsum('hst,bthe->bshe', A, V).reshape(b, s, dim)
        mu = O.mean(axis=-1, keepdims=True)
        var = O.var(axis=-1, keepdims=True)
        Y = (O - mu) / jnp.sqrt(var + GN_EPS) * gn_gamma + gn_beta
        W = jax.nn.relu(x @ wg_w)
        return W * Y @ wo_w

    def _L0_ffn_ref(x, gate_w, w_gate, w_up, w_down, shgate_w, shw_gate, shw_up, shw_down):
        import jax, jax.numpy as jnp
        import numpy as np
        B, L, D = (2, 128, 256)
        E, K = (8, 2)
        H, HS = (176, 352)
        b, l, d = x.shape
        xf = x.reshape(-1, d)
        logits = jnp.einsum('td,ed->te', xf.astype(jnp.float32), gate_w)
        probs = jax.nn.softmax(logits.astype(jnp.float32), axis=-1)
        weights, indices = jax.lax.top_k(probs, K)
        weights = (weights / weights.sum(-1, keepdims=True)).astype(x.dtype)
        onehot = jax.nn.one_hot(indices, E, dtype=x.dtype)
        combine = jnp.einsum('tk,tke->te', weights, onehot)
        g = jnp.einsum('td,edh->teh', xf, w_gate)
        u = jnp.einsum('td,edh->teh', xf, w_up)
        h = jax.nn.silu(g) * u
        out = jnp.einsum('teh,ehd,te->td', h.astype(jnp.float32), w_down.astype(jnp.float32), combine.astype(jnp.float32))
        sgate = jax.nn.sigmoid(xf @ shgate_w)[:, None]
        sh = jax.nn.silu(xf @ shw_gate) * (xf @ shw_up) @ shw_down
        out = out + (sgate * sh).astype(jnp.float32)
        return out.astype(x.dtype).reshape(b, l, d)

    def _L1_xattn_ref(input1, input2, theta_w, theta_b, phi_w, phi_b, g_w, g_b, ln_gamma, ln_beta, out_w, out_b):
        import jax, jax.numpy as jnp
        import numpy as np
        B, DIM1, DIM2, LATENT, T = (16, 128, 128, 64, 256)
        LN_EPS = 1e-05
        theta_x = jnp.einsum('ld,bdt->btl', theta_w, input2) + theta_b
        phi_x = jnp.einsum('ld,bdt->blt', phi_w, input1) + phi_b[:, None]
        scores = jnp.einsum('btl,bls->bts', theta_x, phi_x)
        p = jax.nn.softmax(scores, axis=-1)
        g_x = jnp.einsum('ld,bdt->btl', g_w, input1) + g_b
        t_x = jnp.einsum('bts,bsl->blt', p, g_x)
        mu = jnp.mean(t_x, axis=(1, 2), keepdims=True)
        var = jnp.var(t_x, axis=(1, 2), keepdims=True)
        h = (t_x - mu) * jax.lax.rsqrt(var + LN_EPS) * ln_gamma + ln_beta
        h = jax.nn.relu(h)
        w_t = jnp.einsum('ol,blt->bot', out_w, h) + out_b[None, :, None]
        return w_t + input2

    def _L1_ffn_ref(x, w_gate, w_up, w_down):
        import jax, jax.numpy as jnp
        import numpy as np
        EPS = 1e-05

        def _quant_weight(w):
            scale = jnp.mean(jnp.abs(w)) + EPS
            wq = jnp.clip(jnp.round(w / scale), -1.0, 1.0)
            return (wq, scale)

        def _quant_act(x):
            s = jnp.max(jnp.abs(x), axis=-1, keepdims=True) / 127.0 + EPS
            xq = jnp.clip(jnp.round(x / s), -128.0, 127.0)
            return (xq, s)

        def _qlinear(x, w):
            wq, ws = _quant_weight(w)
            xq, xs = _quant_act(x)
            y = jnp.einsum('bsi,oi->bso', xq, wq)
            return y * xs * ws
        gate = jax.nn.silu(_qlinear(x, w_gate))
        up = _qlinear(x, w_up)
        return _qlinear(gate * up, w_down)
    x = x + _L0_xattn_ref(_layernorm(x, axis=-1), ctx_2048, ctx_2048, L0_xattn_Wh, L0_xattn_wg_w, L0_xattn_wo_w, L0_xattn_gn_gamma, L0_xattn_gn_beta)
    x = x + _L0_ffn_ref(_layernorm(x, axis=-1), L0_ffn_gate_w, L0_ffn_w_gate, L0_ffn_w_up, L0_ffn_w_down, L0_ffn_shgate_w, L0_ffn_shw_gate, L0_ffn_shw_up, L0_ffn_shw_down)
    x = x + _L1_xattn_ref(_layernorm(x, axis=-1), ctx_2048, L1_xattn_theta_w, L1_xattn_theta_b, L1_xattn_phi_w, L1_xattn_phi_b, L1_xattn_g_w, L1_xattn_g_b, L1_xattn_ln_gamma, L1_xattn_ln_beta, L1_xattn_out_w, L1_xattn_out_b)
    x = x + _L1_ffn_ref(_layernorm(x, axis=-1), L1_ffn_w_gate, L1_ffn_w_up, L1_ffn_w_down)
    return x

_drawn_inputs = setup_inputs


def setup_inputs(seed=0):
    import zlib

    import numpy as np

    out = dict(_drawn_inputs(seed))
    spreads = {'L0_xattn_gn_gamma': (1.0, 0.2),
     'L0_xattn_gn_beta': (0.0, 0.1),
     'L1_xattn_theta_b': (0.0, 0.1),
     'L1_xattn_phi_b': (0.0, 2.0),
     'L1_xattn_g_b': (0.0, 0.275),
     'L1_xattn_ln_gamma': (1.0, 0.2),
     'L1_xattn_ln_beta': (0.0, 0.496),
     'L1_xattn_out_b': (0.0, 0.293)}
    factors = {'L0_ffn_gate_w': 6.027,
     'L0_ffn_w_gate': 5.377,
     'L0_ffn_w_up': 5.344,
     'L0_ffn_w_down': 5.219,
     'L0_ffn_shgate_w': 8.0,
     'L0_ffn_shw_gate': 5.287,
     'L0_ffn_shw_up': 5.151,
     'L0_ffn_shw_down': 5.048}
    for name, (base, spread) in spreads.items():
        noise = np.random.default_rng([zlib.crc32(name.encode()), seed]).standard_normal(out[name].shape)
        drawn = base * np.exp(spread * noise) if base else spread * noise
        out[name] = jnp.asarray(drawn.astype(out[name].dtype))
    for name, factor in factors.items():
        out[name] = (out[name] * factor).astype(out[name].dtype)
    return out
```

```python
from contextlib import ExitStack

import concourse.bass as bass
from concourse import mybir

ALU = mybir.AluOpType
ACT = mybir.ActivationFunctionType
AX = mybir.AxisListType
F32 = mybir.dt.float32
F32R = mybir.dt.float32r
BF16 = mybir.dt.bfloat16

P = 128
NB = 16
D = 256
DC = D // P
HEADS, HD = 2, 128
NE, HE, HS = 8, 176, 352
HID = NE * HE + HS
NCH = -(-HID // P)
CH = [min(P, HID - P * j) for j in range(NCH)]
NROUTE = NE + 1
GT = 4
NG = NB // GT
GN = GT * P
WPACK = 2 * DC * HID + NCH * D
WSTEP = WPACK // NB
LAT = 64
INNER = 1024
IC = INNER // P
LN_EPS, GN_EPS, Q_EPS = 1e-5, 1e-3, 1e-5
ROUND = 12582912.0
assert WPACK % NB == 0


def steps(eng, count, stages, peel=0):
    deepest = max(lag for lag, _ in stages)

    def peeled(i):
        for lag, f in stages:
            if 0 <= i - lag < count:
                f((i - lag) // 2, (i - lag) % 2)

    first = max(deepest + deepest % 2 + 2, peel)
    for i in range(first):
        peeled(i)
    with eng.Fori(first // 2, count // 2) as t:
        for u in range(2):
            for lag, f in stages:
                f(t + (u - lag) // 2, (u - lag) % 2)
    for i in range(count, count + deepest):
        peeled(i)


def entry(tile, t, u):
    rest = " ".join("abc"[: len(tile.shape) - 2])
    v = tile.rearrange(f"p (t u) {rest} -> p t u {rest}", u=2)
    return v[:, bass.ds(t, 1), u].rearrange(f"p o {rest} -> p (o {rest.split()[0]}) {' '.join(rest.split()[1:])}")


class Core:

    def __init__(self, nc, stack):
        self.nc, self.stack, self.sems = nc, stack, []

    def sb(self, name, shape, dt=F32, stack=None):
        return (stack or self.stack).enter_context(self.nc.sbuf_tensor(name, shape, dt))

    def sem(self, name):
        self.sems.append(self.nc.alloc_semaphore(name=name))
        return self.sems[-1]

    def sem2(self, name):
        return [self.sem(f"{name}{u}") for u in range(2)]

    def end(self):
        self.nc.all_engine_barrier()
        self.nc.clear_and_free_semaphores(self.sems)
        self.nc.all_engine_barrier()


class Norm:

    def __init__(self, core, name, rows=P):
        self.stats = core.sb(f"{name}_stats", [rows, 2, 6])
        self.mv = core.sb(f"{name}_mv", [rows, 2, 2])
        self.ve = core.sb(f"{name}_ve", [rows, 2])
        self.rstd = core.sb(f"{name}_rstd", [rows, 2])
        self.stats_done = core.sem2(f"{name}_stats_done")
        self.mv_done = core.sem2(f"{name}_mv_done")
        self.ve_done = core.sem2(f"{name}_ve_done")
        self.rstd_done = core.sem2(f"{name}_rstd_done")
        self.h_done = core.sem2(f"{name}_h_done")


def two(ap, n=D):
    return ap[:, 0:n].rearrange("p (c n) -> p c n", c=2)



def norm_stats(dve, n, src, t, u, base=0):
    dve.bn_stats(n.stats[:, u], src).then_inc(n.stats_done[u], 1)


def stats_landed(dve, n, t, u, base=0):
    if not isinstance(t, int):
        dve.wait_ge(n.stats_done[u], t + base + 1)


def norm_aggr(dve, n, t, u, eps, base=0):
    if isinstance(t, int):
        dve.wait_ge(n.stats_done[u], t + base + 1)
    dve.bn_aggr(n.mv[:, u], n.stats[:, u]).then_inc(n.mv_done[u], 1)
    dve.wait_ge(n.mv_done[u], t + base + 1)
    dve.wait_ge(n.rstd_done[u], t + base)
    dve.tensor_scalar(n.ve[:, u:u + 1], n.mv[:, u, 1:2], eps, None, ALU.add).then_inc(n.ve_done[u], 1)


def norm_rstd(pool, n, half, t, u, base=0):
    pool.wait_ge(n.ve_done[u], t + base + 1)
    pool.tensor_tensor(n.rstd[:, u:u + 1], n.ve[:, u:u + 1], half[:, u:u + 1], ALU.pow).then_inc(n.rstd_done[u], 1)


def normalise(dve, n, out, src, t, u, base=0):
    dve.wait_ge(n.rstd_done[u], t + base + 1)
    dve.tensor_scalar(out, src, n.mv[:, u, 0:1], n.rstd[:, u:u + 1], ALU.subtract, ALU.mult).then_inc(n.h_done[u], 1)


def program(nc, a, out, upto="all"):
    with ExitStack() as stack:
        whole = Core(nc, stack)
        bank = [stack.enter_context(nc.psum_tensor(f"bank{i}", [P, 512], F32)) for i in range(8)]
        x = whole.sb("x", [P, NB, D])
        ident = whole.sb("ident", [P, P])
        identb = whole.sb("identb", [P, P], BF16)
        half = whole.sb("half", [P, 2])
        with ExitStack() as part:
            first_layers(nc, a, Core(nc, part), bank, x, ident, identb, half)
        if upto == "B":
            with nc.Block() as block:
                @block.sync
                def _(sp):
                    done = nc.alloc_semaphore(name="done")
                    sp.dma_start(out["x2"], x[:]).then_inc(done, 16)
                    sp.wait_ge(done, 16)
            return
        with ExitStack() as part:
            last_layers(nc, a, out, Core(nc, part), bank, x, ident, identb, half)


def first_layers(nc, a, core, bank, x, ident, identb, half):
    sb, sem, sem2 = core.sb, core.sem, core.sem2
    h = sb("h", [P, 2, D])
    ln, gn = Norm(core, "ln"), Norm(core, "gn")
    s1 = ExitStack()
    v = sb("v", [P, NB, D], F32, s1)
    w = sb("w", [P, NB, D], F32, s1)
    s2 = ExitStack()
    w_hi = sb("w_hi", [P, WPACK], F32R, s2)
    w_lo = sb("w_lo", [P, WPACK], F32R, s2)
    h2_hi = sb("h2_hi", [P, NB, DC, P], F32R, s2)
    h2_lo = sb("h2_lo", [P, NB, DC, P], F32R, s2)
    gates = sb("gates", [3 * NROUTE, NB, P], BF16, s2)
    spread = sb("spread", [3 * NROUTE, NCH * P], BF16, s2)
    before = sb("before", [P, NE, NE], F32, s2)
    s3 = ExitStack()
    w_raw = sb("w_raw", [P, 2, WSTEP], F32, s3)
    ctxT = sb("ctxT", [P, 2, HEADS, P], F32, s3)
    hT = sb("hT", [P, 2, DC, P], F32, s3)
    r = sb("r", [P, 2, HEADS, P], F32, s3)
    wh = sb("wh", [P, HEADS, HD], F32, s3)
    whT = sb("whT", [P, HEADS, HD], F32, s3)
    whwh = sb("whwh", [P, HEADS, HD], F32, s3)
    wg = sb("wg", [P, DC, D], F32, s3)
    wo = sb("wo", [P, DC, D], F32, s3)
    decayT = sb("decayT", [P, HEADS, P], F32, s3)
    attT = sb("attT", [P, HEADS, P], F32, s3)
    gamma = sb("gamma", [P, D], F32, s3)
    beta = sb("beta", [P, D], F32, s3)
    nmr = sb("nmr", [P, 2], F32, s3)
    router = sb("router", [P, DC, P], F32, s3)
    router_hi = sb("router_hi", [P, DC, P], F32R, s3)
    router_lo = sb("router_lo", [P, DC, P], F32R, s3)
    y = sb("y", [P, 2, D], F32, s3)
    yb = sb("yb", [P, 2, D], F32, s3)
    prod = sb("prod", [P, 2, D], F32, s3)
    prodT = sb("prodT", [P, 2, DC, P], F32, s3)

    s3.close()
    s5 = ExitStack()
    silu_g = sb("silu_g", [P, 2, GN], F32, s5)
    act_f = sb("act_f", [P, 2, GN], F32, s5)
    act_hi = sb("act_hi", [P, 2, GN], F32R, s5)
    act_lo = sb("act_lo", [P, 2, GN], F32R, s5)
    gate3 = sb("gate3", [P, NB, 3 * NROUTE], BF16, s5)
    s5.close()
    lgT = v[0:NROUTE, :, 0:P]
    lg = v[:, :, P:P + NROUTE]
    gate = v[:, :, P + 16:P + 16 + NROUTE]
    rest = v[:, :, P + 32:P + 32 + NROUTE]
    above = w[:, :, 0:NE * NE].rearrange("p b (e f) -> p b e f", e=NE)
    equal = w[:, :, NE * NE:2 * NE * NE].rearrange("p b (e f) -> p b e f", e=NE)
    rank = w[:, :, P:P + NE]
    chosen = w[:, :, P + 16:P + 16 + NROUTE]
    mine = w[:, :, P + 32:P + 32 + NE]
    middle = w[:, :, P + 48:P + 49]
    s2.close()
    s1.close()

    consts_in = sem("consts_in")
    cast_in = sem("cast_in")
    x_in = sem2("x_in")
    ctxT_in = sem2("ctxT_in")
    wraw_in = sem2("wraw_in")
    exponents = sem("exponents")
    wh_ready = sem("wh_ready")
    whwh_done = sem("whwh_done")
    hT_done = sem2("hT_done")
    hT_copied = sem2("hT_copied")
    v_done = sem2("v_done")
    v_copied = sem2("v_copied")
    r_done = sem2("r_done")
    r_copied = sem2("r_copied")
    w_done = sem2("w_done")
    w_copied = sem2("w_copied")
    scored = sem2("scored")
    whi_done = sem2("whi_done")
    wlo_done = sem2("wlo_done")
    att_masked = sem("att_masked")
    att_done = sem("att_done")

    router_split = sem("router_split")
    o_done = sem2("o_done")
    nmr_done = sem2("nmr_done")
    y_done = sem2("y_done")
    yg_done = sem2("yg_done")
    yb_done = sem2("yb_done")
    prod_done = sem2("prod_done")
    prodT_done = sem2("prodT_done")
    prodT_copied = sem2("prodT_copied")
    delta_done = sem2("delta_done")
    x1_done = sem2("x1_done")
    h2T_done = sem2("h2T_done")
    h2hi_done = sem2("h2hi_done")
    h2lo_done = sem2("h2lo_done")

    logitsT_done = sem("logitsT_done")
    logitsT_copied = sem("logitsT_copied")
    logits_done = sem("logits_done")
    routing = sem("routing")
    tanh_done = sem("tanh_done")
    gate3_done = sem("gate3_done")
    gatesT_done = sem("gatesT_done")
    gatesT_copied = sem("gatesT_copied")
    g_done = sem2("g_done")
    u_done = sem2("u_done")
    spread_done = sem2("spread_done")
    silu_done = sem2("silu_done")
    su_done = sem2("su_done")
    act_done = sem2("act_done")
    acthi_done = sem2("acthi_done")
    actlo_done = sem2("actlo_done")
    down_done = sem2("down_done")
    x2_done = sem("x2_done")

    psT, psV, psR, psW = [bank[0], bank[1]], bank[2], bank[3], bank[4]
    psS = [bank[5], bank[6]]
    psO, psPT, psD, psHT = [bank[0], bank[1]], bank[2], bank[3], [bank[4], bank[7]]

    psG, psU, psC, psY = bank[0:2], bank[2:4], bank[4:6], bank[6:8]

    def tokens(ap, g, c):
        return ap[:].rearrange("p (g b) c s -> p g b c s", g=NG)[:, bass.ds(g, 1), :, c].rearrange("p o b s -> p (o b) s")

    core.stack.callback(core.end)
    block = core.stack.enter_context(nc.Block())

    ROUTED = 12

    @block.sync
    def _(sp):
        for dst, src in ((ident, "ident"), (whT, "whT"), (wh, "wh")):
            sp.dma_start(dst[:], a[src]).then_inc(consts_in, 16)
        for dst, src in ((wg, "wg"), (decayT, "decayT"), (wo, "wo"), (gamma, "gamma"), (beta, "beta"), (router, "router"), (before, "before")):
            sp.dma_start(dst[:], a[src]).then_inc(consts_in, 16)

        def load_x(t, u):
            sp.wait_ge(x_in[u], 16 * t)
            sp.dma_start(entry(x[:], t, u), a["x"].rearrange("(t u) p d -> t u p d", u=2)[bass.ds(t, 1), u].rearrange("o p d -> p (o d)")).then_inc(x_in[u], 16)

        def load_ctxT(t, u):
            sp.wait_ge(ctxT_in[u], 16 * t)
            sp.wait_ge(scored[u], t)
            sp.dma_start(ctxT[:, u], a["ctxT"].rearrange("p (t u) h s -> p t u h s", u=2)[:, bass.ds(t, 1), u].rearrange("p o h s -> p (o h) s")).then_inc(ctxT_in[u], 16)

        steps(sp, NB, [(0, load_x), (2, load_ctxT)])

    @block.vector
    def _(dve):
        dve.wait_ge(consts_in, 10 * 16)
        dve.wait_ge(whwh_done, 1)
        dve.tensor_copy(whwh[:], two(bank[0])).then_inc(wh_ready, 1)

        def s_stats(t, u):
            dve.wait_ge(x_in[u], 16 * (t + 1))
            dve.wait_ge(ln.h_done[u], t)
            norm_stats(dve, ln, entry(x[:], t, u), t, u)

        def s_aggr(t, u):
            norm_aggr(dve, ln, t, u, LN_EPS)

        def s_h(t, u):
            stats_landed(dve, ln, t + u, 1 - u)
            dve.wait_ge(hT_done[u], t)
            normalise(dve, ln, h[:, u], entry(x[:], t, u), t, u)

        def s_w(t, u):
            dve.wait_ge(w_done[u], t + 1)
            dve.tensor_scalar(entry(w[:], t, u), psW[:, 0:D], 0.0, None, ALU.max).then_inc(w_copied[u], 1)

        steps(dve, NB, [(0, s_stats), (1, s_h), (0, s_aggr), (2, s_w)])
        for u in range(2):
            dve.wait_ge(scored[u], NB // 2)
        for k in range(HEADS):
            dve.tensor_tensor(attT[:, k], psS[k][:, 0:P], decayT[:, k], ALU.mult).then_inc(att_masked, 1)
        dve.wait_ge(att_masked, HEADS)
        dve.scalar_tensor_tensor(out=attT[:], in0=attT[:], scalar=-1.0, in1=attT[:], op0=ALU.mult, op1=ALU.max).then_inc(att_masked, 1)
        dve.wait_ge(att_masked, HEADS + 1)
        dve.tensor_scalar(attT[:], attT[:], 1.0, None, ALU.max).then_inc(att_done, 1)

        def s_h2(t, u):
            dve.wait_ge(h2T_done[u], t)
            normalise(dve, ln, h[:, u], entry(x[:], t, u), t, u, NB // 2)

        def s_prod(t, u):
            stats_landed(dve, ln, t + u - 1, 1 - u, NB // 2)
            dve.wait_ge(yb_done[u], t + 1)
            dve.wait_ge(prodT_done[u], t)
            dve.tensor_tensor(prod[:, u], y[:, u], entry(w[:], t, u), ALU.mult).then_inc(prod_done[u], 1)

        def s_x1(t, u):
            dve.wait_ge(delta_done[u], t + 1)
            dve.tensor_tensor(entry(x[:], t, u), psD[:, 0:D], entry(x[:], t, u), ALU.add).then_inc(x1_done[u], 1)

        def s_stats2(t, u):
            if isinstance(t, int):
                dve.wait_ge(x1_done[u], t + 1)
            norm_stats(dve, ln, entry(x[:], t, u), t, u, NB // 2)

        def s_lo(t, u):
            if not isinstance(t, int):
                dve.wait_ge(x1_done[u], t + 2)
            dve.wait_ge(h2hi_done[u], t + 1)
            dve.tensor_tensor(entry(h2_lo[:], t, u), two(psHT[u]), entry(h2_hi[:], t, u).bitcast(F32),
                              ALU.subtract).then_inc(h2lo_done[u], 1)

        def s_aggr2(t, u):
            norm_aggr(dve, ln, t, u, LN_EPS, NB // 2)

        def s_gstats(t, u):
            dve.wait_ge(o_done[u], t + 1)
            norm_stats(dve, gn, psO[u][:, 0:D], t, u)

        def s_nmr(t, u):
            stats_landed(dve, gn, t + u, 1 - u)
            dve.wait_ge(gn.rstd_done[u], t + 1)
            dve.wait_ge(y_done[u], t)
            dve.scalar_tensor_tensor(out=nmr[:, u:u + 1], in0=gn.mv[:, u, 0:1], scalar=-1.0, in1=gn.rstd[:, u:u + 1],
                                     op0=ALU.mult, op1=ALU.mult).then_inc(nmr_done[u], 1)

        def s_gaggr(t, u):
            norm_aggr(dve, gn, t, u, GN_EPS)

        steps(dve, NB, [(5, s_h2), (4, s_x1), (6, s_lo), (4, s_stats2), (3, s_prod), (4, s_aggr2), (0, s_gstats), (1, s_nmr), (0, s_gaggr)])
        step = [0]

        def then(op):
            step[0] += 1
            op.then_inc(routing, 1)
            dve.wait_ge(routing, step[0])

        dve.wait_ge(logits_done, 1)
        then(dve.tensor_copy(lg, bank[0][:, 0:16 * NB].rearrange("p (b e) -> p b e", b=NB)[:, :, 0:NROUTE]))
        other = lg[:, :, 0:NE].unsqueeze(2).to_broadcast([P, NB, NE, NE])
        own = lg[:, :, 0:NE].unsqueeze(3).to_broadcast([P, NB, NE, NE])
        dve.memset(chosen, 0.5).then_inc(routing, 1)
        dve.tensor_tensor(above, other, own, ALU.is_gt).then_inc(routing, 1)
        step[0] += 2
        then(dve.tensor_tensor(equal, other, own, ALU.is_equal))
        then(dve.tensor_tensor(equal, equal, before[:].unsqueeze(1).to_broadcast([P, NB, NE, NE]), ALU.mult))
        then(dve.tensor_tensor(above, above, equal, ALU.add))
        then(dve.tensor_reduce(rank, above, AX.X, ALU.add))
        then(dve.tensor_scalar(chosen[:, :, 0:NE], rank, 2.0, 0.5, ALU.is_lt, ALU.mult))
        then(dve.tensor_tensor(mine, chosen[:, :, 0:NE], lg[:, :, 0:NE], ALU.mult))
        then(dve.tensor_reduce(middle, mine, AX.X, ALU.add))
        then(dve.tensor_tensor(gate[:, :, 0:NE], lg[:, :, 0:NE], middle.to_broadcast([P, NB, NE]), ALU.subtract))
        then(dve.tensor_scalar(gate[:, :, NE:NROUTE], lg[:, :, NE:NROUTE], 0.5, None, ALU.mult))
        dve.wait_ge(tanh_done, 1)
        then(dve.scalar_tensor_tensor(out=gate, in0=gate, scalar=1.0, in1=chosen, op0=ALU.add, op1=ALU.mult))
        for q in range(3):
            part = gate3[:, :, q * NROUTE:(q + 1) * NROUTE]
            then(dve.tensor_copy(part, gate if q == 0 else rest))
            if q < 2:
                then(dve.tensor_tensor(rest, gate if q == 0 else rest, part, ALU.subtract))
        dve.sem_inc(gate3_done, 1)
        dve.wait_ge(gatesT_done, 1)
        for k in range(2):
            dve.tensor_copy(gates[:, 8 * k:8 * (k + 1)], bank[2 + k][0:3 * NROUTE, :].bitcast(BF16).rearrange("q (b s) -> q b s", b=8)).then_inc(gatesT_copied, 1)

        for u in range(2):
            dve.sem_inc(su_done[u], 1)
            dve.sem_inc(act_done[u], 1)
        dve.sem_inc(x2_done, 1)

        def weigh(g, j):
            u, n, m = j % 2, 7 * g + j // 2, CH[j]
            dve.wait_ge(silu_done[u], n + 2)
            dve.wait_ge(u_done[u], n + 1)
            dve.wait_ge(acthi_done[u], n + 1)
            dve.wait_ge(actlo_done[u], n + 1)
            dve.tensor_tensor(act_f[0:m, u], silu_g[0:m, u], psU[u][0:m, :], ALU.mult).then_inc(su_done[u], 1)
            dve.wait_ge(su_done[u], n + 2)
            dve.wait_ge(spread_done[u], n + 1)
            dve.tensor_tensor(act_f[0:m, u], act_f[0:m, u], psC[u][0:m, :], ALU.mult).then_inc(act_done[u], 1)

        with dve.Fori(0, NG) as g:
            for j in range(NCH):
                weigh(g, j)
            for u in range(2):
                dve.wait_ge(down_done[u], 7 * g + 8)
            for k in range(2):
                xs = x[:].rearrange("p (g i) d -> p g i d", g=NG)[:, bass.ds(g, 1), 2 * k:2 * k + 2].rearrange("p o i d -> p (o i d)")
                dve.tensor_tensor(xs, psY[k][:, :], xs, ALU.add).then_inc(x2_done, 1)

    @block.gpsimd
    def _(pool):
        pool.dma_start(identb[:], a["ident"]).then_inc(cast_in, 16)
        pool.dma_start(spread[:], a["spread"]).then_inc(cast_in, 16)
        pool.memset(half[:], -0.5).then_inc(exponents, 1)
        pool.wait_ge(exponents, 1)

        def s_rstd(t, u):
            norm_rstd(pool, ln, half, t, u)

        def s_wlo(t, u):
            pool.wait_ge(whi_done[u], t + 1)
            pool.tensor_tensor(entry(w_lo[:].rearrange("p (b n) -> p b n", b=NB), t, u), w_raw[:, u],
                               entry(w_hi[:].rearrange("p (b n) -> p b n", b=NB), t, u).bitcast(F32), ALU.subtract).then_inc(wlo_done[u], 1)

        steps(pool, NB, [(0, s_rstd), (2, s_wlo)])
        pool.wait_ge(router_split, 1)
        pool.tensor_tensor(router_lo[:], router[:], router_hi[:].bitcast(F32), ALU.subtract).then_inc(router_split, 1)

        def s_rstd2(t, u):
            norm_rstd(pool, ln, half, t, u, NB // 2)

        def s_affine(t, u):
            pool.wait_ge(y_done[u], t + 1)
            pool.tensor_tensor(y[:, u], y[:, u], gamma[:], ALU.mult).then_inc(yg_done[u], 1)
            pool.wait_ge(yg_done[u], t + 1)
            pool.tensor_tensor(y[:, u], y[:, u], beta[:], ALU.add).then_inc(yb_done[u], 1)

        def s_grstd(t, u):
            norm_rstd(pool, gn, half, t, u)

        steps(pool, NB, [(4, s_rstd2), (2, s_affine), (0, s_grstd)])

        for u in range(2):
            pool.sem_inc(actlo_done[u], 1)

        def low(g, j):
            u, n, m = j % 2, 7 * g + j // 2, CH[j]
            pool.wait_ge(acthi_done[u], n + 2)
            pool.tensor_tensor(act_lo[0:m, u], act_f[0:m, u], act_hi[0:m, u].bitcast(F32), ALU.subtract).then_inc(actlo_done[u], 1)

        with pool.Fori(0, NG) as g:
            for j in range(NCH):
                low(g, j)

    @block.scalar
    def _(act):
        def s_hT(t, u):
            act.wait_ge(hT_done[u], t + 1)
            act.wait_ge(w_done[u], t)
            act.activation(hT[:, u], two(psT[u]), ACT.Copy).then_inc(hT_copied[u], 1)

        def s_v(t, u):
            act.wait_ge(v_done[u], t + 1)
            act.activation(entry(v[:], t, u), psV[:, 0:D], ACT.Copy).then_inc(v_copied[u], 1)

        def s_r(t, u):
            act.wait_ge(r_done[u], t + 1)
            act.wait_ge(scored[u], t)
            act.activation(r[:, u], two(psR), ACT.Copy).then_inc(r_copied[u], 1)

        def load_wraw(t, u):
            act.wait_ge(wraw_in[u], 16 * t)
            act.wait_ge(wlo_done[u], t)
            act.dma_start(w_raw[:, u], a["wpack"].rearrange("p (t u n) -> p t u n", u=2, n=WSTEP)[:, bass.ds(t, 1), u].rearrange("p o n -> p (o n)")).then_inc(wraw_in[u], 16)

        def s_whi(t, u):
            act.wait_ge(wraw_in[u], 16 * (t + 1))
            act.activation(entry(w_hi[:].rearrange("p (b n) -> p b n", b=NB), t, u), w_raw[:, u], ACT.Copy).then_inc(whi_done[u], 1)

        steps(act, NB, [(1, s_hT), (2, s_v), (2, s_r), (0, load_wraw), (1, s_whi)])
        act.activation(router_hi[:], router[:], ACT.Copy).then_inc(router_split, 1)

        def s_h2hi(t, u):
            act.wait_ge(h2T_done[u], t + 1)
            act.activation(entry(h2_hi[:], t, u), two(psHT[u]), ACT.Copy).then_inc(h2hi_done[u], 1)

        def s_prodT(t, u):
            act.wait_ge(prodT_done[u], t + 1)
            act.wait_ge(delta_done[u], t)
            act.activation(prodT[:, u], two(psPT), ACT.Copy).then_inc(prodT_copied[u], 1)

        def s_y(t, u):
            act.wait_ge(nmr_done[u], t + 1)
            act.wait_ge(prod_done[u], t)
            act.activation(y[:, u], psO[u][:, 0:D], ACT.Identity, bias=nmr[:, u:u + 1],
                           scale=gn.rstd[:, u:u + 1]).then_inc(y_done[u], 1)

        steps(act, NB, [(5, s_h2hi), (3, s_prodT), (1, s_y)])
        for g in range(NG):
            act.wait_ge(logitsT_done, g + 1)
            act.activation(lgT[:, GT * g:GT * (g + 1)], bank[5 + g % 2][0:NROUTE, :].rearrange("q (b s) -> q b s", b=GT), ACT.Copy).then_inc(logitsT_copied, 1)
        act.wait_ge(routing, ROUTED)
        act.activation(gate, gate, ACT.Tanh).then_inc(tanh_done, 1)

        for u in range(2):
            act.sem_inc(silu_done[u], 1)
            act.sem_inc(acthi_done[u], 1)

        def silu(g, j):
            u, n, m = j % 2, 7 * g + j // 2, CH[j]
            act.wait_ge(g_done[u], n + 1)
            act.wait_ge(su_done[u], n + 1)
            act.activation(silu_g[0:m, u], psG[u][0:m, :], ACT.Silu).then_inc(silu_done[u], 1)

        def high(g, j):
            u, n, m = j % 2, 7 * g + j // 2, CH[j]
            act.wait_ge(act_done[u], n + 2)
            act.wait_ge(down_done[u], n + 1)
            act.activation(act_hi[0:m, u], act_f[0:m, u], ACT.Copy).then_inc(acthi_done[u], 1)

        with act.Fori(0, NG) as g:
            for j in range(NCH):
                silu(g, j)
                if j:
                    high(g, j - 1)
            high(g, NCH - 1)

    @block.tensor
    def _(pe):
        pe.wait_ge(consts_in, 10 * 16)
        for k in range(HEADS):
            mm = pe.matmul(bank[0][:, k * P:(k + 1) * P], whT[:, k], whT[:, k], start=True, stop=True)
        mm.then_inc(whwh_done, 1)
        pe.wait_ge(wh_ready, 1)

        def s_T(t, u):
            pe.wait_ge(ln.h_done[u], t + 1)
            pe.wait_ge(hT_copied[u], t)
            for c in range(DC):
                mm = pe.transpose(psT[u][:, c * P:(c + 1) * P], h[:, u, c * P:(c + 1) * P], ident[:])
            mm.then_inc(hT_done[u], 1)

        def s_main(t, u):
            pe.wait_ge(ctxT_in[u], 16 * (t + 1))
            pe.wait_ge(v_copied[1 - u], t + u)
            for k in range(HEADS):
                mm = pe.matmul(psV[:, k * P:(k + 1) * P], ctxT[:, u, k], wh[:, k], start=True, stop=True)
            mm.then_inc(v_done[u], 1)
            pe.wait_ge(hT_copied[u], t + 1)
            pe.wait_ge(r_copied[1 - u], t + u)
            for k in range(HEADS):
                mm = pe.matmul(psR[:, k * P:(k + 1) * P], whwh[:, k], hT[:, u, k], start=True, stop=True)
            mm.then_inc(r_done[u], 1)
            pe.wait_ge(w_copied[1 - u], t + u)
            for c in range(DC):
                mm = pe.matmul(psW[:, 0:D], hT[:, u, c], wg[:, c], start=(c == 0), stop=(c == DC - 1))
            mm.then_inc(w_done[u], 1)
            pe.wait_ge(r_copied[u], t + 1)
            first = isinstance(t, int) and t == 0 and u == 0
            last = isinstance(t, int) and t == NB // 2 - 1 and u == 1
            for k in range(HEADS):
                mm = pe.matmul(psS[k][:, 0:P], ctxT[:, u, k], r[:, u, k], start=first, stop=last, skip_group_check=True)
            mm.then_inc(scored[u], 1)

        steps(pe, NB, [(1, s_T), (2, s_main)], peel=4)

        def s_h2T(t, u):
            pe.wait_ge(ln.h_done[u], t + NB // 2 + 1)
            pe.wait_ge(h2lo_done[u], t)
            for c in range(DC):
                mm = pe.transpose(psHT[u][:, c * P:(c + 1) * P], h[:, u, c * P:(c + 1) * P], ident[:])
            mm.then_inc(h2T_done[u], 1)

        def s_wo(t, u):
            pe.wait_ge(prodT_copied[u], t + 1)
            pe.wait_ge(x1_done[1 - u], t + u)
            for c in range(DC):
                mm = pe.matmul(psD[:, 0:D], prodT[:, u, c], wo[:, c], start=(c == 0), stop=(c == DC - 1))
            mm.then_inc(delta_done[u], 1)

        def s_pT(t, u):
            pe.wait_ge(prod_done[u], t + 1)
            pe.wait_ge(prodT_copied[1 - u], t + u)
            for c in range(DC):
                mm = pe.transpose(psPT[:, c * P:(c + 1) * P], prod[:, u, c * P:(c + 1) * P], ident[:])
            mm.then_inc(prodT_done[u], 1)

        def s_o(t, u):
            pe.wait_ge(y_done[u], t)
            for k in range(HEADS):
                mm = pe.matmul(psO[u][:, k * HD:(k + 1) * HD], attT[:, k], entry(v[:], t, u)[:, k * HD:(k + 1) * HD],
                               start=True, stop=True)
            mm.then_inc(o_done[u], 1)

        for u in range(2):
            pe.wait_ge(v_copied[u], NB // 2)
            pe.wait_ge(w_copied[u], NB // 2)
        pe.wait_ge(att_done, 1)
        steps(pe, NB, [(5, s_h2T), (4, s_wo), (3, s_pT), (0, s_o)])

        pe.wait_ge(router_split, 2)
        for u in range(2):
            pe.wait_ge(h2lo_done[u], NB // 2)
        for g in range(NG):
            if g >= 2:
                pe.wait_ge(logitsT_copied, g - 1)
            n = 0
            for c in range(DC):
                for wt, xt in ((router_hi, h2_hi), (router_hi, h2_lo), (router_lo, h2_hi)):
                    mm = pe.matmul(bank[5 + g % 2][:, :], wt[:, c], xt[:, GT * g:GT * (g + 1), c], start=(n == 0), stop=(n == 5))
                    n += 1
            mm.then_inc(logitsT_done, 1)
        pe.wait_ge(logitsT_copied, NG)
        for b in range(NB):
            mm = pe.transpose(bank[0][:, 16 * b:16 * b + NROUTE], lgT[:, b], ident[0:NROUTE, 0:NROUTE])
        mm.then_inc(logits_done, 1)
        pe.wait_ge(gate3_done, 1)
        pe.wait_ge(cast_in, 32)
        for b in range(NB):
            mm = pe.transpose(bank[2 + b // 8][0:3 * NROUTE, :].bitcast(BF16)[:, (b % 8) * P:(b % 8 + 1) * P], gate3[:, b], identb[:])
        mm.then_inc(gatesT_done, 1)
        pe.wait_ge(gatesT_copied, 2)

        for u in range(2):
            pe.sem_inc(down_done[u], 1)

        def up(g, j):
            u, n, m = j % 2, 7 * g + j // 2, CH[j]
            pe.wait_ge(act_done[u], n + 1)
            for ps, base, free, done in ((psG, 0, silu_done, g_done), (psU, DC * HID, su_done, u_done)):
                pe.wait_ge(free[u], n + 1)
                i = 0
                for c in range(DC):
                    cols = base + c * HID + j * P
                    for wt, xt in ((w_hi, h2_hi), (w_hi, h2_lo), (w_lo, h2_hi)):
                        mm = pe.matmul(ps[u][0:m, :], wt[:, cols:cols + m], tokens(xt, g, c), start=(i == 0), stop=(i == 5))
                        i += 1
                mm.then_inc(done[u], 1)
            pe.matmul(psC[u][0:m, :], spread[:, j * P:j * P + m], gates[:].rearrange("q (g b) s -> q g (b s)", g=NG)[:, bass.ds(g, 1)].rearrange("q o n -> q (o n)"),
                      start=True, stop=True).then_inc(spread_done[u], 1)

        def down(g, j):
            u, n, m = j % 2, 7 * g + j // 2, CH[j]
            pe.wait_ge(actlo_done[u], n + 2)
            if j == 0:
                pe.wait_ge(x2_done, 2 * g + 1)
            cols = 2 * DC * HID + j * D
            for i in range(GT):
                for q, (at, wt) in enumerate(((act_hi, w_hi), (act_hi, w_lo), (act_lo, w_hi))):
                    mm = pe.matmul(psY[i // 2][:, (i % 2) * D:(i % 2 + 1) * D], at[0:m, u, i * P:(i + 1) * P], wt[0:m, cols:cols + D],
                                   start=(j == 0 and q == 0 and i % 2 == 0), stop=(j == NCH - 1 and q == 2 and i % 2 == 1),
                                   skip_group_check=True)
            mm.then_inc(down_done[u], 1)

        with pe.Fori(0, NG) as g:
            for j in range(NCH):
                up(g, j)
                if j:
                    down(g, j - 1)
            down(g, NCH - 1)


def last_layers(nc, a, out, core, bank, x, ident, identb, half):
    sb, sem, sem2 = core.sb, core.sem, core.sem2
    h = sb("h_late", [P, 2, D])
    ln = Norm(core, "ln_late")
    lnq = Norm(core, "ln_quant")
    thetaw, phiw, gw = (sb(n, [P, LAT], F32) for n in ("thetaw", "phiw", "gw"))
    outw = sb("outw", [LAT, P], F32)
    thetab, phib, gb = (sb(n, [LAT, 1], F32) for n in ("thetab", "phib", "gb"))
    outb = sb("outb", [P, 1], F32)
    lngamma, lnbeta = (sb(n, [LAT, D], F32) for n in ("lngamma", "lnbeta"))
    mean64 = sb("mean64", [LAT, P], F32)
    phi = sb("phi", [LAT, 2, D], F32)
    theta = sb("theta", [LAT, 2, D], F32)
    gx = sb("gx", [P, 2, 2, LAT], F32)
    negmax = sb("negmax", [P, 2, 2], F32)
    prob = sb("prob", [P, 2, 2, D], F32)
    probsum = sb("probsum", [P, 2, 2], F32)
    probinv = sb("probinv", [P, 2, 2], F32)
    probT = sb("probT", [P, 2, 2, D], F32)
    tx = sb("tx", [LAT, 2, D], F32)
    tstats = sb("tstats", [LAT, 2, 6], F32)
    tmv = sb("tmv", [LAT, 2, 2], F32)
    tall = sb("tall", [LAT, 2, 2], F32)
    tneg = sb("tneg", [LAT, 2], F32)
    tve = sb("tve", [LAT, 2], F32)
    trstd = sb("trstd", [LAT, 2], F32)
    ty = sb("ty", [LAT, 2, D], F32)
    th = sb("th", [LAT, 2, D], F32)
    xc = sb("xc", [P, 2, D], F32)
    hmax = sb("hmax", [P, 2, 4], F32)
    yscale = sb("yscale", [P, 2, 2], F32)
    qf = sb("qf", [P, 2, D], F32)
    xq = sb("xq", [P, 2, D], BF16)
    xqT = sb("xqT", [P, 2, DC, P], BF16)
    silu2 = sb("silu2", [P, 2, INNER], F32)
    gu = sb("gu", [P, 2, INNER], F32)
    gus = sb("gus", [P, 2, 5], F32)
    oscale = sb("oscale", [P, 2], F32)
    hq = sb("hq", [P, 2, INNER], BF16)
    hqT = sb("hqT", [P, 2, IC, P], BF16)
    x4 = sb("x4", [P, 2, D], F32)
    ones = sb("ones", [P, P], F32)
    roundc = sb("roundc", [P, 1], F32)
    ctxn = sb("ctxn", [P, NB, D], F32)
    wraw2 = [sb(f"wraw2{i}", [P, 2048], F32) for i in range(3)]
    wq = [sb(f"wq{i}", [P, 2048], BF16) for i in range(3)]
    wabs = sb("wabs", [P, 4], F32)
    wscale = sb("wscale", [P, 4], F32)
    winv = sb("winv", [P, 4], F32)
    late_in = sem("late_in")
    late_set = sem("late_set")
    wabs_done = sem("wabs_done")
    wtotal_done = sem("wtotal_done")
    winv_done = sem("winv_done")
    wrounded = sem("wrounded")
    wclipped = sem("wclipped")
    wq_done = sem("wq_done")
    proj_done = sem2("proj_done")
    gx_psum = sem2("gx_psum")
    proj_copied = sem2("proj_copied")
    gx_copied = sem2("gx_copied")
    score_done = sem2("score_done")
    max_done = sem2("max_done")
    exp_done = sem2("exp_done")
    inv_done = sem2("inv_done")
    prob_done = sem2("prob_done")
    probT_done = sem2("probT_done")
    probT_copied = sem2("probT_copied")
    pv_done = sem2("pv_done")
    tx_done = sem2("tx_done")
    tstats_done = sem2("tstats_done")
    tstep = sem2("tstep")
    tmean_done = sem2("tmean_done")
    tve_done = sem2("tve_done")
    trstd_done = sem2("trstd_done")
    ty_done = sem2("ty_done")
    th_done = sem2("th_done")
    out_done = sem2("out_done")
    xc_done = sem2("xc_done")
    x3_done = sem2("x3_done")
    hmax_done = sem2("hmax_done")
    qscale_done = sem2("qscale_done")
    qf_done = sem2("qf_done")
    xq_done = sem2("xq_done")
    xqT_done = sem2("xqT_done")
    xqT_copied = sem2("xqT_copied")
    gate_done = sem2("gate_done")
    up_done = sem2("up_done")
    silu2_done = sem2("silu2_done")
    gu_done = sem2("gu_done")
    gumax_done = sem2("gumax_done")
    guscale_done = sem2("guscale_done")
    guround_done = sem2("guround_done")
    hq_done = sem2("hq_done")
    hqT_done = sem2("hqT_done")
    hqT_copied = sem2("hqT_copied")
    down2_done = sem2("down2_done")
    x4_done = sem2("x4_done")
    stored = sem2("stored")

    psXq, psGate, psUp, psHq, psDown = bank[0], bank[1:3], bank[3:5], bank[5], bank[6]
    psProj, psGx, psScore, psProbT, psTx, psMean, psOut = bank[0], bank[1], bank[2:4], bank[4], bank[5], bank[6], bank[7]
    LATE_IN = 14 * 16

    core.stack.callback(core.end)
    block = core.stack.enter_context(nc.Block())

    @block.sync
    def _(sp):
        for dst, src in ((phiw, "phiw"), (thetaw, "thetaw"), (gw, "gw"), (ctxn, "ctx"), (thetab, "thetab"), (phib, "phib"), (gb, "gb"),
                         (lngamma, "lngamma"), (lnbeta, "lnbeta"), (outw, "outw"), (outb, "outb"),
                         (wraw2[0], "qgate"), (wraw2[1], "qup"), (wraw2[2], "qdown")):
            if src == "ctx":
                sp.dma_start(dst[:], a[src].rearrange("b p d -> p b d")).then_inc(late_in, 16)
            elif src[0] == "q":
                sp.dma_start(dst[:], a[src].rearrange("p c n -> p (c n)")).then_inc(late_in, 16)
            else:
                sp.dma_start(dst[:], a[src]).then_inc(late_in, 16)


        def store(t, u):
            sp.wait_ge(x4_done[u], t + 1)
            sp.dma_start(out.rearrange("(t u) p d -> t u p d", u=2)[bass.ds(t, 1), u].rearrange("o p d -> p (o d)"), x4[:, u]).then_inc(stored[u], 16)

        steps(sp, NB, [(0, store)])
        for u in range(2):
            sp.wait_ge(stored[u], 16 * NB // 2)

    @block.vector
    def _(dve):
        dve.wait_ge(late_in, LATE_IN)
        dve.memset(mean64[:], 1.0 / LAT).then_inc(late_set, 1)
        dve.memset(ones[:], 1.0).then_inc(late_set, 1)
        dve.memset(roundc[:], ROUND).then_inc(late_set, 1)
        dve.memset(wabs[:], 0.0).then_inc(late_set, 1)

        def c_stats(t, u):
            norm_stats(dve, ln, entry(x[:], t, u), t, u)

        def c_h(t, u):
            stats_landed(dve, ln, t + u, 1 - u)
            dve.wait_ge(gx_psum[u], t)
            normalise(dve, ln, h[:, u], entry(x[:], t, u), t, u)

        def c_aggr(t, u):
            norm_aggr(dve, ln, t, u, LN_EPS)

        def c_max(t, u):
            dve.wait_ge(score_done[u], t + 1)
            dve.wait_ge(exp_done[u], t)
            dve.tensor_reduce(negmax[:, u], two(psScore[u], 512), AX.X, ALU.max, negate=True).then_inc(max_done[u], 1)

        def c_prob(t, u):
            dve.wait_ge(exp_done[u], t + 1)
            dve.reciprocal(probinv[:, u], probsum[:, u]).then_inc(inv_done[u], 1)
            dve.wait_ge(inv_done[u], t + 1)
            for k in range(2):
                op = dve.tensor_scalar(prob[:, u, k], prob[:, u, k], probinv[:, u, k:k + 1], None, ALU.mult)
            op.then_inc(prob_done[u], 1)

        def c_gx(t, u):
            dve.wait_ge(gx_psum[u], t + 1)
            if not (isinstance(t, int) and t == NB // 2 - 1 and u == 1):
                dve.wait_ge(gx_psum[1 - u], t + u + 1)
            dve.wait_ge(pv_done[u], t)
            dve.tensor_copy(gx[:, u], two(psGx[:, u * 2 * LAT:(u + 1) * 2 * LAT], 2 * LAT)).then_inc(gx_copied[u], 1)

        def c_tstats(t, u):
            dve.wait_ge(tx_done[u], t + 1)
            dve.bn_stats(tstats[:, u], tx[:, u]).then_inc(tstats_done[u], 1)

        def c_var(t, u):
            if not isinstance(t, int):
                dve.wait_ge(tstats_done[1 - u], t + u + 1)
            dve.wait_ge(tmean_done[u], t + 1)
            dve.tensor_copy(tall[:, u], psMean[0:LAT, 0:2]).then_inc(tstep[u], 1)
            dve.wait_ge(tstep[u], 4 * t + 3)
            dve.scalar_tensor_tensor(out=tneg[:, u:u + 1], in0=tall[:, u, 0:1], scalar=tall[:, u, 0:1], in1=tall[:, u, 1:2],
                                     op0=ALU.mult, op1=ALU.subtract).then_inc(tstep[u], 1)
            dve.wait_ge(tstep[u], 4 * t + 4)
            dve.tensor_scalar(tve[:, u:u + 1], tneg[:, u:u + 1], -1.0, LN_EPS, ALU.mult, ALU.add).then_inc(tve_done[u], 1)

        def c_taggr(t, u):
            if isinstance(t, int):
                dve.wait_ge(tstats_done[u], t + 1)
            dve.bn_aggr(tmv[:, u], tstats[:, u]).then_inc(tstep[u], 1)
            dve.wait_ge(tstep[u], 4 * t + 1)
            dve.scalar_tensor_tensor(out=tmv[:, u, 1:2], in0=tmv[:, u, 0:1], scalar=tmv[:, u, 0:1], in1=tmv[:, u, 1:2],
                                     op0=ALU.mult, op1=ALU.add).then_inc(tstep[u], 1)

        def c_x3(t, u):
            dve.wait_ge(out_done[u], t + 1)
            dve.wait_ge(xc_done[u], t + 1)
            dve.scalar_tensor_tensor(out=entry(x[:], t, u), in0=psOut[:, 0:D], scalar=outb[:, 0:1], in1=xc[:, u],
                                     op0=ALU.add, op1=ALU.add).then_inc(x3_done[u], 1)

        def c_y(t, u):
            dve.wait_ge(th_done[u], t)
            dve.scalar_tensor_tensor(out=ty[:, u], in0=tx[:, u], scalar=tall[:, u, 0:1], in1=lngamma[:],
                                     op0=ALU.subtract, op1=ALU.mult).then_inc(ty_done[u], 1)
            dve.wait_ge(ty_done[u], 2 * t + 1)
            dve.wait_ge(trstd_done[u], t + 1)
            dve.scalar_tensor_tensor(out=ty[:, u], in0=ty[:, u], scalar=trstd[:, u:u + 1], in1=lnbeta[:],
                                     op0=ALU.mult, op1=ALU.add).then_inc(ty_done[u], 1)

        steps(dve, NB, [(3, c_gx), (0, c_stats), (1, c_h), (0, c_aggr), (2, c_max), (3, c_prob), (4, c_tstats), (5, c_var),
                        (4, c_taggr), (6, c_x3), (5, c_y)])

        dve.wait_ge(late_set, 4)
        for i in range(3):
            dve.tensor_reduce(wabs[:, i:i + 1], wraw2[i][:], AX.X, ALU.add, apply_absolute_value=True).then_inc(wabs_done, 1)
        dve.wait_ge(wtotal_done, 1)
        dve.tensor_scalar(wscale[:, 0:3], psDown[:, 0:3], 1.0 / (INNER * D), Q_EPS, ALU.mult, ALU.add).then_inc(winv_done, 1)
        dve.wait_ge(winv_done, 1)
        dve.reciprocal(winv[:, 0:3], wscale[:, 0:3]).then_inc(winv_done, 1)
        for i in range(3):
            dve.wait_ge(wrounded, i + 1)
            dve.tensor_scalar(wraw2[i][:], wraw2[i][:], ROUND - 1.0, ROUND + 1.0, ALU.max, ALU.min).then_inc(wclipped, 1)
            dve.wait_ge(wclipped, i + 1)
            dve.tensor_scalar(wq[i][:], wraw2[i][:], ROUND, None, ALU.subtract).then_inc(wq_done, 1)

        def d_stats(t, u):
            norm_stats(dve, lnq, entry(x[:], t, u), t, u)

        def d_h(t, u):
            stats_landed(dve, lnq, t + u, 1 - u)
            normalise(dve, lnq, h[:, u], entry(x[:], t, u), t, u)

        def d_aggr(t, u):
            norm_aggr(dve, lnq, t, u, LN_EPS)

        def d_quant(t, u):
            dve.wait_ge(lnq.h_done[u], t + 1)
            dve.tensor_reduce(hmax[:, u, 0:1], h[:, u], AX.X, ALU.max, apply_absolute_value=True).then_inc(hmax_done[u], 1)
            dve.wait_ge(hmax_done[u], 3 * t + 1)
            dve.tensor_scalar(hmax[:, u, 1:2], hmax[:, u, 0:1], 1.0 / 127.0, Q_EPS, ALU.mult, ALU.add).then_inc(hmax_done[u], 1)
            dve.wait_ge(hmax_done[u], 3 * t + 2)
            dve.reciprocal(hmax[:, u, 2:3], hmax[:, u, 1:2]).then_inc(hmax_done[u], 1)
            dve.wait_ge(silu2_done[u], 2 * t)
            dve.tensor_scalar(yscale[:, u], wscale[:, 0:2], hmax[:, u, 1:2], None, ALU.mult).then_inc(qscale_done[u], 1)
            dve.wait_ge(hmax_done[u], 3 * t + 3)
            dve.tensor_scalar(qf[:, u], h[:, u], hmax[:, u, 2:3], ROUND, ALU.mult, ALU.add).then_inc(qf_done[u], 1)
            dve.wait_ge(qf_done[u], t + 1)
            dve.wait_ge(xqT_done[u], t)
            dve.tensor_scalar(xq[:, u], qf[:, u], ROUND, None, ALU.subtract).then_inc(xq_done[u], 1)

        def d_gu(t, u):
            dve.wait_ge(guround_done[u], t)
            for k in range(2):
                dve.wait_ge(silu2_done[u], 2 * t + k + 1)
                if k == 0:
                    dve.wait_ge(up_done[u], t + 1)
                dve.tensor_tensor(gu[:, u, k * 512:(k + 1) * 512], psUp[k][:, :], silu2[:, u, k * 512:(k + 1) * 512],
                                  ALU.mult).then_inc(gu_done[u], 1)
            dve.wait_ge(gu_done[u], 2 * t + 2)
            dve.tensor_reduce(gus[:, u, 0:1], gu[:, u], AX.X, ALU.max, apply_absolute_value=True).then_inc(gumax_done[u], 1)
            dve.wait_ge(gumax_done[u], t + 1)
            dve.tensor_scalar(gus[:, u, 1:2], gus[:, u, 0:1], yscale[:, u, 1:2], None, ALU.mult).then_inc(guscale_done[u], 1)
            dve.wait_ge(guscale_done[u], 5 * t + 1)
            dve.tensor_scalar(gus[:, u, 2:3], gus[:, u, 1:2], 1.0 / 127.0, Q_EPS, ALU.mult, ALU.add).then_inc(guscale_done[u], 1)
            dve.wait_ge(guscale_done[u], 5 * t + 2)
            dve.reciprocal(gus[:, u, 3:4], gus[:, u, 2:3]).then_inc(guscale_done[u], 1)
            dve.tensor_scalar(oscale[:, u:u + 1], gus[:, u, 2:3], wscale[:, 2:3], None, ALU.mult).then_inc(guscale_done[u], 1)
            dve.wait_ge(guscale_done[u], 5 * t + 4)
            dve.tensor_scalar(gus[:, u, 4:5], gus[:, u, 3:4], yscale[:, u, 1:2], None, ALU.mult).then_inc(guscale_done[u], 1)

        def d_hq(t, u):
            dve.wait_ge(guround_done[u], t + 1)
            dve.wait_ge(hqT_done[u], t)
            dve.tensor_scalar(hq[:, u], silu2[:, u], ROUND, None, ALU.subtract).then_inc(hq_done[u], 1)

        def d_x4(t, u):
            dve.wait_ge(down2_done[u], t + 1)
            dve.wait_ge(stored[u], 16 * t)
            dve.scalar_tensor_tensor(out=x4[:, u], in0=psDown[:, 0:D], scalar=oscale[:, u:u + 1], in1=entry(x[:], t, u),
                                     op0=ALU.mult, op1=ALU.add).then_inc(x4_done[u], 1)

        steps(dve, NB, [(0, d_stats), (1, d_h), (0, d_aggr), (1, d_quant), (4, d_x4), (3, d_hq), (2, d_gu)])

    @block.gpsimd
    def _(pool):
        pool.wait_ge(late_in, LATE_IN)
        def c_rstd(t, u):
            norm_rstd(pool, ln, half, t, u)

        def c_xc(t, u):
            pool.wait_ge(x3_done[u], t)
            pool.tensor_tensor(xc[:, u], entry(x[:], t, u), entry(ctxn[:], t, u), ALU.add).then_inc(xc_done[u], 1)

        def c_trstd(t, u):
            pool.wait_ge(tve_done[u], t + 1)
            pool.tensor_tensor(trstd[:, u:u + 1], tve[:, u:u + 1], half[0:LAT, u:u + 1], ALU.pow).then_inc(trstd_done[u], 1)

        steps(pool, NB, [(0, c_rstd), (4, c_xc), (5, c_trstd)])

        def d_rstd(t, u):
            norm_rstd(pool, lnq, half, t, u)

        steps(pool, NB, [(0, d_rstd)])

    @block.scalar
    def _(act):
        act.wait_ge(late_in, LATE_IN)

        def c_proj(t, u):
            act.wait_ge(proj_done[u], t + 1)
            act.wait_ge(score_done[u], t)
            act.activation(phi[:, u], psProj[0:LAT, 0:D], ACT.Identity, bias=phib[:, 0:1])
            act.activation(theta[:, u], psProj[0:LAT, D:2 * D], ACT.Identity, bias=thetab[:, 0:1]).then_inc(proj_copied[u], 1)

        def c_exp(t, u):
            act.wait_ge(max_done[u], t + 1)
            act.wait_ge(probT_done[u], t)
            act.wait_ge(inv_done[u], t)
            for k in range(2):
                op = act.activation(prob[:, u, k], psScore[u][:, k * D:(k + 1) * D], ACT.Exp, bias=negmax[:, u, k:k + 1],
                                    accum_out=probsum[:, u, k:k + 1])
            op.then_inc(exp_done[u], 1)

        def c_probT(t, u):
            act.wait_ge(probT_done[u], t + 1)
            act.wait_ge(pv_done[u], t)
            act.activation(probT[:, u], two(psProbT, 512), ACT.Copy).then_inc(probT_copied[u], 1)

        def c_tx(t, u):
            act.wait_ge(pv_done[u], t + 1)
            act.wait_ge(ty_done[u], 2 * t)
            act.wait_ge(tstats_done[u], t)
            act.activation(tx[:, u], psTx[0:LAT, 0:D], ACT.Identity, bias=gb[:, 0:1]).then_inc(tx_done[u], 1)

        def c_th(t, u):
            act.wait_ge(ty_done[u], 2 * t + 2)
            act.wait_ge(out_done[u], t)
            act.activation(th[:, u], ty[:, u], ACT.Relu).then_inc(th_done[u], 1)

        steps(act, NB, [(1, c_proj), (2, c_exp), (3, c_probT), (4, c_tx), (5, c_th)])

        act.wait_ge(winv_done, 2)
        act.wait_ge(late_set, 4)
        for i in range(3):
            act.activation(wraw2[i][:], wraw2[i][:], ACT.Identity, bias=roundc[:, 0:1], scale=winv[:, i:i + 1]).then_inc(wrounded, 1)

        def d_xqT(t, u):
            act.wait_ge(xqT_done[u], t + 1)
            act.wait_ge(up_done[u], t)
            act.activation(xqT[:, u], psXq[:].bitcast(BF16)[:, 0:D].rearrange("p (c n) -> p c n", c=DC), ACT.Copy).then_inc(xqT_copied[u], 1)

        def d_silu(t, u):
            act.wait_ge(hq_done[u], t)
            for k in range(2):
                act.wait_ge(gate_done[u], 2 * t + k + 1)
                if k == 0:
                    act.wait_ge(qscale_done[u], t + 1)
                act.activation(silu2[:, u, k * 512:(k + 1) * 512], psGate[k][:, :], ACT.Silu, scale=yscale[:, u, 0:1]).then_inc(silu2_done[u], 1)

        def d_round(t, u):
            act.wait_ge(guscale_done[u], 5 * t + 5)
            act.activation(silu2[:, u], gu[:, u], ACT.Identity, bias=roundc[:, 0:1], scale=gus[:, u, 4:5]).then_inc(guround_done[u], 1)

        def d_hqT(t, u):
            act.wait_ge(hqT_done[u], t + 1)
            act.wait_ge(down2_done[u], t)
            act.activation(hqT[:, u], psHq[:].bitcast(BF16).rearrange("p (c n) -> p c n", c=IC), ACT.Copy).then_inc(hqT_copied[u], 1)

        steps(act, NB, [(1, d_xqT), (3, d_round), (3, d_hqT), (2, d_silu)])

    @block.tensor
    def _(pe):
        pe.wait_ge(late_in, LATE_IN)
        pe.wait_ge(late_set, 4)

        def c_proj(t, u):
            pe.wait_ge(proj_copied[1 - u], t + u)
            pe.matmul(psProj[0:LAT, D:2 * D], thetaw[:], entry(ctxn[:], t, u), start=True, stop=True)
            pe.wait_ge(ln.h_done[u], t + 1)
            pe.matmul(psProj[0:LAT, 0:D], phiw[:], h[:, u], start=True, stop=True).then_inc(proj_done[u], 1)
            pe.wait_ge(gx_copied[u], t)
            for k in range(2):
                mm = pe.matmul(psGx[:, (2 * u + k) * LAT:(2 * u + k + 1) * LAT], h[:, u, k * P:(k + 1) * P], gw[:], start=True, stop=True)
            mm.then_inc(gx_psum[u], 1)

        def c_score(t, u):
            pe.wait_ge(proj_copied[u], t + 1)
            pe.wait_ge(exp_done[u], t)
            for k in range(2):
                mm = pe.matmul(psScore[u][:, k * D:(k + 1) * D], theta[:, u, k * P:(k + 1) * P], phi[:, u], start=True, stop=True)
            mm.then_inc(score_done[u], 1)

        def c_probT(t, u):
            pe.wait_ge(prob_done[u], t + 1)
            pe.wait_ge(probT_copied[1 - u], t + u)
            for sh in range(2):
                for th_ in range(2):
                    mm = pe.transpose(psProbT[:, sh * D + th_ * P:sh * D + (th_ + 1) * P], prob[:, u, th_, sh * P:(sh + 1) * P], ident[:])
            mm.then_inc(probT_done[u], 1)

        def c_pv(t, u):
            pe.wait_ge(probT_copied[u], t + 1)
            pe.wait_ge(gx_copied[u], t + 1)
            pe.wait_ge(tx_done[1 - u], t + u)
            for k in range(2):
                mm = pe.matmul(psTx[0:LAT, 0:D], gx[:, u, k], probT[:, u, k], start=(k == 0), stop=(k == 1))
            mm.then_inc(pv_done[u], 1)

        def c_mean(t, u):
            pe.wait_ge(tstep[u], 4 * t + 2)
            pe.wait_ge(tve_done[1 - u], t + u)
            pe.matmul(psMean[:, 0:2], mean64[:], tmv[:, u], start=True, stop=True).then_inc(tmean_done[u], 1)

        def c_out(t, u):
            pe.wait_ge(th_done[u], t + 1)
            pe.wait_ge(x3_done[1 - u], t + u)
            pe.matmul(psOut[:, 0:D], outw[:], th[:, u], start=True, stop=True).then_inc(out_done[u], 1)

        steps(pe, NB, [(1, c_proj), (2, c_score), (3, c_probT), (4, c_pv), (5, c_mean), (6, c_out)])

        pe.wait_ge(wabs_done, 3)
        pe.wait_ge(x3_done[1], NB // 2)
        pe.matmul(psDown[:, 0:4], ones[:], wabs[:], start=True, stop=True).then_inc(wtotal_done, 1)
        pe.wait_ge(wq_done, 3)

        def d_xqT(t, u):
            pe.wait_ge(xq_done[u], t + 1)
            pe.wait_ge(xqT_copied[1 - u], t + u)
            for c in range(DC):
                mm = pe.transpose(psXq[:].bitcast(BF16)[:, c * P:(c + 1) * P], xq[:, u, c * P:(c + 1) * P], identb[:])
            mm.then_inc(xqT_done[u], 1)

        def d_up(t, u):
            pe.wait_ge(xqT_copied[u], t + 1)
            for i, (ps, done, free) in enumerate(((psGate, gate_done, silu2_done), (psUp, up_done, gu_done))):
                pe.wait_ge(free[1 - u], 2 * (t + u))
                for k in range(2):
                    for c in range(DC):
                        mm = pe.matmul(ps[k][:, :], xqT[:, u, c], wq[i][:, c * INNER + k * 512:c * INNER + (k + 1) * 512],
                                       start=(c == 0), stop=(c == DC - 1))
                    if i == 0 or k == 1:
                        mm.then_inc(done[u], 1)

        def d_hqT(t, u):
            pe.wait_ge(hq_done[u], t + 1)
            pe.wait_ge(hqT_copied[1 - u], t + u)
            for c in range(IC):
                mm = pe.transpose(psHq[:].bitcast(BF16)[:, c * P:(c + 1) * P], hq[:, u, c * P:(c + 1) * P], identb[:])
            mm.then_inc(hqT_done[u], 1)

        def d_down(t, u):
            pe.wait_ge(hqT_copied[u], t + 1)
            pe.wait_ge(x4_done[1 - u], t + u)
            for c in range(IC):
                mm = pe.matmul(psDown[:, 0:D], hqT[:, u, c], wq[2][:, c * D:(c + 1) * D], start=(c == 0), stop=(c == IC - 1))
            mm.then_inc(down2_done[u], 1)

        steps(pe, NB, [(1, d_xqT), (2, d_up), (3, d_hqT), (3, d_down)])


def kernel(x, ctx_2048, L0_xattn_Wh, L0_xattn_wg_w, L0_xattn_wo_w, L0_xattn_gn_gamma, L0_xattn_gn_beta,
           L0_ffn_gate_w, L0_ffn_w_gate, L0_ffn_w_up, L0_ffn_w_down, L0_ffn_shgate_w, L0_ffn_shw_gate,
           L0_ffn_shw_up, L0_ffn_shw_down, L1_xattn_theta_w, L1_xattn_theta_b, L1_xattn_phi_w,
           L1_xattn_phi_b, L1_xattn_g_w, L1_xattn_g_b, L1_xattn_ln_gamma, L1_xattn_ln_beta,
           L1_xattn_out_w, L1_xattn_out_b, L1_ffn_w_gate, L1_ffn_w_up, L1_ffn_w_down):
    import numpy as np
    import concourse.bacc as bacc
    from concourse.bass_utils import run_bass_kernel_spmd

    arr = np.asarray
    c = np.ascontiguousarray

    def rows(m):
        return c(m.reshape(-1, P, m.shape[1]).transpose(1, 0, 2))

    def side(experts, shared):
        return np.concatenate([arr(experts).transpose(1, 0, 2).reshape(D, -1), arr(shared)], 1)

    down = np.concatenate([arr(L0_ffn_w_down).reshape(-1, D), arr(L0_ffn_shw_down), np.zeros((NCH * P - HID, D), np.float32)], 0)
    gates = np.concatenate([arr(L0_ffn_gate_w), arr(L0_ffn_shgate_w)[None], np.zeros((P - NROUTE, D), np.float32)], 0)
    wh = arr(L0_xattn_Wh)
    arrays = {
        "x": c(arr(x)), "ctx": c(arr(ctx_2048)),
        "ctxT": c(arr(ctx_2048).reshape(NB, P, HEADS, HD).transpose(3, 0, 2, 1)),
        "wh": c(wh.transpose(1, 0, 2)), "whT": c(wh.transpose(2, 0, 1)),
        "wg": rows(arr(L0_xattn_wg_w)), "wo": rows(arr(L0_xattn_wo_w)),
        "gamma": c(np.broadcast_to(arr(L0_xattn_gn_gamma), (P, D))),
        "beta": c(np.broadcast_to(arr(L0_xattn_gn_beta), (P, D))),
        "wpack": c(np.concatenate([rows(m).reshape(P, -1) for m in
                                   (side(L0_ffn_w_gate, L0_ffn_shw_gate), side(L0_ffn_w_up, L0_ffn_shw_up), down)], 1)),
        "router": rows(c(gates.T)),
        "thetaw": c(arr(L1_xattn_theta_w).T), "phiw": c(arr(L1_xattn_phi_w).T), "gw": c(arr(L1_xattn_g_w).T),
        "outw": c(arr(L1_xattn_out_w).T), "thetab": c(arr(L1_xattn_theta_b)[:, None]), "phib": c(arr(L1_xattn_phi_b)[:, None]),
        "gb": c(arr(L1_xattn_g_b)[:, None]), "outb": c(arr(L1_xattn_out_b)[:, None]),
        "lngamma": c(arr(L1_xattn_ln_gamma)), "lnbeta": c(arr(L1_xattn_ln_beta)),
        "qgate": rows(arr(L1_ffn_w_gate).T), "qup": rows(arr(L1_ffn_w_up).T), "qdown": rows(arr(L1_ffn_w_down).T),
        **constants(),
    }
    nc = bacc.Bacc("TRN2", target_bir_lowering=False, num_devices=1)
    aps = {k: nc.dram_tensor(f"in_{k}", m.shape, mybir.dt.from_np(m.dtype), kind="ExternalInput").ap() for k, m in arrays.items()}
    out = nc.dram_tensor("out", (NB, P, D), F32, kind="ExternalOutput").ap()
    program(nc, aps, out)
    r = run_bass_kernel_spmd(nc, [{f"in_{k}": m for k, m in arrays.items()}], core_ids=[0])
    return r.results[0]["out"]


def constants():
    import numpy as np

    gamma = 1.0 - 2.0 ** (-5.0 - np.arange(HEADS))
    late = np.arange(P)[None, :] - np.arange(P)[:, None]
    mask = np.where(late[None] <= 0, gamma[:, None, None] ** late[None].astype(np.float64), 0.0)
    mask = mask / np.sqrt(mask.sum(-1))[:, None, :]
    spread = np.zeros((3, NROUTE, NCH * P), np.float32)
    for e in range(NE):
        spread[:, e, e * HE:(e + 1) * HE] = 1.0
    spread[:, NE, NE * HE:HID] = 1.0
    before = np.broadcast_to(np.tril(np.ones((NE, NE), np.float32), -1), (P, NE, NE))
    return {
        "ident": np.eye(P, dtype=np.float32),
        "decayT": np.ascontiguousarray((mask / np.sqrt(HD)).transpose(2, 0, 1).astype(np.float32)),
        "spread": spread.reshape(3 * NROUTE, NCH * P),
        "before": np.ascontiguousarray(before),
    }
```

```python
from contextlib import ExitStack

import concourse.bass as bass
from concourse import mybir

ALU = mybir.AluOpType
ACT = mybir.ActivationFunctionType
AX = mybir.AxisListType
F32 = mybir.dt.float32
F32R = mybir.dt.float32r
BF16 = mybir.dt.bfloat16

P = 128
NB = 16
D = 256
DC = D // P
HEADS, HD = 2, 128
NE, HE, HS = 8, 176, 352
HID = NE * HE + HS
NCH = -(-HID // P)
CH = [min(P, HID - P * j) for j in range(NCH)]
NROUTE = NE + 1
GT = 4
NG = NB // GT
GN = GT * P
WPACK = 2 * DC * HID + NCH * D
WSTEP = WPACK // NB
LAT = 64
INNER = 1024
IC = INNER // P
LN_EPS, GN_EPS, Q_EPS = 1e-5, 1e-3, 1e-5
ROUND = 12582912.0
assert WPACK % NB == 0


def steps(eng, count, stages, peel=0):
    deepest = max(lag for lag, _ in stages)

    def peeled(i):
        for lag, f in stages:
            if 0 <= i - lag < count:
                f((i - lag) // 2, (i - lag) % 2)

    first = max(deepest + deepest % 2 + 2, peel)
    for i in range(first):
        peeled(i)
    with eng.Fori(first // 2, count // 2) as t:
        for u in range(2):
            for lag, f in stages:
                f(t + (u - lag) // 2, (u - lag) % 2)
    for i in range(count, count + deepest):
        peeled(i)


def entry(tile, t, u):
    rest = " ".join("abc"[: len(tile.shape) - 2])
    v = tile.rearrange(f"p (t u) {rest} -> p t u {rest}", u=2)
    return v[:, bass.ds(t, 1), u].rearrange(f"p o {rest} -> p (o {rest.split()[0]}) {' '.join(rest.split()[1:])}")


class Core:

    def __init__(self, nc, stack):
        self.nc, self.stack, self.sems = nc, stack, []

    def sb(self, name, shape, dt=F32, stack=None):
        return (stack or self.stack).enter_context(self.nc.sbuf_tensor(name, shape, dt))

    def sem(self, name):
        self.sems.append(self.nc.alloc_semaphore(name=name))
        return self.sems[-1]

    def sem2(self, name):
        return [self.sem(f"{name}{u}") for u in range(2)]

    def end(self):
        self.nc.all_engine_barrier()
        self.nc.clear_and_free_semaphores(self.sems)
        self.nc.all_engine_barrier()


class Norm:

    def __init__(self, core, name, rows=P):
        self.stats = core.sb(f"{name}_stats", [rows, 2, 6])
        self.mv = core.sb(f"{name}_mv", [rows, 2, 2])
        self.ve = core.sb(f"{name}_ve", [rows, 2])
        self.rstd = core.sb(f"{name}_rstd", [rows, 2])
        self.stats_done = core.sem2(f"{name}_stats_done")
        self.mv_done = core.sem2(f"{name}_mv_done")
        self.ve_done = core.sem2(f"{name}_ve_done")
        self.rstd_done = core.sem2(f"{name}_rstd_done")
        self.h_done = core.sem2(f"{name}_h_done")


def two(ap, n=D):
    return ap[:, 0:n].rearrange("p (c n) -> p c n", c=2)



def norm_stats(dve, n, src, t, u, base=0):
    dve.bn_stats(n.stats[:, u], src).then_inc(n.stats_done[u], 1)


def stats_landed(dve, n, t, u, base=0):
    if not isinstance(t, int):
        dve.wait_ge(n.stats_done[u], t + base + 1)


def norm_aggr(dve, n, t, u, eps, base=0):
    if isinstance(t, int):
        dve.wait_ge(n.stats_done[u], t + base + 1)
    dve.bn_aggr(n.mv[:, u], n.stats[:, u]).then_inc(n.mv_done[u], 1)
    dve.wait_ge(n.mv_done[u], t + base + 1)
    dve.wait_ge(n.rstd_done[u], t + base)
    dve.tensor_scalar(n.ve[:, u:u + 1], n.mv[:, u, 1:2], eps, None, ALU.add).then_inc(n.ve_done[u], 1)


def norm_rstd(pool, n, half, t, u, base=0):
    pool.wait_ge(n.ve_done[u], t + base + 1)
    pool.tensor_tensor(n.rstd[:, u:u + 1], n.ve[:, u:u + 1], half[:, u:u + 1], ALU.pow).then_inc(n.rstd_done[u], 1)


def normalise(dve, n, out, src, t, u, base=0):
    dve.wait_ge(n.rstd_done[u], t + base + 1)
    dve.tensor_scalar(out, src, n.mv[:, u, 0:1], n.rstd[:, u:u + 1], ALU.subtract, ALU.mult).then_inc(n.h_done[u], 1)


def program(nc, a, out, upto="all"):
    with ExitStack() as stack:
        whole = Core(nc, stack)
        bank = [stack.enter_context(nc.psum_tensor(f"bank{i}", [P, 512], F32)) for i in range(8)]
        x = whole.sb("x", [P, NB, D])
        ident = whole.sb("ident", [P, P])
        identb = whole.sb("identb", [P, P], BF16)
        half = whole.sb("half", [P, 2])
        kept = whole.sb("kept", [P, NB, D])
        late_w = whole.sb("late_w", [P, 3, IC * D])
        wabs_part = whole.sb("wabs_part", [P, NG, 3])
        late_in = whole.sem("late_in")
        late = (kept, late_w, wabs_part, late_in)
        with ExitStack() as part:
            first_layers(nc, a, Core(nc, part), bank, x, ident, identb, half, late)
        if upto == "B":
            with nc.Block() as block:
                @block.sync
                def _(sp):
                    done = nc.alloc_semaphore(name="done")
                    sp.dma_start(out["x2"], x[:]).then_inc(done, 16)
                    sp.wait_ge(done, 16)
            return
        with ExitStack() as part:
            last_layers(nc, a, out, Core(nc, part), bank, x, ident, half, late)


def first_layers(nc, a, core, bank, x, ident, identb, half, late):
    sb, sem, sem2 = core.sb, core.sem, core.sem2
    h = sb("h", [P, 2, D])
    ln, gn = Norm(core, "ln"), Norm(core, "gn")
    s1 = ExitStack()
    v, late_w, wabs_part, late_in = late
    w = late_w[:, 0:2].rearrange("p i (b d) -> p (i b) d", b=NB // 2)
    w_raw = late_w[:, 2, 0:2 * WSTEP].rearrange("p (u n) -> p u n", u=2)
    ctxT = late_w[:, 2, 2 * WSTEP:2 * WSTEP + 2 * D].rearrange("p (u h s) -> p u h s", u=2, h=HEADS)
    s2 = ExitStack()
    w_hi = sb("w_hi", [P, WPACK], F32R, s2)
    w_lo = sb("w_lo", [P, WPACK], F32R, s2)
    h2_hi = sb("h2_hi", [P, NB, DC, P], F32R, s2)
    h2_lo = sb("h2_lo", [P, NB, DC, P], F32R, s2)
    gates = sb("gates", [3 * NROUTE, NB, P], BF16, s2)
    spread = sb("spread", [3 * NROUTE, NCH * P], BF16, s2)
    before = sb("before", [P, NE, NE], F32, s2)
    s3 = ExitStack()
    hT = sb("hT", [P, 2, DC, P], F32, s3)
    r = sb("r", [P, 2, HEADS, P], F32, s3)
    wh = sb("wh", [P, HEADS, HD], F32, s3)
    whT = sb("whT", [P, HEADS, HD], F32, s3)
    whwh = sb("whwh", [P, HEADS, HD], F32, s3)
    wg = sb("wg", [P, DC, D], F32, s3)
    wo = sb("wo", [P, DC, D], F32, s3)
    decayT = sb("decayT", [P, HEADS, P], F32, s3)
    attT = sb("attT", [P, HEADS, P], F32, s3)
    gamma = sb("gamma", [P, D], F32, s3)
    beta = sb("beta", [P, D], F32, s3)
    nmr = sb("nmr", [P, 2], F32, s3)
    router = sb("router", [P, DC, P], F32, s3)
    router_hi = sb("router_hi", [P, DC, P], F32R, s3)
    router_lo = sb("router_lo", [P, DC, P], F32R, s3)
    y = sb("y", [P, 2, D], F32, s3)
    prod = sb("prod", [P, 2, D], F32, s3)
    prodT = sb("prodT", [P, 2, DC, P], F32, s3)

    s3.close()
    s5 = ExitStack()
    silu_g = sb("silu_g", [P, 2, GN], F32, s5)
    act_f = sb("act_f", [P, 2, GN], F32, s5)
    act_hi = sb("act_hi", [P, 2, GN], F32R, s5)
    act_lo = sb("act_lo", [P, 2, GN], F32R, s5)
    gate3 = sb("gate3", [P, NB, 3 * NROUTE], BF16, s5)
    s5.close()
    lgT = v[0:NROUTE, :, 0:P]
    lg = v[:, :, P:P + NROUTE]
    gate = v[:, :, P + 16:P + 16 + NROUTE]
    rest = v[:, :, P + 32:P + 32 + NROUTE]
    above = w[:, :, 0:NE * NE].rearrange("p b (e f) -> p b e f", e=NE)
    equal = w[:, :, NE * NE:2 * NE * NE].rearrange("p b (e f) -> p b e f", e=NE)
    rank = w[:, :, P:P + NE]
    chosen = w[:, :, P + 16:P + 16 + NROUTE]
    mine = w[:, :, P + 32:P + 32 + NE]
    middle = w[:, :, P + 48:P + 49]
    s2.close()
    s1.close()

    consts_in = sem("consts_in")
    cast_in = sem("cast_in")
    x_in = sem2("x_in")
    ctxT_in = sem2("ctxT_in")
    wraw_in = sem2("wraw_in")
    exponents = sem("exponents")
    wh_ready = sem("wh_ready")
    whwh_done = sem("whwh_done")
    hT_done = sem2("hT_done")
    hT_copied = sem2("hT_copied")
    v_done = sem2("v_done")
    v_copied = sem2("v_copied")
    r_done = sem2("r_done")
    r_copied = sem2("r_copied")
    w_done = sem2("w_done")
    w_copied = sem2("w_copied")
    scored = sem2("scored")
    whi_done = sem2("whi_done")
    wlo_done = sem2("wlo_done")
    att_masked = sem("att_masked")
    att_done = sem("att_done")

    router_split = sem("router_split")
    o_done = sem2("o_done")
    nmr_done = sem2("nmr_done")
    y_done = sem2("y_done")
    yg_done = sem2("yg_done")
    yb_done = sem2("yb_done")
    prod_done = sem2("prod_done")
    prodT_done = sem2("prodT_done")
    prodT_copied = sem2("prodT_copied")
    delta_done = sem2("delta_done")
    x1_done = sem2("x1_done")
    h2T_done = sem2("h2T_done")
    h2hi_done = sem2("h2hi_done")
    h2lo_done = sem2("h2lo_done")

    logitsT_done = sem("logitsT_done")
    logitsT_copied = sem("logitsT_copied")
    logits_done = sem("logits_done")
    routing = sem("routing")
    tanh_done = sem("tanh_done")
    gate3_done = sem("gate3_done")
    gatesT_done = sem("gatesT_done")
    gatesT_copied = sem("gatesT_copied")
    g_done = sem2("g_done")
    u_done = sem2("u_done")
    spread_done = sem2("spread_done")
    silu_done = sem2("silu_done")
    su_done = sem2("su_done")
    act_done = sem2("act_done")
    acthi_done = sem2("acthi_done")
    actlo_done = sem2("actlo_done")
    down_done = sem2("down_done")
    x2_done = sem("x2_done")

    psT, psV, psR, psW = [bank[0], bank[1]], bank[2], bank[3], bank[4]
    psS = [bank[5], bank[6]]
    psO, psPT, psD, psHT = [bank[0], bank[1]], bank[2], bank[3], [bank[4], bank[7]]

    psG, psU, psC, psY = bank[0:2], bank[2:4], bank[4:6], bank[6:8]

    def tokens(ap, g, c):
        return ap[:].rearrange("p (g b) c s -> p g b c s", g=NG)[:, bass.ds(g, 1), :, c].rearrange("p o b s -> p (o b) s")

    core.stack.callback(core.end)
    block = core.stack.enter_context(nc.Block())

    ROUTED = 12

    @block.sync
    def _(sp):
        for dst, src in ((ident, "ident"), (whT, "whT"), (wh, "wh")):
            sp.dma_start(dst[:], a[src]).then_inc(consts_in, 16)
        for dst, src in ((wg, "wg"), (decayT, "decayT"), (wo, "wo"), (gamma, "gamma"), (beta, "beta"), (router, "router"), (before, "before")):
            sp.dma_start(dst[:], a[src]).then_inc(consts_in, 16)

        def load_x(t, u):
            sp.wait_ge(x_in[u], 16 * t)
            sp.dma_start(entry(x[:], t, u), a["x"].rearrange("(t u) p d -> t u p d", u=2)[bass.ds(t, 1), u].rearrange("o p d -> p (o d)")).then_inc(x_in[u], 16)

        def load_ctxT(t, u):
            sp.wait_ge(ctxT_in[u], 16 * t)
            sp.wait_ge(scored[u], t)
            sp.dma_start(ctxT[:, u], a["ctxT"].rearrange("p (t u) h s -> p t u h s", u=2)[:, bass.ds(t, 1), u].rearrange("p o h s -> p (o h) s")).then_inc(ctxT_in[u], 16)

        steps(sp, NB, [(0, load_x), (2, load_ctxT)])

        for u in range(2):
            sp.wait_ge(wlo_done[u], NB // 2)
        sp.wait_ge(gatesT_copied, 2)
        sp.dma_start(v[:], a["ctx"].rearrange("b p d -> p b d")).then_inc(late_in, 16)
        for i, src in enumerate(("qgate", "qup", "qdown")):
            sp.dma_start(late_w[:, i], a[src].rearrange("p c n -> p (c n)")).then_inc(late_in, 16)

    @block.vector
    def _(dve):
        dve.wait_ge(consts_in, 10 * 16)
        dve.wait_ge(whwh_done, 1)
        dve.tensor_copy(whwh[:], two(bank[0])).then_inc(wh_ready, 1)

        def s_stats(t, u):
            dve.wait_ge(x_in[u], 16 * (t + 1))
            dve.wait_ge(ln.h_done[u], t)
            norm_stats(dve, ln, entry(x[:], t, u), t, u)

        def s_aggr(t, u):
            norm_aggr(dve, ln, t, u, LN_EPS)

        def s_h(t, u):
            stats_landed(dve, ln, t + u, 1 - u)
            dve.wait_ge(hT_done[u], t)
            normalise(dve, ln, h[:, u], entry(x[:], t, u), t, u)

        def s_w(t, u):
            dve.wait_ge(w_done[u], t + 1)
            dve.tensor_scalar(entry(w[:], t, u), psW[:, 0:D], 0.0, None, ALU.max).then_inc(w_copied[u], 1)

        steps(dve, NB, [(3, s_w), (0, s_stats), (1, s_h), (0, s_aggr)])
        for u in range(2):
            dve.wait_ge(scored[u], NB // 2)
        for k in range(HEADS):
            dve.tensor_tensor(attT[:, k], psS[k][:, 0:P], decayT[:, k], ALU.mult).then_inc(att_masked, 1)
        dve.wait_ge(att_masked, HEADS)
        dve.scalar_tensor_tensor(out=attT[:], in0=attT[:], scalar=-1.0, in1=attT[:], op0=ALU.mult, op1=ALU.max).then_inc(att_masked, 1)
        dve.wait_ge(att_masked, HEADS + 1)
        dve.tensor_scalar(attT[:], attT[:], 1.0, None, ALU.max).then_inc(att_done, 1)

        def s_h2(t, u):
            dve.wait_ge(h2T_done[u], t)
            if not isinstance(t, int):
                dve.wait_ge(x1_done[u], t + 2)
            normalise(dve, ln, h[:, u], entry(x[:], t, u), t, u, NB // 2)

        def s_prod(t, u):
            stats_landed(dve, ln, t - 1, u, NB // 2)
            dve.wait_ge(yb_done[u], t + 1)
            dve.wait_ge(prodT_done[u], t)
            dve.tensor_tensor(prod[:, u], y[:, u], entry(w[:], t, u), ALU.mult).then_inc(prod_done[u], 1)

        def s_x1(t, u):
            dve.wait_ge(delta_done[u], t + 1)
            dve.tensor_tensor(entry(x[:], t, u), psD[:, 0:D], entry(x[:], t, u), ALU.add).then_inc(x1_done[u], 1)

        def s_stats2(t, u):
            if isinstance(t, int):
                dve.wait_ge(x1_done[u], t + 1)
            norm_stats(dve, ln, entry(x[:], t, u), t, u, NB // 2)

        def s_lo(t, u):
            dve.wait_ge(h2hi_done[u], t + 1)
            dve.tensor_tensor(entry(h2_lo[:], t, u), two(psHT[u]), entry(h2_hi[:], t, u).bitcast(F32),
                              ALU.subtract).then_inc(h2lo_done[u], 1)

        def s_aggr2(t, u):
            norm_aggr(dve, ln, t, u, LN_EPS, NB // 2)

        def s_gstats(t, u):
            dve.wait_ge(o_done[u], t + 1)
            norm_stats(dve, gn, psO[u][:, 0:D], t, u)

        def s_nmr(t, u):
            stats_landed(dve, gn, t + u, 1 - u)
            dve.wait_ge(gn.rstd_done[u], t + 1)
            dve.wait_ge(y_done[u], t)
            dve.scalar_tensor_tensor(out=nmr[:, u:u + 1], in0=gn.mv[:, u, 0:1], scalar=-1.0, in1=gn.rstd[:, u:u + 1],
                                     op0=ALU.mult, op1=ALU.mult).then_inc(nmr_done[u], 1)

        def s_gaggr(t, u):
            norm_aggr(dve, gn, t, u, GN_EPS)

        steps(dve, NB, [(0, s_gstats), (1, s_nmr), (0, s_gaggr), (4, s_x1), (6, s_h2), (4, s_stats2), (2, s_prod), (4, s_aggr2), (7, s_lo)])
        step = [0]

        def then(op):
            step[0] += 1
            op.then_inc(routing, 1)
            dve.wait_ge(routing, step[0])

        dve.wait_ge(logits_done, 1)
        then(dve.tensor_copy(lg, bank[0][:, 0:16 * NB].rearrange("p (b e) -> p b e", b=NB)[:, :, 0:NROUTE]))
        other = lg[:, :, 0:NE].unsqueeze(2).to_broadcast([P, NB, NE, NE])
        own = lg[:, :, 0:NE].unsqueeze(3).to_broadcast([P, NB, NE, NE])
        dve.memset(chosen, 0.5).then_inc(routing, 1)
        dve.tensor_tensor(above, other, own, ALU.is_gt).then_inc(routing, 1)
        step[0] += 2
        then(dve.tensor_tensor(equal, other, own, ALU.is_equal))
        then(dve.tensor_tensor(equal, equal, before[:].unsqueeze(1).to_broadcast([P, NB, NE, NE]), ALU.mult))
        then(dve.tensor_tensor(above, above, equal, ALU.add))
        then(dve.tensor_reduce(rank, above, AX.X, ALU.add))
        then(dve.tensor_scalar(chosen[:, :, 0:NE], rank, 2.0, 0.5, ALU.is_lt, ALU.mult))
        then(dve.tensor_tensor(mine, chosen[:, :, 0:NE], lg[:, :, 0:NE], ALU.mult))
        then(dve.tensor_reduce(middle, mine, AX.X, ALU.add))
        then(dve.tensor_tensor(gate[:, :, 0:NE], lg[:, :, 0:NE], middle.to_broadcast([P, NB, NE]), ALU.subtract))
        then(dve.tensor_scalar(gate[:, :, NE:NROUTE], lg[:, :, NE:NROUTE], 0.5, None, ALU.mult))
        dve.wait_ge(tanh_done, 1)
        then(dve.scalar_tensor_tensor(out=gate, in0=gate, scalar=1.0, in1=chosen, op0=ALU.add, op1=ALU.mult))
        for q in range(3):
            part = gate3[:, :, q * NROUTE:(q + 1) * NROUTE]
            then(dve.tensor_copy(part, gate if q == 0 else rest))
            if q < 2:
                then(dve.tensor_tensor(rest, gate if q == 0 else rest, part, ALU.subtract))
        dve.sem_inc(gate3_done, 1)
        dve.wait_ge(gatesT_done, 1)
        for k in range(2):
            dve.tensor_copy(gates[:, 8 * k:8 * (k + 1)], bank[2 + k][0:3 * NROUTE, :].bitcast(BF16).rearrange("q (b s) -> q b s", b=8)).then_inc(gatesT_copied, 1)

        for u in range(2):
            dve.sem_inc(su_done[u], 1)
            dve.sem_inc(act_done[u], 1)
        dve.sem_inc(x2_done, 1)

        def weigh(g, j):
            u, n, m = j % 2, 7 * g + j // 2, CH[j]
            dve.wait_ge(silu_done[u], n + 2)
            dve.wait_ge(u_done[u], n + 1)
            dve.wait_ge(acthi_done[u], n + 1)
            dve.wait_ge(actlo_done[u], n + 1)
            dve.tensor_tensor(act_f[0:m, u], silu_g[0:m, u], psU[u][0:m, :], ALU.mult).then_inc(su_done[u], 1)
            dve.wait_ge(su_done[u], n + 2)
            dve.wait_ge(spread_done[u], n + 1)
            dve.tensor_tensor(act_f[0:m, u], act_f[0:m, u], psC[u][0:m, :], ALU.mult).then_inc(act_done[u], 1)

        def add_down(g):
            dve.wait_ge(down_done[0], 7 * g + 8)
            dve.wait_ge(down_done[1], 7 * g + 8)
            for k in range(2):
                xs = x[:].rearrange("p (g i) d -> p g i d", g=NG)[:, bass.ds(g, 1), 2 * k:2 * k + 2].rearrange("p o i d -> p (o i d)")
                dve.tensor_tensor(xs, psY[k][:, :], xs, ALU.add).then_inc(x2_done, 1)

        def group(g):
            for j in range(2, NCH):
                weigh(g, j)
            dve.wait_ge(late_in, 4 * 16)
            dve.tensor_reduce(wabs_part[:, bass.ds(g, 1)].rearrange("p o i -> p (o i)"),
                              late_w[:].rearrange("p i (g n) -> p g i n", g=NG)[:, bass.ds(g, 1)].rearrange("p o i n -> p (o i) n"),
                              AX.X, ALU.add, apply_absolute_value=True)

        weigh(0, 0)
        weigh(0, 1)
        with dve.Fori(0, NG - 1) as g:
            group(g)
            weigh(g + 1, 0)
            weigh(g + 1, 1)
            add_down(g)
        group(NG - 1)
        add_down(NG - 1)

    @block.gpsimd
    def _(pool):
        pool.dma_start(identb[:], a["ident"]).then_inc(cast_in, 16)
        pool.dma_start(spread[:], a["spread"]).then_inc(cast_in, 16)
        pool.memset(half[:], -0.5).then_inc(exponents, 1)
        pool.wait_ge(exponents, 1)

        def s_rstd(t, u):
            norm_rstd(pool, ln, half, t, u)

        def s_wlo(t, u):
            pool.wait_ge(whi_done[u], t + 1)
            pool.tensor_tensor(entry(w_lo[:].rearrange("p (b n) -> p b n", b=NB), t, u), w_raw[:, u],
                               entry(w_hi[:].rearrange("p (b n) -> p b n", b=NB), t, u).bitcast(F32), ALU.subtract).then_inc(wlo_done[u], 1)

        steps(pool, NB, [(0, s_rstd), (1, s_wlo)])
        pool.wait_ge(router_split, 1)
        pool.tensor_tensor(router_lo[:], router[:], router_hi[:].bitcast(F32), ALU.subtract).then_inc(router_split, 1)

        def s_rstd2(t, u):
            norm_rstd(pool, ln, half, t, u, NB // 2)

        def s_yg(t, u):
            pool.wait_ge(y_done[u], t + 1)
            pool.tensor_tensor(y[:, u], y[:, u], gamma[:], ALU.mult).then_inc(yg_done[u], 1)

        def s_yb(t, u):
            pool.wait_ge(yg_done[u], t + 1)
            pool.tensor_tensor(y[:, u], y[:, u], beta[:], ALU.add).then_inc(yb_done[u], 1)

        def s_grstd(t, u):
            pool.wait_ge(y_done[u], t)
            norm_rstd(pool, gn, half, t, u)

        steps(pool, NB, [(0, s_grstd), (1, s_yg), (5, s_rstd2), (1, s_yb)])

        for u in range(2):
            pool.sem_inc(actlo_done[u], 1)

        def low(g, j):
            u, n, m = j % 2, 7 * g + j // 2, CH[j]
            pool.wait_ge(acthi_done[u], n + 2)
            pool.tensor_tensor(act_lo[0:m, u], act_f[0:m, u], act_hi[0:m, u].bitcast(F32), ALU.subtract).then_inc(actlo_done[u], 1)

        with pool.Fori(0, NG) as g:
            for j in range(NCH):
                low(g, j)

    @block.scalar
    def _(act):
        def s_hT(t, u):
            act.wait_ge(hT_done[u], t + 1)
            act.wait_ge(w_done[u], t)
            act.activation(hT[:, u], two(psT[u]), ACT.Copy).then_inc(hT_copied[u], 1)

        def s_v(t, u):
            act.wait_ge(v_done[u], t + 1)
            act.activation(entry(v[:], t, u), psV[:, 0:D], ACT.Copy).then_inc(v_copied[u], 1)

        def s_r(t, u):
            act.wait_ge(r_done[u], t + 1)
            act.wait_ge(scored[u], t)
            act.activation(r[:, u], two(psR), ACT.Copy).then_inc(r_copied[u], 1)

        def load_wraw(t, u):
            act.wait_ge(wraw_in[u], 16 * t)
            act.wait_ge(wlo_done[u], t)
            act.dma_start(w_raw[:, u], a["wpack"].rearrange("p (t u n) -> p t u n", u=2, n=WSTEP)[:, bass.ds(t, 1), u].rearrange("p o n -> p (o n)")).then_inc(wraw_in[u], 16)

        def s_whi(t, u):
            act.wait_ge(wraw_in[u], 16 * (t + 1))
            act.activation(entry(w_hi[:].rearrange("p (b n) -> p b n", b=NB), t, u), w_raw[:, u], ACT.Copy).then_inc(whi_done[u], 1)

        steps(act, NB, [(0, load_wraw), (1, s_whi), (1, s_v), (1, s_r), (0, s_hT)])
        act.activation(router_hi[:], router[:], ACT.Copy).then_inc(router_split, 1)

        def s_h2hi(t, u):
            act.wait_ge(h2T_done[u], t + 1)
            act.activation(entry(h2_hi[:], t, u), two(psHT[u]), ACT.Copy).then_inc(h2hi_done[u], 1)

        def s_prodT(t, u):
            act.wait_ge(prodT_done[u], t + 1)
            act.wait_ge(delta_done[u], t)
            act.activation(prodT[:, u], two(psPT), ACT.Copy).then_inc(prodT_copied[u], 1)

        def s_y(t, u):
            act.wait_ge(nmr_done[u], t + 1)
            act.wait_ge(prod_done[u], t)
            act.activation(y[:, u], psO[u][:, 0:D], ACT.Identity, bias=nmr[:, u:u + 1],
                           scale=gn.rstd[:, u:u + 1]).then_inc(y_done[u], 1)

        steps(act, NB, [(7, s_h2hi), (0, s_y), (2, s_prodT)])
        for g in range(NG):
            act.wait_ge(logitsT_done, g + 1)
            act.activation(lgT[:, GT * g:GT * (g + 1)], bank[5 + g % 2][0:NROUTE, :].rearrange("q (b s) -> q b s", b=GT), ACT.Copy).then_inc(logitsT_copied, 1)
        act.wait_ge(routing, ROUTED)
        act.activation(gate, gate, ACT.Tanh).then_inc(tanh_done, 1)

        for u in range(2):
            act.sem_inc(silu_done[u], 1)
            act.sem_inc(acthi_done[u], 1)

        def silu(g, j):
            u, n, m = j % 2, 7 * g + j // 2, CH[j]
            act.wait_ge(g_done[u], n + 1)
            act.wait_ge(su_done[u], n + 1)
            act.activation(silu_g[0:m, u], psG[u][0:m, :], ACT.Silu).then_inc(silu_done[u], 1)

        def high(g, j):
            u, n, m = j % 2, 7 * g + j // 2, CH[j]
            act.wait_ge(act_done[u], n + 2)
            act.wait_ge(down_done[u], n + 1)
            act.activation(act_hi[0:m, u], act_f[0:m, u], ACT.Copy).then_inc(acthi_done[u], 1)

        with act.Fori(0, NG) as g:
            for j in range(NCH):
                silu(g, j)
                high(g, j)

    @block.tensor
    def _(pe):
        pe.wait_ge(consts_in, 10 * 16)
        for k in range(HEADS):
            mm = pe.matmul(bank[0][:, k * P:(k + 1) * P], whT[:, k], whT[:, k], start=True, stop=True)
        mm.then_inc(whwh_done, 1)
        pe.wait_ge(wh_ready, 1)

        def s_T(t, u):
            pe.wait_ge(ln.h_done[u], t + 1)
            pe.wait_ge(hT_copied[u], t)
            for c in range(DC):
                mm = pe.transpose(psT[u][:, c * P:(c + 1) * P], h[:, u, c * P:(c + 1) * P], ident[:])
            mm.then_inc(hT_done[u], 1)

        def s_v(t, u):
            pe.wait_ge(ctxT_in[u], 16 * (t + 1))
            pe.wait_ge(v_copied[1 - u], t + u)
            for k in range(HEADS):
                mm = pe.matmul(psV[:, k * P:(k + 1) * P], ctxT[:, u, k], wh[:, k], start=True, stop=True)
            mm.then_inc(v_done[u], 1)

        def s_r(t, u):
            pe.wait_ge(hT_copied[u], t + 1)
            pe.wait_ge(r_copied[1 - u], t + u)
            for k in range(HEADS):
                mm = pe.matmul(psR[:, k * P:(k + 1) * P], whwh[:, k], hT[:, u, k], start=True, stop=True)
            mm.then_inc(r_done[u], 1)

        def s_w(t, u):
            pe.wait_ge(w_copied[1 - u], t + u)
            for c in range(DC):
                mm = pe.matmul(psW[:, 0:D], hT[:, u, c], wg[:, c], start=(c == 0), stop=(c == DC - 1))
            mm.then_inc(w_done[u], 1)

        def s_score(t, u):
            pe.wait_ge(r_copied[u], t + 1)
            first = isinstance(t, int) and t == 0 and u == 0
            last = isinstance(t, int) and t == NB // 2 - 1 and u == 1
            for k in range(HEADS):
                mm = pe.matmul(psS[k][:, 0:P], ctxT[:, u, k], r[:, u, k], start=first, stop=last, skip_group_check=True)
            mm.then_inc(scored[u], 1)

        steps(pe, NB, [(0, s_T), (1, s_score), (0, s_v), (0, s_r), (0, s_w)], peel=4)

        def s_h2T(t, u):
            pe.wait_ge(ln.h_done[u], t + NB // 2 + 1)
            pe.wait_ge(h2lo_done[u], t)
            for c in range(DC):
                mm = pe.transpose(psHT[u][:, c * P:(c + 1) * P], h[:, u, c * P:(c + 1) * P], ident[:])
            mm.then_inc(h2T_done[u], 1)

        def s_wo(t, u):
            pe.wait_ge(prodT_copied[u], t + 1)
            pe.wait_ge(x1_done[1 - u], t + u)
            for c in range(DC):
                mm = pe.matmul(psD[:, 0:D], prodT[:, u, c], wo[:, c], start=(c == 0), stop=(c == DC - 1))
            mm.then_inc(delta_done[u], 1)

        def s_pT(t, u):
            pe.wait_ge(prod_done[u], t + 1)
            pe.wait_ge(prodT_copied[1 - u], t + u)
            for c in range(DC):
                mm = pe.transpose(psPT[:, c * P:(c + 1) * P], prod[:, u, c * P:(c + 1) * P], ident[:])
            mm.then_inc(prodT_done[u], 1)

        def s_o(t, u):
            pe.wait_ge(y_done[u], t)
            for k in range(HEADS):
                mm = pe.matmul(psO[u][:, k * HD:(k + 1) * HD], attT[:, k], entry(v[:], t, u)[:, k * HD:(k + 1) * HD],
                               start=True, stop=True)
            mm.then_inc(o_done[u], 1)

        for u in range(2):
            pe.wait_ge(v_copied[u], NB // 2)
            pe.wait_ge(w_copied[u], NB // 2)
        pe.wait_ge(att_done, 1)
        steps(pe, NB, [(4, s_pT), (0, s_o), (4, s_wo), (7, s_h2T)])

        pe.wait_ge(router_split, 2)
        for u in range(2):
            pe.wait_ge(h2lo_done[u], NB // 2)
        for g in range(NG):
            if g >= 2:
                pe.wait_ge(logitsT_copied, g - 1)
            n = 0
            for c in range(DC):
                for wt, xt in ((router_hi, h2_hi), (router_hi, h2_lo), (router_lo, h2_hi)):
                    mm = pe.matmul(bank[5 + g % 2][:, :], wt[:, c], xt[:, GT * g:GT * (g + 1), c], start=(n == 0), stop=(n == 5))
                    n += 1
            mm.then_inc(logitsT_done, 1)
        pe.wait_ge(logitsT_copied, NG)
        for b in range(NB):
            mm = pe.transpose(bank[0][:, 16 * b:16 * b + NROUTE], lgT[:, b], ident[0:NROUTE, 0:NROUTE])
        mm.then_inc(logits_done, 1)
        pe.wait_ge(gate3_done, 1)
        pe.wait_ge(cast_in, 32)
        for b in range(NB):
            mm = pe.transpose(bank[2 + b // 8][0:3 * NROUTE, :].bitcast(BF16)[:, (b % 8) * P:(b % 8 + 1) * P], gate3[:, b], identb[:])
        mm.then_inc(gatesT_done, 1)
        pe.wait_ge(gatesT_copied, 2)

        for u in range(2):
            pe.sem_inc(down_done[u], 1)

        def up(g, j):
            u, n, m = j % 2, 7 * g + j // 2, CH[j]
            pe.wait_ge(act_done[u], n + 1)
            for ps, base, free, done in ((psG, 0, silu_done, g_done), (psU, DC * HID, su_done, u_done)):
                pe.wait_ge(free[u], n + 1)
                i = 0
                for c in range(DC):
                    cols = base + c * HID + j * P
                    for wt, xt in ((w_hi, h2_hi), (w_hi, h2_lo), (w_lo, h2_hi)):
                        mm = pe.matmul(ps[u][0:m, :], wt[:, cols:cols + m], tokens(xt, g, c), start=(i == 0), stop=(i == 5))
                        i += 1
                mm.then_inc(done[u], 1)
            pe.matmul(psC[u][0:m, :], spread[:, j * P:j * P + m], gates[:].rearrange("q (g b) s -> q g (b s)", g=NG)[:, bass.ds(g, 1)].rearrange("q o n -> q (o n)"),
                      start=True, stop=True).then_inc(spread_done[u], 1)

        def down(g, j):
            u, n, m = j % 2, 7 * g + j // 2, CH[j]
            pe.wait_ge(actlo_done[u], n + 2)
            if j == 0:
                pe.wait_ge(x2_done, 2 * g + 1)
            cols = 2 * DC * HID + j * D
            for i in range(GT):
                for q, (at, wt) in enumerate(((act_hi, w_hi), (act_hi, w_lo), (act_lo, w_hi))):
                    mm = pe.matmul(psY[i // 2][:, (i % 2) * D:(i % 2 + 1) * D], at[0:m, u, i * P:(i + 1) * P], wt[0:m, cols:cols + D],
                                   start=(j == 0 and q == 0 and i % 2 == 0), stop=(j == NCH - 1 and q == 2 and i % 2 == 1),
                                   skip_group_check=True)
            mm.then_inc(down_done[u], 1)

        up(0, 0)
        up(0, 1)
        with pe.Fori(0, NG - 1) as g:
            for j in range(2, NCH):
                up(g, j)
                down(g, j - 2)
            for j in range(2):
                up(g + 1, j)
                down(g, NCH - 2 + j)
        for j in range(2, NCH):
            up(NG - 1, j)
            down(NG - 1, j - 2)
        for j in range(2):
            down(NG - 1, NCH - 2 + j)


def last_layers(nc, a, out, core, bank, x, ident, half, late):
    sb, sem, sem2 = core.sb, core.sem, core.sem2
    ctxn, late_w, wabs_part, late_in = late
    h = sb("h_late", [P, 2, D])
    ln = Norm(core, "ln_late")
    lnq = Norm(core, "ln_quant")
    thetaw = sb("thetaw", [P, P])
    gphiw = sb("gphiw", [P, P])
    outw = sb("outw", [P, P])
    projb = sb("projb", [P, 2])
    gb = sb("gb", [LAT, 1])
    outb = sb("outb", [P, 1])
    lngamma, lnbeta = (sb(n, [LAT, D]) for n in ("lngamma", "lnbeta"))
    mean64 = sb("mean64", [LAT, P])
    gphi = sb("gphi", [P, 2, D])
    theta = sb("theta", [P, 2, D])
    gx = sb("gx", [P, 2, 2, LAT])
    negmax = sb("negmax", [P, 2, 2])
    prob = sb("prob", [P, 2, 2, D])
    probsum = sb("probsum", [P, 2, 2])
    probinv = sb("probinv", [P, 2, 2])
    probT = sb("probT", [P, 2, 2, D])
    tx = sb("tx", [LAT, 2, D])
    tstats = sb("tstats", [LAT, 2, 6])
    tmv = sb("tmv", [LAT, 2, 2])
    tall = sb("tall", [LAT, 2, 2])
    tneg = sb("tneg", [LAT, 2])
    tve = sb("tve", [LAT, 2])
    trstd = sb("trstd", [LAT, 2])
    ty = sb("ty", [LAT, 2, D])
    th = sb("th", [P, 2, D])
    xc = sb("xc", [P, 2, D])
    wabs = sb("wabs", [P, 4])
    ones = sb("ones", [P, P])
    wscale = sb("wscale", [P, 4])
    thr = sb("thr", [P, 2, 3])
    wneg = sb("wneg", [P, 2, 3, P])
    wq = sb("wq", [P, 3, IC * D], BF16)
    hmax = sb("hmax", [P, 2, 3])
    yscale = sb("yscale", [P, 2, 3])
    qf = sb("qf", [P, 2, D])
    xqT = sb("xqT", [P, 2, DC, P], BF16)
    silu2 = sb("silu2", [P, 2, INNER])
    gu = sb("gu", [P, 2, INNER])
    gus = sb("gus", [P, 2, 4])
    oscale = sb("oscale", [P, 2])
    hqT = sb("hqT", [P, 2, IC, P], BF16)
    x4 = sb("x4", [P, 2, D])
    roundc = sb("roundc", [P, 2])

    small_in = sem("small_in")
    late_set = sem("late_set")
    wabs_done = sem("wabs_done")
    wtotal_done = sem("wtotal_done")
    wscale_done = sem("wscale_done")
    wneg_done = sem2("wneg_done")
    wq_done = sem2("wq_done")
    proj_done = sem2("proj_done")
    proj_copied = sem2("proj_copied")
    gx_psum = sem2("gx_psum")
    gx_copied = sem2("gx_copied")
    score_done = sem2("score_done")
    max_done = sem2("max_done")
    exp_done = sem2("exp_done")
    inv_done = sem2("inv_done")
    prob_done = sem2("prob_done")
    probT_done = sem2("probT_done")
    probT_copied = sem2("probT_copied")
    pv_done = sem2("pv_done")
    tx_done = sem2("tx_done")
    tstats_done = sem2("tstats_done")
    tstep = sem2("tstep")
    tmean_done = sem2("tmean_done")
    tve_done = sem2("tve_done")
    trstd_done = sem2("trstd_done")
    ty_done = sem2("ty_done")
    th_done = sem2("th_done")
    out_done = sem2("out_done")
    xc_done = sem2("xc_done")
    x3_done = sem2("x3_done")
    hmax_done = sem2("hmax_done")
    qscale_done = sem2("qscale_done")
    qf_done = sem2("qf_done")
    xqT_done = sem2("xqT_done")
    xqT_copied = sem2("xqT_copied")
    gate_done = sem2("gate_done")
    up_done = sem2("up_done")
    silu2_done = sem2("silu2_done")
    gu_done = sem2("gu_done")
    hqT_done = sem2("hqT_done")
    hqT_copied = sem2("hqT_copied")
    gumax_done = sem2("gumax_done")
    guscale_done = sem2("guscale_done")
    guround_done = sem2("guround_done")
    down2_done = sem2("down2_done")
    x4_done = sem2("x4_done")
    stored = sem2("stored")

    psProj, psScore, psProbT, psTx, psOut, psGx, psMean = bank[0], bank[1:3], bank[3], bank[4], bank[5], bank[6], bank[7]
    psXq, psGate, psUp, psHq, psDown = bank[0], bank[1:3], bank[3:5], bank[5:7], bank[7]
    SMALL = 8

    core.stack.callback(core.end)
    block = core.stack.enter_context(nc.Block())

    @block.sync
    def _(sp):
        for dst, src in ((gphiw, "gphiw"), (thetaw, "thetaw"), (projb, "projb"), (gb, "gb"), (outb, "outb"), (lngamma, "lngamma"),
                         (lnbeta, "lnbeta"), (outw, "outw")):
            sp.dma_start(dst[:], a[src]).then_inc(small_in, 16)

        def store(t, u):
            sp.wait_ge(x4_done[u], t + 1)
            sp.dma_start(out.rearrange("(t u) p d -> t u p d", u=2)[bass.ds(t, 1), u].rearrange("o p d -> p (o d)"), x4[:, u]).then_inc(stored[u], 16)

        steps(sp, NB, [(0, store)])
        for u in range(2):
            sp.wait_ge(stored[u], 16 * NB // 2)

    @block.vector
    def _(dve):
        dve.tensor_reduce(wabs[:, 0:3], wabs_part[:].rearrange("p g i -> p i g"), AX.X, ALU.add).then_inc(wabs_done, 1)
        dve.memset(mean64[:], 1.0 / LAT).then_inc(late_set, 1)
        dve.memset(th[LAT:P], 0.0).then_inc(late_set, 1)
        dve.wait_ge(wtotal_done, 1)
        dve.tensor_scalar(wscale[:, 0:2], psMean[:, 0:2], 1.0 / (INNER * D), Q_EPS, ALU.mult, ALU.add).then_inc(wscale_done, 1)
        dve.tensor_scalar(wscale[:, 3:4], psMean[:, 2:3], 1.0 / (INNER * D), Q_EPS, ALU.mult, ALU.add).then_inc(wscale_done, 1)
        dve.wait_ge(wscale_done, 2)
        for k, half_scale in enumerate((0.5, -0.5)):
            dve.tensor_scalar(thr[:, k, 0:2], wscale[:, 0:2], half_scale, None, ALU.mult).then_inc(wscale_done, 1)
            dve.tensor_scalar(thr[:, k, 2:3], wscale[:, 3:4], half_scale, None, ALU.mult).then_inc(wscale_done, 1)
        dve.tensor_scalar(wscale[:, 2:3], wscale[:, 1:2], 1.0 / 127.0, None, ALU.mult).then_inc(wscale_done, 1)
        dve.wait_ge(wscale_done, 7)

        def c_stats(t, u):
            norm_stats(dve, ln, entry(x[:], t, u), t, u)

        def c_h(t, u):
            stats_landed(dve, ln, t + u, 1 - u)
            dve.wait_ge(proj_done[u], t)
            normalise(dve, ln, h[:, u], entry(x[:], t, u), t, u)

        def c_aggr(t, u):
            norm_aggr(dve, ln, t, u, LN_EPS)

        def c_max(t, u):
            dve.wait_ge(score_done[u], t + 1)
            dve.wait_ge(exp_done[u], t)
            dve.tensor_reduce(negmax[:, u], two(psScore[u], 512), AX.X, ALU.max, negate=True).then_inc(max_done[u], 1)

        def c_inv(t, u):
            dve.wait_ge(exp_done[u], t + 1)
            dve.wait_ge(prob_done[u], t)
            dve.reciprocal(probinv[:, u], probsum[:, u]).then_inc(inv_done[u], 1)

        def c_tstats(t, u):
            dve.wait_ge(tx_done[u], t + 1)
            dve.bn_stats(tstats[:, u], tx[:, u]).then_inc(tstats_done[u], 1)

        def c_var(t, u):
            if not isinstance(t, int):
                dve.wait_ge(tstats_done[1 - u], t + u + 1)
            dve.wait_ge(tmean_done[u], t + 1)
            dve.tensor_copy(tall[:, u], psMean[0:LAT, 0:2]).then_inc(tstep[u], 1)
            dve.wait_ge(tstep[u], 4 * t + 3)
            dve.scalar_tensor_tensor(out=tneg[:, u:u + 1], in0=tall[:, u, 0:1], scalar=tall[:, u, 0:1], in1=tall[:, u, 1:2],
                                     op0=ALU.mult, op1=ALU.subtract).then_inc(tstep[u], 1)
            dve.wait_ge(tstep[u], 4 * t + 4)
            dve.tensor_scalar(tve[:, u:u + 1], tneg[:, u:u + 1], -1.0, LN_EPS, ALU.mult, ALU.add).then_inc(tve_done[u], 1)

        def c_taggr(t, u):
            if isinstance(t, int):
                dve.wait_ge(tstats_done[u], t + 1)
            dve.bn_aggr(tmv[:, u], tstats[:, u]).then_inc(tstep[u], 1)
            dve.wait_ge(tstep[u], 4 * t + 1)
            dve.scalar_tensor_tensor(out=tmv[:, u, 1:2], in0=tmv[:, u, 0:1], scalar=tmv[:, u, 0:1], in1=tmv[:, u, 1:2],
                                     op0=ALU.mult, op1=ALU.add).then_inc(tstep[u], 1)

        def c_y1(t, u):
            dve.wait_ge(th_done[u], t)
            dve.wait_ge(tstep[u], 4 * t + 3)
            dve.scalar_tensor_tensor(out=ty[:, u], in0=tx[:, u], scalar=tall[:, u, 0:1], in1=lngamma[:],
                                     op0=ALU.subtract, op1=ALU.mult).then_inc(ty_done[u], 1)

        def c_y2(t, u):
            dve.wait_ge(ty_done[u], 2 * t + 1)
            dve.wait_ge(trstd_done[u], t + 1)
            dve.scalar_tensor_tensor(out=ty[:, u], in0=ty[:, u], scalar=trstd[:, u:u + 1], in1=lnbeta[:],
                                     op0=ALU.mult, op1=ALU.add).then_inc(ty_done[u], 1)

        def c_x3(t, u):
            dve.wait_ge(out_done[u], t + 1)
            dve.wait_ge(xc_done[u], t + 1)
            dve.scalar_tensor_tensor(out=entry(x[:], t, u), in0=psOut[:, 0:D], scalar=outb[:, 0:1], in1=xc[:, u],
                                     op0=ALU.add, op1=ALU.add).then_inc(x3_done[u], 1)

        def c_wneg(t, u):
            for i in range(3):
                op = dve.tensor_scalar(wneg[:, u, i], entry(late_w[:, i].rearrange("p (b n) -> p b n", b=NB), t, u), thr[:, 1, i:i + 1], None,
                                       ALU.is_lt)
            op.then_inc(wneg_done[u], 1)

        def c_wq(t, u):
            dve.wait_ge(wneg_done[u], t + 1)
            for i in range(3):
                op = dve.scalar_tensor_tensor(out=entry(wq[:, i].rearrange("p (b n) -> p b n", b=NB), t, u),
                                              in0=entry(late_w[:, i].rearrange("p (b n) -> p b n", b=NB), t, u), scalar=thr[:, 0, i:i + 1],
                                              in1=wneg[:, u, i], op0=ALU.is_gt, op1=ALU.subtract)
            op.then_inc(wq_done[u], 1)

        dve.wait_ge(small_in, SMALL * 16)
        steps(dve, NB, [(0, c_stats), (1, c_h), (0, c_aggr), (2, c_max), (4, c_tstats), (5, c_var), (4, c_taggr), (0, c_wneg), (2, c_inv),
                        (5, c_y1), (1, c_wq), (5, c_y2), (6, c_x3)])

        def d_stats(t, u):
            norm_stats(dve, lnq, entry(x[:], t, u), t, u)

        def d_h(t, u):
            stats_landed(dve, lnq, t + u, 1 - u)
            dve.wait_ge(qf_done[u], t)
            normalise(dve, lnq, h[:, u], entry(x[:], t, u), t, u)

        def d_aggr(t, u):
            norm_aggr(dve, lnq, t, u, LN_EPS)

        def d_hmax(t, u):
            dve.wait_ge(lnq.h_done[u], t + 1)
            dve.tensor_reduce(hmax[:, u, 0:1], h[:, u], AX.X, ALU.max, apply_absolute_value=True).then_inc(hmax_done[u], 1)

        def d_hscale(t, u):
            dve.wait_ge(hmax_done[u], 3 * t + 1)
            dve.tensor_scalar(hmax[:, u, 1:2], hmax[:, u, 0:1], 1.0 / 127.0, Q_EPS, ALU.mult, ALU.add).then_inc(hmax_done[u], 1)
            dve.wait_ge(hmax_done[u], 3 * t + 2)
            dve.reciprocal(hmax[:, u, 2:3], hmax[:, u, 1:2]).then_inc(hmax_done[u], 1)
            dve.wait_ge(silu2_done[u], 2 * t)
            dve.tensor_scalar(yscale[:, u], wscale[:, 0:3], hmax[:, u, 1:2], None, ALU.mult).then_inc(qscale_done[u], 1)

        def d_gu(k):
            def stage(t, u):
                dve.wait_ge(silu2_done[u], 2 * t + 2 - k)
                dve.wait_ge(up_done[u], t + 1)
                dve.wait_ge(guround_done[u], t)
                dve.tensor_tensor(gu[:, u, k * 512:(k + 1) * 512], psUp[k][:, :], silu2[:, u, k * 512:(k + 1) * 512],
                                  ALU.mult).then_inc(gu_done[u], 1)
            return stage

        def d_gumax(t, u):
            dve.wait_ge(gu_done[u], 2 * t + 2)
            dve.tensor_reduce(gus[:, u, 0:1], gu[:, u], AX.X, ALU.max, apply_absolute_value=True).then_inc(gumax_done[u], 1)

        def d_guscale(t, u):
            dve.wait_ge(gumax_done[u], t + 1)
            dve.wait_ge(qscale_done[u], t + 1)
            dve.tensor_scalar(gus[:, u, 1:2], gus[:, u, 0:1], yscale[:, u, 2:3], Q_EPS, ALU.mult, ALU.add).then_inc(guscale_done[u], 1)
            dve.wait_ge(guscale_done[u], 4 * t + 1)
            dve.reciprocal(gus[:, u, 2:3], gus[:, u, 1:2]).then_inc(guscale_done[u], 1)
            dve.tensor_scalar(oscale[:, u:u + 1], gus[:, u, 1:2], wscale[:, 3:4], None, ALU.mult).then_inc(guscale_done[u], 1)
            dve.wait_ge(guscale_done[u], 4 * t + 3)
            dve.tensor_scalar(gus[:, u, 3:4], gus[:, u, 2:3], yscale[:, u, 1:2], None, ALU.mult).then_inc(guscale_done[u], 1)

        def d_x4(t, u):
            dve.wait_ge(down2_done[u], t + 1)
            dve.wait_ge(stored[u], 16 * t)
            dve.scalar_tensor_tensor(out=x4[:, u], in0=psDown[:, 0:D], scalar=oscale[:, u:u + 1], in1=entry(x[:], t, u),
                                     op0=ALU.mult, op1=ALU.add).then_inc(x4_done[u], 1)

        steps(dve, NB, [(0, d_stats), (1, d_h), (0, d_aggr), (3, d_gumax), (1, d_hmax), (3, d_guscale), (2, d_gu(1)), (1, d_hscale),
                        (2, d_gu(0)), (4, d_x4)])

    @block.gpsimd
    def _(pool):
        pool.memset(ones[:], 1.0).then_inc(late_set, 1)
        pool.memset(roundc[:, 0:1], ROUND).then_inc(late_set, 1)
        pool.memset(roundc[:, 1:2], -ROUND).then_inc(late_set, 1)

        def c_rstd(t, u):
            norm_rstd(pool, ln, half, t, u)

        def c_prob(t, u):
            pool.wait_ge(inv_done[u], t + 1)
            pool.tensor_tensor(prob[:, u], prob[:, u], probinv[:, u].unsqueeze(2).to_broadcast([P, 2, D]), ALU.mult).then_inc(prob_done[u], 1)

        def c_xc(t, u):
            pool.wait_ge(x3_done[u], t)
            pool.tensor_tensor(xc[:, u], entry(x[:], t, u), entry(ctxn[:], t, u), ALU.add).then_inc(xc_done[u], 1)

        def c_trstd(t, u):
            pool.wait_ge(tve_done[u], t + 1)
            pool.tensor_tensor(trstd[:, u:u + 1], tve[:, u:u + 1], half[0:LAT, u:u + 1], ALU.pow).then_inc(trstd_done[u], 1)

        steps(pool, NB, [(5, c_trstd), (0, c_rstd), (2, c_prob), (5, c_xc)])

        def d_rstd(t, u):
            norm_rstd(pool, lnq, half, t, u)

        steps(pool, NB, [(0, d_rstd)])

    @block.scalar
    def _(act):
        act.wait_ge(small_in, SMALL * 16)

        def c_gphi(t, u):
            act.wait_ge(proj_done[u], t + 1)
            act.wait_ge(score_done[u], t)
            act.wait_ge(gx_psum[u], t)
            act.activation(gphi[:, u], psProj[:, 0:D], ACT.Identity, bias=projb[:, 1:2]).then_inc(proj_copied[u], 1)

        def c_theta(t, u):
            act.wait_ge(proj_done[u], t + 1)
            act.activation(theta[:, u], psProj[:, D:2 * D], ACT.Identity, bias=projb[:, 0:1]).then_inc(proj_copied[u], 1)

        def c_gx(t, u):
            act.wait_ge(gx_psum[u], t + 1)
            act.wait_ge(pv_done[u], t)
            act.activation(gx[:, u], two(psGx)[:, :, 0:LAT], ACT.Copy).then_inc(gx_copied[u], 1)

        def c_exp(t, u):
            act.wait_ge(max_done[u], t + 1)
            act.wait_ge(probT_done[u], t)
            act.wait_ge(inv_done[u], t)
            for k in range(2):
                op = act.activation(prob[:, u, k], psScore[u][:, k * D:(k + 1) * D], ACT.Exp, bias=negmax[:, u, k:k + 1],
                                    accum_out=probsum[:, u, k:k + 1])
            op.then_inc(exp_done[u], 1)

        def c_probT(t, u):
            act.wait_ge(probT_done[u], t + 1)
            act.wait_ge(pv_done[u], t)
            act.activation(probT[:, u], two(psProbT, 512), ACT.Copy).then_inc(probT_copied[u], 1)

        def c_tx(t, u):
            act.wait_ge(pv_done[u], t + 1)
            act.wait_ge(ty_done[u], 2 * t)
            act.wait_ge(tstats_done[u], t)
            act.activation(tx[:, u], psTx[0:LAT, 0:D], ACT.Identity, bias=gb[:, 0:1]).then_inc(tx_done[u], 1)

        def c_th(t, u):
            act.wait_ge(ty_done[u], 2 * t + 2)
            act.wait_ge(out_done[u], t)
            act.activation(th[0:LAT, u], ty[:, u], ACT.Relu).then_inc(th_done[u], 1)

        steps(act, NB, [(0, c_gphi), (0, c_theta), (1, c_gx), (2, c_tx), (4, c_th), (1, c_probT), (0, c_exp)])

        def d_silu(k):
            def stage(t, u):
                act.wait_ge(gate_done[u], t + 1)
                act.wait_ge(hqT_done[u], 2 * t)
                act.activation(silu2[:, u, k * 512:(k + 1) * 512], psGate[k][:, :], ACT.Silu, scale=yscale[:, u, 0:1]).then_inc(silu2_done[u], 1)
            return stage

        def d_round(t, u):
            act.wait_ge(guscale_done[u], 4 * t + 4)
            act.activation(silu2[:, u], gu[:, u], ACT.Identity, bias=roundc[:, 0:1], scale=gus[:, u, 3:4]).then_inc(guround_done[u], 1)

        def d_qf(t, u):
            act.wait_ge(qscale_done[u], t + 1)
            act.wait_ge(xqT_done[u], t)
            act.activation(qf[:, u], h[:, u], ACT.Identity, bias=roundc[:, 0:1], scale=hmax[:, u, 2:3]).then_inc(qf_done[u], 1)

        def d_xqT(t, u):
            act.wait_ge(xqT_done[u], t + 1)
            act.wait_ge(up_done[u], t)
            act.activation(xqT[:, u], two(psXq), ACT.Identity, bias=roundc[:, 1:2]).then_inc(xqT_copied[u], 1)

        def d_hqT(k):
            def stage(t, u):
                act.wait_ge(hqT_done[u], 2 * t + 2 - k)
                act.wait_ge(down2_done[u], t)
                act.activation(hqT[:, u, 4 * k:4 * (k + 1)], psHq[k][:, :].rearrange("p (c n) -> p c n", c=4), ACT.Identity,
                               bias=roundc[:, 1:2]).then_inc(hqT_copied[u], 1)
            return stage

        act.wait_ge(late_set, 5)
        steps(act, NB, [(3, d_hqT(1)), (3, d_hqT(0)), (1, d_silu(1)), (1, d_silu(0)), (2, d_round), (0, d_qf), (0, d_xqT)])

    @block.tensor
    def _(pe):
        pe.wait_ge(late_set, 5)
        pe.wait_ge(wabs_done, 1)
        pe.matmul(psMean[:, 0:3], ones[:], wabs[:, 0:3], start=True, stop=True).then_inc(wtotal_done, 1)

        pe.wait_ge(small_in, SMALL * 16)

        def c_theta(t, u):
            pe.wait_ge(proj_copied[1 - u], 2 * (t + u))
            pe.matmul(psProj[:, D:2 * D], thetaw[:], entry(ctxn[:], t, u), start=True, stop=True)

        def c_gphi(t, u):
            pe.wait_ge(ln.h_done[u], t + 1)
            pe.matmul(psProj[:, 0:D], gphiw[:], h[:, u], start=True, stop=True).then_inc(proj_done[u], 1)

        def c_gx(t, u):
            pe.wait_ge(proj_copied[u], 2 * t + 1)
            pe.wait_ge(gx_copied[1 - u], t + u)
            for k in range(2):
                mm = pe.transpose(psGx[:, k * P:(k + 1) * P], gphi[:, u, k * P:(k + 1) * P], ident[:])
            mm.then_inc(gx_psum[u], 1)

        def c_score(t, u):
            pe.wait_ge(proj_copied[u], 2 * t + 2)
            pe.wait_ge(exp_done[u], t)
            for k in range(2):
                mm = pe.matmul(psScore[u][:, k * D:(k + 1) * D], theta[:, u, k * P:(k + 1) * P], gphi[:, u], start=True, stop=True)
            mm.then_inc(score_done[u], 1)

        def c_probT(t, u):
            pe.wait_ge(prob_done[u], t + 1)
            pe.wait_ge(probT_copied[1 - u], t + u)
            for sh in range(2):
                for th_ in range(2):
                    mm = pe.transpose(psProbT[:, sh * D + th_ * P:sh * D + (th_ + 1) * P], prob[:, u, th_, sh * P:(sh + 1) * P], ident[:])
            mm.then_inc(probT_done[u], 1)

        def c_pv(t, u):
            pe.wait_ge(probT_copied[u], t + 1)
            pe.wait_ge(gx_copied[u], t + 1)
            pe.wait_ge(tx_done[1 - u], t + u)
            for k in range(2):
                mm = pe.matmul(psTx[0:LAT, 0:D], gx[:, u, k], probT[:, u, k], start=(k == 0), stop=(k == 1))
            mm.then_inc(pv_done[u], 1)

        def c_mean(t, u):
            pe.wait_ge(tstep[u], 4 * t + 2)
            pe.wait_ge(tve_done[1 - u], t + u)
            pe.matmul(psMean[:, 0:2], mean64[:], tmv[:, u], start=True, stop=True).then_inc(tmean_done[u], 1)

        def c_out(t, u):
            pe.wait_ge(th_done[u], t + 1)
            pe.wait_ge(x3_done[1 - u], t + u)
            pe.matmul(psOut[:, 0:D], outw[:], th[:, u], start=True, stop=True).then_inc(out_done[u], 1)

        steps(pe, NB, [(4, c_mean), (2, c_probT), (0, c_theta), (5, c_out), (0, c_gphi), (2, c_pv), (1, c_gx), (0, c_score)])

        for u in range(2):
            pe.wait_ge(wq_done[u], NB // 2)
            pe.wait_ge(x3_done[u], NB // 2)

        def d_xqT(t, u):
            pe.wait_ge(qf_done[u], t + 1)
            pe.wait_ge(xqT_copied[1 - u], t + u)
            for c in range(DC):
                mm = pe.transpose(psXq[:, c * P:(c + 1) * P], qf[:, u, c * P:(c + 1) * P], ident[:])
            mm.then_inc(xqT_done[u], 1)

        def both(ps, i, u):
            for k in range(2):
                for c in range(DC):
                    mm = pe.matmul(ps[k][:, :], xqT[:, u, c], wq[:, i, c * INNER + k * 512:c * INNER + (k + 1) * 512],
                                   start=(c == 0), stop=(c == DC - 1))
            return mm

        def d_gate(t, u):
            pe.wait_ge(xqT_copied[u], t + 1)
            pe.wait_ge(silu2_done[1 - u], 2 * (t + u))
            both(psGate, 0, u).then_inc(gate_done[u], 1)

        def d_up(t, u):
            pe.wait_ge(gu_done[1 - u], 2 * (t + u))
            both(psUp, 1, u).then_inc(up_done[u], 1)

        def d_hqT(k):
            def stage(t, u):
                pe.wait_ge(guround_done[u], t + 1)
                pe.wait_ge(hqT_copied[1 - u], 2 * (t + u))
                for c in range(4):
                    n = (4 * k + c) * P
                    mm = pe.transpose(psHq[k][:, c * P:(c + 1) * P], silu2[:, u, n:n + P], ident[:])
                mm.then_inc(hqT_done[u], 1)
            return stage

        def d_down(t, u):
            pe.wait_ge(hqT_copied[u], 2 * t + 2)
            pe.wait_ge(x4_done[1 - u], t + u)
            for c in range(IC):
                mm = pe.matmul(psDown[:, 0:D], hqT[:, u, c], wq[:, 2, c * D:(c + 1) * D], start=(c == 0), stop=(c == IC - 1))
            mm.then_inc(down2_done[u], 1)

        steps(pe, NB, [(1, d_up), (3, d_down), (2, d_hqT(1)), (0, d_xqT), (2, d_hqT(0)), (0, d_gate)])


def kernel(x, ctx_2048, L0_xattn_Wh, L0_xattn_wg_w, L0_xattn_wo_w, L0_xattn_gn_gamma, L0_xattn_gn_beta,
           L0_ffn_gate_w, L0_ffn_w_gate, L0_ffn_w_up, L0_ffn_w_down, L0_ffn_shgate_w, L0_ffn_shw_gate,
           L0_ffn_shw_up, L0_ffn_shw_down, L1_xattn_theta_w, L1_xattn_theta_b, L1_xattn_phi_w,
           L1_xattn_phi_b, L1_xattn_g_w, L1_xattn_g_b, L1_xattn_ln_gamma, L1_xattn_ln_beta,
           L1_xattn_out_w, L1_xattn_out_b, L1_ffn_w_gate, L1_ffn_w_up, L1_ffn_w_down):
    import numpy as np
    import concourse.bacc as bacc
    from concourse.bass_utils import run_bass_kernel_spmd

    arr = np.asarray
    c = np.ascontiguousarray

    def rows(m):
        return c(m.reshape(-1, P, m.shape[1]).transpose(1, 0, 2))

    def side(experts, shared):
        return np.concatenate([arr(experts).transpose(1, 0, 2).reshape(D, -1), arr(shared)], 1)

    down = np.concatenate([arr(L0_ffn_w_down).reshape(-1, D), arr(L0_ffn_shw_down), np.zeros((NCH * P - HID, D), np.float32)], 0)
    gates = np.concatenate([arr(L0_ffn_gate_w), arr(L0_ffn_shgate_w)[None], np.zeros((P - NROUTE, D), np.float32)], 0)
    wh = arr(L0_xattn_Wh)
    none = np.zeros((P, P - LAT), np.float32)
    arrays = {
        "x": c(arr(x)), "ctx": c(arr(ctx_2048)),
        "ctxT": c(arr(ctx_2048).reshape(NB, P, HEADS, HD).transpose(3, 0, 2, 1)),
        "wh": c(wh.transpose(1, 0, 2)), "whT": c(wh.transpose(2, 0, 1)),
        "wg": rows(arr(L0_xattn_wg_w)), "wo": rows(arr(L0_xattn_wo_w)),
        "gamma": c(np.broadcast_to(arr(L0_xattn_gn_gamma), (P, D))),
        "beta": c(np.broadcast_to(arr(L0_xattn_gn_beta), (P, D))),
        "wpack": c(np.concatenate([rows(m).reshape(P, -1) for m in
                                   (side(L0_ffn_w_gate, L0_ffn_shw_gate), side(L0_ffn_w_up, L0_ffn_shw_up), down)], 1)),
        "router": rows(c(gates.T)),
        "thetaw": c(np.concatenate([none, arr(L1_xattn_theta_w).T], 1)),
        "gphiw": c(np.concatenate([arr(L1_xattn_g_w).T, arr(L1_xattn_phi_w).T], 1)),
        "outw": c(np.concatenate([arr(L1_xattn_out_w).T, none.T], 0)),
        "projb": c(np.stack([np.concatenate([none[0], arr(b)]) for b in (L1_xattn_theta_b, L1_xattn_phi_b)], 1)),
        "gb": c(arr(L1_xattn_g_b)[:, None]), "outb": c(arr(L1_xattn_out_b)[:, None]),
        "lngamma": c(arr(L1_xattn_ln_gamma)), "lnbeta": c(arr(L1_xattn_ln_beta)),
        "qgate": rows(arr(L1_ffn_w_gate).T), "qup": rows(arr(L1_ffn_w_up).T), "qdown": rows(arr(L1_ffn_w_down).T),
        **constants(),
    }
    nc = bacc.Bacc("TRN2", target_bir_lowering=False, num_devices=1)
    aps = {k: nc.dram_tensor(f"in_{k}", m.shape, mybir.dt.from_np(m.dtype), kind="ExternalInput").ap() for k, m in arrays.items()}
    out = nc.dram_tensor("out", (NB, P, D), F32, kind="ExternalOutput").ap()
    program(nc, aps, out)
    r = run_bass_kernel_spmd(nc, [{f"in_{k}": m for k, m in arrays.items()}], core_ids=[0])
    return r.results[0]["out"]


def constants():
    import numpy as np

    gamma = 1.0 - 2.0 ** (-5.0 - np.arange(HEADS))
    late = np.arange(P)[None, :] - np.arange(P)[:, None]
    mask = np.where(late[None] <= 0, gamma[:, None, None] ** late[None].astype(np.float64), 0.0)
    mask = mask / np.sqrt(mask.sum(-1))[:, None, :]
    spread = np.zeros((3, NROUTE, NCH * P), np.float32)
    for e in range(NE):
        spread[:, e, e * HE:(e + 1) * HE] = 1.0
    spread[:, NE, NE * HE:HID] = 1.0
    before = np.broadcast_to(np.tril(np.ones((NE, NE), np.float32), -1), (P, NE, NE))
    return {
        "ident": np.eye(P, dtype=np.float32),
        "decayT": np.ascontiguousarray((mask / np.sqrt(HD)).transpose(2, 0, 1).astype(np.float32)),
        "spread": spread.reshape(3 * NROUTE, NCH * P),
        "before": np.ascontiguousarray(before),
    }
```

```python
from contextlib import ExitStack

import concourse.bass as bass
from concourse import mybir

ALU = mybir.AluOpType
ACT = mybir.ActivationFunctionType
AX = mybir.AxisListType
F32 = mybir.dt.float32
F32R = mybir.dt.float32r
BF16 = mybir.dt.bfloat16

P = 128
NB = 16
D = 256
DC = D // P
HEADS, HD = 2, 128
NE, HE, HS = 8, 176, 352
HID = NE * HE + HS
NCH = -(-HID // P)
CH = [min(P, HID - P * j) for j in range(NCH)]
NROUTE = NE + 1
GT = 4
NG = NB // GT
GN = GT * P
WPACK = 2 * DC * HID + NCH * D
WSTEP = WPACK // (2 * NB)
LAT = 64
INNER = 1024
IC = INNER // P
LN_EPS, GN_EPS, Q_EPS = 1e-5, 1e-3, 1e-5
ROUND = 12582912.0
assert WPACK % (2 * NB) == 0


def steps(eng, count, stages, peel=0):
    deepest = max(lag for lag, _ in stages)

    def peeled(i):
        for lag, f in stages:
            if 0 <= i - lag < count:
                f((i - lag) // 2, (i - lag) % 2)

    first = max(deepest + deepest % 2 + 2, peel)
    for i in range(first):
        peeled(i)
    with eng.Fori(first // 2, count // 2) as t:
        for u in range(2):
            for lag, f in stages:
                f(t + (u - lag) // 2, (u - lag) % 2)
    for i in range(count, count + deepest):
        peeled(i)


def entry(tile, t, u):
    rest = " ".join("abc"[: len(tile.shape) - 2])
    v = tile.rearrange(f"p (t u) {rest} -> p t u {rest}", u=2)
    return v[:, bass.ds(t, 1), u].rearrange(f"p o {rest} -> p (o {rest.split()[0]}) {' '.join(rest.split()[1:])}")


SMALL = [("gphiw", [P, P]), ("thetaw", [P, P]), ("projb", [P, 2]), ("gb", [LAT, 1]), ("outb", [P, 1]), ("lngamma", [LAT, D]),
         ("lnbeta", [LAT, D]), ("outw", [P, P])]


def part(packed, t, u, base):
    return packed.rearrange("p (t u n) -> p t u n", u=2, n=WSTEP)[:, bass.ds(t + base, 1), u].rearrange("p o n -> p (o n)")


class Core:

    def __init__(self, nc, stack):
        self.nc, self.stack, self.sems = nc, stack, []

    def sb(self, name, shape, dt=F32, stack=None):
        return (stack or self.stack).enter_context(self.nc.sbuf_tensor(name, shape, dt))

    def sem(self, name):
        self.sems.append(self.nc.alloc_semaphore(name=name))
        return self.sems[-1]

    def sem2(self, name):
        return [self.sem(f"{name}{u}") for u in range(2)]

    def end(self):
        self.nc.all_engine_barrier()
        self.nc.clear_and_free_semaphores(self.sems)
        self.nc.all_engine_barrier()


class Norm:

    def __init__(self, core, name, rows=P):
        self.stats = core.sb(f"{name}_stats", [rows, 2, 6])
        self.mv = core.sb(f"{name}_mv", [rows, 2, 2])
        self.ve = core.sb(f"{name}_ve", [rows, 2])
        self.rstd = core.sb(f"{name}_rstd", [rows, 2])
        self.stats_done = core.sem2(f"{name}_stats_done")
        self.mv_done = core.sem2(f"{name}_mv_done")
        self.ve_done = core.sem2(f"{name}_ve_done")
        self.rstd_done = core.sem2(f"{name}_rstd_done")
        self.h_done = core.sem2(f"{name}_h_done")


def two(ap, n=D):
    return ap[:, 0:n].rearrange("p (c n) -> p c n", c=2)



def norm_stats(dve, n, src, t, u, base=0):
    dve.bn_stats(n.stats[:, u], src).then_inc(n.stats_done[u], 1)


def stats_landed(dve, n, t, u, base=0):
    if not isinstance(t, int):
        dve.wait_ge(n.stats_done[u], t + base + 1)


def norm_aggr(dve, n, t, u, eps, base=0):
    if isinstance(t, int):
        dve.wait_ge(n.stats_done[u], t + base + 1)
    dve.bn_aggr(n.mv[:, u], n.stats[:, u]).then_inc(n.mv_done[u], 1)
    dve.wait_ge(n.mv_done[u], t + base + 1)
    dve.wait_ge(n.rstd_done[u], t + base)
    dve.tensor_scalar(n.ve[:, u:u + 1], n.mv[:, u, 1:2], eps, None, ALU.add).then_inc(n.ve_done[u], 1)


def norm_rstd(pool, n, half, t, u, base=0):
    pool.wait_ge(n.ve_done[u], t + base + 1)
    pool.tensor_tensor(n.rstd[:, u:u + 1], n.ve[:, u:u + 1], half[:, u:u + 1], ALU.pow).then_inc(n.rstd_done[u], 1)


def normalise(dve, n, out, src, t, u, base=0):
    dve.wait_ge(n.rstd_done[u], t + base + 1)
    dve.tensor_scalar(out, src, n.mv[:, u, 0:1], n.rstd[:, u:u + 1], ALU.subtract, ALU.mult).then_inc(n.h_done[u], 1)


def program(nc, a, out):
    with ExitStack() as stack:
        whole = Core(nc, stack)
        bank = [stack.enter_context(nc.psum_tensor(f"bank{i}", [P, 512], F32)) for i in range(8)]
        x = whole.sb("x", [P, NB, D])
        ident = whole.sb("ident", [P, P])
        identb = whole.sb("identb", [P, P], BF16)
        half = whole.sb("half", [P, 2])
        kept = whole.sb("kept", [P, NB, D])
        late_w = whole.sb("late_w", [P, 3, IC * D])
        wabs_part = whole.sb("wabs_part", [P, NG, 3])
        wscale = whole.sb("wscale", [P, 4])
        late_in = whole.sem("late_in")
        small = [whole.sb(name, shape) for name, shape in SMALL]
        late = (kept, late_w, wabs_part, wscale, small, late_in)
        with ExitStack() as part:
            first_layers(nc, a, Core(nc, part), bank, x, ident, identb, half, late)
        with ExitStack() as part:
            last_layers(nc, a, out, Core(nc, part), bank, x, ident, half, late)


def first_layers(nc, a, core, bank, x, ident, identb, half, late):
    sb, sem, sem2 = core.sb, core.sem, core.sem2
    h = sb("h", [P, 2, D])
    ln, gn = Norm(core, "ln"), Norm(core, "gn")
    v, late_w, wabs_part, wscale, small, late_in = late
    w = late_w[:, 0:2].rearrange("p i (b d) -> p (i b) d", b=NB // 2)
    used = 0

    def beside_w(n):
        nonlocal used
        used += n
        return late_w[:, 2, used - n:used]

    w_raw = beside_w(2 * WSTEP).rearrange("p (u n) -> p u n", u=2)
    ctxT = beside_w(2 * D).rearrange("p (u h s) -> p u h s", u=2, h=HEADS)
    r = beside_w(2 * D).rearrange("p (u h s) -> p u h s", u=2, h=HEADS)
    whT = beside_w(HEADS * HD).rearrange("p (h e) -> p h e", h=HEADS)
    s2 = ExitStack()
    w_hi = sb("w_hi", [P, WPACK], F32R, s2)
    w_lo = sb("w_lo", [P, WPACK], F32R, s2)
    h2_hi = sb("h2_hi", [P, NB, DC, P], F32R, s2)
    h2_lo = sb("h2_lo", [P, NB, DC, P], F32R, s2)
    gates = sb("gates", [3 * NROUTE, NB, P], BF16, s2)
    ones = sb("ones", [P, P], F32, s2)
    wabs = sb("wabs", [P, 3], F32, s2)
    thr = sb("thr", [P, 2, 3], F32, s2)
    spread = sb("spread", [3 * NROUTE, NCH * P], BF16, s2)
    s3 = ExitStack()
    hT = sb("hT", [P, 2, DC, P], F32, s3)
    wh = sb("wh", [P, HEADS, HD], F32, s3)
    whwh = sb("whwh", [P, HEADS, HD], F32, s3)
    wg = sb("wg", [P, DC, D], F32, s3)
    wo = sb("wo", [P, DC, D], F32, s3)
    decayT = sb("decayT", [P, HEADS, P], F32, s3)
    attT = sb("attT", [P, HEADS, P], F32, s3)
    gamma = sb("gamma", [P, D], F32, s3)
    beta = sb("beta", [P, D], F32, s3)
    nmr = sb("nmr", [P, 2], F32, s3)
    router = sb("router", [P, DC, P], F32, s3)
    router_hi = sb("router_hi", [P, DC, P], F32R, s3)
    router_lo = sb("router_lo", [P, DC, P], F32R, s3)
    y = hT[:].rearrange("p u c s -> p u (c s)")
    prod = sb("prod", [P, 2, D], F32, s3)
    prodT = sb("prodT", [P, 2, DC, P], F32, s3)

    s3.close()
    s5 = ExitStack()
    silu_g = sb("silu_g", [P, 2, GN], F32, s5)
    act_f = sb("act_f", [P, 2, GN], F32, s5)
    act_hi = sb("act_hi", [P, 2, GN], F32R, s5)
    act_lo = sb("act_lo", [P, 2, GN], F32R, s5)
    wneg = sb("wneg", [P, 2, 512], F32, s5)
    wfirst = sb("wfirst", [P, 512], BF16, s5)
    gate3 = sb("gate3", [P, NB, 3 * NROUTE], BF16, s5)
    s5.close()
    lgT = v[0:NROUTE, :, 0:P]
    lg = v[:, :, P:P + NROUTE]
    gate = v[:, :, P + 16:P + 16 + NROUTE]
    rest = v[:, :, P + 32:P + 32 + NROUTE]
    above = w[:, :, 0:NE * NE].rearrange("p b (e f) -> p b e f", e=NE)
    rank = w[:, :, P:P + NE]
    chosen = w[:, :, P + 16:P + 16 + NROUTE]
    mine = w[:, :, P + 32:P + 32 + NE]
    middle = w[:, :, P + 48:P + 49]
    s2.close()

    first_in = sem("first_in")
    consts_in = sem("consts_in")
    cast_in = sem("cast_in")
    x_in = sem2("x_in")
    ctxT_in = sem2("ctxT_in")
    wraw_in = sem2("wraw_in")
    exponents = sem("exponents")
    wh_ready = sem("wh_ready")
    whwh_done = sem("whwh_done")
    hT_done = sem2("hT_done")
    hT_copied = sem2("hT_copied")
    v_done = sem2("v_done")
    v_copied = sem2("v_copied")
    r_done = sem2("r_done")
    r_copied = sem2("r_copied")
    w_done = sem2("w_done")
    w_copied = sem2("w_copied")
    scored = sem2("scored")
    whi_done = sem2("whi_done")
    wlo_done = sem2("wlo_done")
    att_masked = sem("att_masked")
    att_done = sem("att_done")
    router_split = sem("router_split")
    o_done = sem2("o_done")
    nmr_done = sem2("nmr_done")
    y_done = sem2("y_done")
    yg_done = sem2("yg_done")
    yb_done = sem2("yb_done")
    prod_done = sem2("prod_done")
    prodT_done = sem2("prodT_done")
    prodT_copied = sem2("prodT_copied")
    delta_done = sem2("delta_done")
    x1_done = sem2("x1_done")
    h2T_done = sem2("h2T_done")
    h2hi_done = sem2("h2hi_done")
    h2lo_done = sem2("h2lo_done")
    logitsT_done = sem("logitsT_done")
    logitsT_copied = sem("logitsT_copied")
    logits_done = sem("logits_done")
    routing = sem("routing")
    tanh_done = sem("tanh_done")
    gate3_done = sem("gate3_done")
    gatesT_done = sem("gatesT_done")
    gatesT_copied = sem("gatesT_copied")
    g_done = sem2("g_done")
    u_done = sem2("u_done")
    spread_done = sem2("spread_done")
    silu_done = sem2("silu_done")
    su_done = sem2("su_done")
    act_done = sem2("act_done")
    acthi_done = sem2("acthi_done")
    actlo_done = sem2("actlo_done")
    down_done = sem2("down_done")
    x2_done = sem("x2_done")
    wabs_done = sem("wabs_done")
    wtotal_done = sem("wtotal_done")
    wscale_done = sem("wscale_done")
    wneg_done = sem("wneg_done")
    wfirst_done = sem("wfirst_done")

    psT, psV, psR, psW = [bank[0], bank[1]], bank[2], bank[3], bank[4]
    psS = [bank[5], bank[6]]
    psO, psPT, psD, psHT = [bank[0], bank[1]], bank[2], bank[3], [bank[4], bank[7]]

    psG, psU, psC, psY = bank[0:2], bank[2:4], bank[4:6], bank[6:8]

    def tokens(ap, g, c):
        return ap[:].rearrange("p (g b) c s -> p g b c s", g=NG)[:, bass.ds(g, 1), :, c].rearrange("p o b s -> p (o b) s")

    core.stack.callback(core.end)
    block = core.stack.enter_context(nc.Block())

    ROUTED = 9

    @block.sync
    def _(sp):
        for dst, src in ((whT, "whT"), (ident, "ident"), (wh, "wh"), (wg, "wg")):
            sp.dma_start(dst[:], a[src]).then_inc(first_in, 16)

        def load_x(t, u):
            sp.wait_ge(x_in[u], 16 * t)
            sp.dma_start(entry(x[:], t, u), a["x"].rearrange("(t u) p d -> t u p d", u=2)[bass.ds(t, 1), u].rearrange("o p d -> p (o d)")).then_inc(x_in[u], 16)

        def load_ctxT(t, u):
            sp.wait_ge(ctxT_in[u], 16 * t)
            sp.wait_ge(scored[u], t)
            sp.dma_start(ctxT[:, u], a["ctxT"].rearrange("p (t u) h s -> p t u h s", u=2)[:, bass.ds(t, 1), u].rearrange("p o h s -> p (o h) s")).then_inc(ctxT_in[u], 16)

        steps(sp, NB, [(0, load_x), (2, load_ctxT)])

        for u in range(2):
            sp.wait_ge(wlo_done[u], NB)
        sp.wait_ge(gatesT_copied, 2)
        sp.dma_start(v[:], a["ctx"].rearrange("b p d -> p b d")).then_inc(late_in, 16)
        for i, src in enumerate(("qgate", "qup", "qdown")):
            sp.dma_start(late_w[:, i], a[src].rearrange("p c n -> p (c n)")).then_inc(late_in, 16)
        for dst, (src, _) in zip(small, SMALL):
            sp.dma_start(dst[:], a[src]).then_inc(late_in, 16)

    @block.vector
    def _(dve):
        def s_stats(t, u):
            dve.wait_ge(x_in[u], 16 * (t + 1))
            dve.wait_ge(ln.h_done[u], t)
            norm_stats(dve, ln, entry(x[:], t, u), t, u)

        def s_aggr(t, u):
            norm_aggr(dve, ln, t, u, LN_EPS)

        def s_h(t, u):
            stats_landed(dve, ln, t + u, 1 - u)
            dve.wait_ge(hT_done[u], t)
            normalise(dve, ln, h[:, u], entry(x[:], t, u), t, u)

        def s_w(t, u):
            dve.wait_ge(w_done[u], t + 1)
            dve.tensor_scalar(entry(w[:], t, u), psW[:, 0:D], 0.0, None, ALU.max).then_inc(w_copied[u], 1)

        steps(dve, NB, [(3, s_w), (0, s_stats), (1, s_h), (0, s_aggr)])
        dve.wait_ge(consts_in, 5 * 16)
        for u in range(2):
            dve.wait_ge(scored[u], NB // 2)
        for k in range(HEADS):
            dve.tensor_tensor(attT[:, k], psS[k][:, 0:P], decayT[:, k], ALU.mult).then_inc(att_masked, 1)
        dve.wait_ge(att_masked, HEADS)
        dve.scalar_tensor_tensor(out=attT[:], in0=attT[:], scalar=-1.0, in1=attT[:], op0=ALU.mult, op1=ALU.max).then_inc(att_masked, 1)
        dve.wait_ge(att_masked, HEADS + 1)
        dve.tensor_scalar(attT[:], attT[:], 1.0, None, ALU.max).then_inc(att_done, 1)

        def s_h2(t, u):
            dve.wait_ge(h2T_done[u], t)
            if not isinstance(t, int):
                dve.wait_ge(x1_done[u], t + 2)
            normalise(dve, ln, h[:, u], entry(x[:], t, u), t, u, NB // 2)

        def s_prod(t, u):
            stats_landed(dve, ln, t - 1, u, NB // 2)
            dve.wait_ge(yb_done[u], t + 1)
            dve.wait_ge(prodT_done[u], t)
            dve.tensor_tensor(prod[:, u], y[:, u], entry(w[:], t, u), ALU.mult).then_inc(prod_done[u], 1)

        def s_x1(t, u):
            dve.wait_ge(delta_done[u], t + 1)
            dve.tensor_tensor(entry(x[:], t, u), psD[:, 0:D], entry(x[:], t, u), ALU.add).then_inc(x1_done[u], 1)

        def s_stats2(t, u):
            if isinstance(t, int):
                dve.wait_ge(x1_done[u], t + 1)
            norm_stats(dve, ln, entry(x[:], t, u), t, u, NB // 2)

        def s_lo(t, u):
            dve.wait_ge(h2hi_done[u], t + 1)
            dve.tensor_tensor(entry(h2_lo[:], t, u), two(psHT[u]), entry(h2_hi[:], t, u).bitcast(F32),
                              ALU.subtract).then_inc(h2lo_done[u], 1)

        def s_aggr2(t, u):
            norm_aggr(dve, ln, t, u, LN_EPS, NB // 2)

        def s_gstats(t, u):
            dve.wait_ge(o_done[u], t + 1)
            norm_stats(dve, gn, psO[u][:, 0:D], t, u)

        def s_nmr(t, u):
            stats_landed(dve, gn, t + u, 1 - u)
            dve.wait_ge(gn.rstd_done[u], t + 1)
            dve.wait_ge(y_done[u], t)
            dve.scalar_tensor_tensor(out=nmr[:, u:u + 1], in0=gn.mv[:, u, 0:1], scalar=-1.0, in1=gn.rstd[:, u:u + 1],
                                     op0=ALU.mult, op1=ALU.mult).then_inc(nmr_done[u], 1)

        def s_gaggr(t, u):
            norm_aggr(dve, gn, t, u, GN_EPS)

        steps(dve, NB, [(0, s_gstats), (1, s_nmr), (0, s_gaggr), (4, s_x1), (6, s_h2), (4, s_stats2), (2, s_prod), (4, s_aggr2), (7, s_lo)])
        for u in range(2):
            dve.sem_inc(su_done[u], 1)
            dve.sem_inc(act_done[u], 1)
        dve.sem_inc(x2_done, 1)

        step = [0]

        def then(op):
            step[0] += 1
            op.then_inc(routing, 1)
            dve.wait_ge(routing, step[0])

        dve.memset(chosen, 0.5)
        then(dve.memset(above, 0.0))
        dve.wait_ge(logits_done, 1)
        then(dve.tensor_copy(lg, bank[7][:, 0:16 * NB].rearrange("p (b e) -> p b e", b=NB)[:, :, 0:NROUTE]))
        for e in range(NE):
            own = lg[:, :, e:e + 1]
            if e:
                op = dve.tensor_tensor(above[:, :, e, 0:e], lg[:, :, 0:e], own.to_broadcast([P, NB, e]), ALU.is_ge)
            if e < NE - 1:
                op = dve.tensor_tensor(above[:, :, e, e + 1:NE], lg[:, :, e + 1:NE], own.to_broadcast([P, NB, NE - 1 - e]), ALU.is_gt)
        then(op)
        then(dve.tensor_reduce(rank, above, AX.X, ALU.add))
        then(dve.tensor_scalar(chosen[:, :, 0:NE], rank, 2.0, 0.5, ALU.is_lt, ALU.mult))
        then(dve.tensor_tensor(mine, chosen[:, :, 0:NE], lg[:, :, 0:NE], ALU.mult))
        then(dve.tensor_reduce(middle, mine, AX.X, ALU.add))
        then(dve.tensor_tensor(gate[:, :, 0:NE], lg[:, :, 0:NE], middle.to_broadcast([P, NB, NE]), ALU.subtract))
        then(dve.tensor_scalar(gate[:, :, NE:NROUTE], lg[:, :, NE:NROUTE], 0.5, None, ALU.mult))
        dve.wait_ge(tanh_done, 1)
        then(dve.scalar_tensor_tensor(out=gate, in0=gate, scalar=1.0, in1=chosen, op0=ALU.add, op1=ALU.mult))
        for q in range(3):
            part = gate3[:, :, q * NROUTE:(q + 1) * NROUTE]
            then(dve.tensor_copy(part, gate if q == 0 else rest))
            if q < 2:
                then(dve.tensor_tensor(rest, gate if q == 0 else rest, part, ALU.subtract))
        dve.sem_inc(gate3_done, 1)
        dve.wait_ge(gatesT_done, 1)
        for k in range(2):
            dve.tensor_copy(gates[:, 8 * k:8 * (k + 1)], bank[4 + k][0:3 * NROUTE, :].bitcast(BF16).rearrange("q (b s) -> q b s", b=8)).then_inc(gatesT_copied, 1)

        def weigh(g, j):
            u, n, m = j % 2, 7 * g + j // 2, CH[j]
            dve.wait_ge(silu_done[u], n + 2)
            dve.wait_ge(u_done[u], n + 1)
            dve.wait_ge(acthi_done[u], n + 1)
            dve.wait_ge(actlo_done[u], n + 1)
            dve.tensor_tensor(act_f[0:m, u], silu_g[0:m, u], psU[u][0:m, :], ALU.mult).then_inc(su_done[u], 1)
            dve.wait_ge(su_done[u], n + 2)
            dve.wait_ge(spread_done[u], n + 1)
            dve.tensor_tensor(act_f[0:m, u], act_f[0:m, u], psC[u][0:m, :], ALU.mult).then_inc(act_done[u], 1)

        def add_down(g):
            dve.wait_ge(down_done[0], 7 * g + 8)
            dve.wait_ge(down_done[1], 7 * g + 8)
            for k in range(2):
                xs = x[:].rearrange("p (g i) d -> p g i d", g=NG)[:, bass.ds(g, 1), 2 * k:2 * k + 2].rearrange("p o i d -> p (o i d)")
                dve.tensor_tensor(xs, psY[k][:, :], xs, ALU.add).then_inc(x2_done, 1)

        def weights_abs(g):
            dve.wait_ge(late_in, (4 + len(SMALL)) * 16)
            return dve.tensor_reduce(wabs_part[:, bass.ds(g, 1)].rearrange("p o i -> p (o i)"),
                                     late_w[:].rearrange("p i (g n) -> p g i n", g=NG)[:, bass.ds(g, 1)].rearrange("p o i n -> p (o i) n"),
                                     AX.X, ALU.add, apply_absolute_value=True)

        def weights_scale():
            dve.wait_ge(wtotal_done, 1)
            dve.tensor_scalar(wscale[:, 0:2], psC[0][:, 0:2], 1.0 / (INNER * D), Q_EPS, ALU.mult, ALU.add).then_inc(wscale_done, 1)
            dve.tensor_scalar(wscale[:, 3:4], psC[0][:, 2:3], 1.0 / (INNER * D), Q_EPS, ALU.mult, ALU.add).then_inc(wscale_done, 1)
            dve.wait_ge(wscale_done, 2)
            for k, factor in enumerate((0.5, -0.5)):
                dve.tensor_scalar(thr[:, k, 0:2], wscale[:, 0:2], factor, None, ALU.mult).then_inc(wscale_done, 1)
                dve.tensor_scalar(thr[:, k, 2:3], wscale[:, 3:4], factor, None, ALU.mult).then_inc(wscale_done, 1)
            dve.tensor_scalar(wscale[:, 2:3], wscale[:, 1:2], 1.0 / 127.0, None, ALU.mult).then_inc(wscale_done, 1)
            dve.wait_ge(wscale_done, 7)

        def quantise(q):
            i, k = q // 4, q % 4
            raw = late_w[:, i, 512 * k:512 * (k + 1)]
            dst = late_w[:, i].bitcast(BF16)[:, 512 * k:512 * (k + 1)]
            dve.tensor_scalar(wneg[:, q % 2], raw, thr[:, 1, i:i + 1], None, ALU.is_lt).then_inc(wneg_done, 1)
            dve.wait_ge(wneg_done, q + 1)
            if k == 0:
                dve.wait_ge(wfirst_done, 2 * i)
            op = dve.scalar_tensor_tensor(out=wfirst[:] if k == 0 else dst, in0=raw, scalar=thr[:, 0, i:i + 1], in1=wneg[:, q % 2],
                                          op0=ALU.is_gt, op1=ALU.subtract)
            if k == 0:
                op.then_inc(wfirst_done, 1)
                dve.wait_ge(wfirst_done, 2 * i + 1)
                dve.tensor_copy(dst, wfirst[:]).then_inc(wfirst_done, 1)

        weigh(0, 0)
        weigh(0, 1)
        with dve.Fori(0, NG - 1) as g:
            for j in range(2, NCH):
                weigh(g, j)
            weights_abs(g).then_inc(wabs_done, 1)
            weigh(g + 1, 0)
            weigh(g + 1, 1)
            add_down(g)
        part = 0
        for j in range(2, NCH):
            if j == 4:
                weights_scale()
            weigh(NG - 1, j)
            if j == 2:
                weights_abs(NG - 1).then_inc(wabs_done, 1)
                dve.wait_ge(wabs_done, NG)
                dve.tensor_reduce(wabs[:], wabs_part[:].rearrange("p g i -> p i g"), AX.X, ALU.add).then_inc(wabs_done, 1)
            for _ in range(0 if j < 4 else 2 if j < 6 else 1):
                quantise(part)
                part += 1
        assert part == 12
        add_down(NG - 1)

    @block.gpsimd
    def _(pool):
        pool.dma_start(identb[:], a["ident"]).then_inc(cast_in, 16)
        pool.dma_start(spread[:], a["spread"]).then_inc(cast_in, 16)
        for dst, src in ((decayT, "decayT"), (wo, "wo"), (gamma, "gamma"), (beta, "beta"), (router, "router")):
            pool.dma_start(dst[:], a[src]).then_inc(consts_in, 16)
        pool.memset(half[:], -0.5).then_inc(exponents, 1)
        pool.memset(ones[:], 1.0).then_inc(exponents, 1)
        pool.wait_ge(exponents, 1)

        def s_rstd(t, u):
            norm_rstd(pool, ln, half, t, u)

        def s_wlo(t, u, base=0):
            pool.wait_ge(whi_done[u], t + base + 1)
            pool.tensor_tensor(part(w_lo[:], t, u, base), w_raw[:, u], part(w_hi[:], t, u, base).bitcast(F32), ALU.subtract).then_inc(wlo_done[u], 1)

        def s_wlo2(t, u):
            s_wlo(t, u, NB // 2)

        steps(pool, NB, [(0, s_rstd), (1, s_wlo)])
        pool.wait_ge(router_split, 1)
        pool.tensor_tensor(router_lo[:], router[:], router_hi[:].bitcast(F32), ALU.subtract).then_inc(router_split, 1)

        def s_rstd2(t, u):
            norm_rstd(pool, ln, half, t, u, NB // 2)

        def s_yg(t, u):
            pool.wait_ge(y_done[u], t + 1)
            pool.tensor_tensor(y[:, u], y[:, u], gamma[:], ALU.mult).then_inc(yg_done[u], 1)

        def s_yb(t, u):
            pool.wait_ge(yg_done[u], t + 1)
            pool.tensor_tensor(y[:, u], y[:, u], beta[:], ALU.add).then_inc(yb_done[u], 1)

        def s_grstd(t, u):
            pool.wait_ge(y_done[u], t)
            norm_rstd(pool, gn, half, t, u)

        steps(pool, NB, [(0, s_grstd), (1, s_yg), (5, s_rstd2), (1, s_yb), (2, s_wlo2)])

        for u in range(2):
            pool.sem_inc(actlo_done[u], 1)

        def low(g, j):
            u, n, m = j % 2, 7 * g + j // 2, CH[j]
            pool.wait_ge(acthi_done[u], n + 2)
            pool.tensor_tensor(act_lo[0:m, u], act_f[0:m, u], act_hi[0:m, u].bitcast(F32), ALU.subtract).then_inc(actlo_done[u], 1)

        with pool.Fori(0, NG) as g:
            for j in range(NCH):
                low(g, j)

    @block.scalar
    def _(act):
        act.wait_ge(whwh_done, 1)
        act.activation(whwh[:], two(psV), ACT.Copy).then_inc(wh_ready, 1)

        def s_hT(t, u):
            act.wait_ge(hT_done[u], t + 1)
            act.wait_ge(w_done[u], t)
            act.activation(hT[:, u], two(psT[u]), ACT.Copy).then_inc(hT_copied[u], 1)

        def s_v(t, u):
            act.wait_ge(v_done[u], t + 1)
            act.activation(entry(v[:], t, u), psV[:, 0:D], ACT.Copy).then_inc(v_copied[u], 1)

        def s_r(t, u):
            act.wait_ge(r_done[u], t + 1)
            act.wait_ge(scored[u], t)
            act.activation(r[:, u], two(psR), ACT.Copy).then_inc(r_copied[u], 1)

        def load_wraw(t, u, base=0):
            act.wait_ge(wlo_done[u], t + base)
            act.dma_start(w_raw[:, u], part(a["wpack"], t, u, base)).then_inc(wraw_in[u], 16)

        def s_whi(t, u, base=0):
            act.wait_ge(wraw_in[u], 16 * (t + base + 1))
            act.activation(part(w_hi[:], t, u, base), w_raw[:, u], ACT.Copy).then_inc(whi_done[u], 1)

        def load_wraw2(t, u):
            load_wraw(t, u, NB // 2)

        def s_whi2(t, u):
            s_whi(t, u, NB // 2)

        steps(act, NB, [(0, load_wraw), (1, s_whi), (1, s_v), (1, s_r), (0, s_hT)])
        act.wait_ge(consts_in, 5 * 16)
        act.activation(router_hi[:], router[:], ACT.Copy).then_inc(router_split, 1)

        def s_h2hi(t, u):
            act.wait_ge(h2T_done[u], t + 1)
            act.activation(entry(h2_hi[:], t, u), two(psHT[u]), ACT.Copy).then_inc(h2hi_done[u], 1)

        def s_prodT(t, u):
            act.wait_ge(prodT_done[u], t + 1)
            act.wait_ge(delta_done[u], t)
            act.activation(prodT[:, u], two(psPT), ACT.Copy).then_inc(prodT_copied[u], 1)

        def s_y(t, u):
            act.wait_ge(nmr_done[u], t + 1)
            act.wait_ge(prod_done[u], t)
            act.activation(y[:, u], psO[u][:, 0:D], ACT.Identity, bias=nmr[:, u:u + 1],
                           scale=gn.rstd[:, u:u + 1]).then_inc(y_done[u], 1)

        steps(act, NB, [(7, s_h2hi), (0, s_y), (2, s_prodT), (0, load_wraw2), (1, s_whi2)])
        for u in range(2):
            act.sem_inc(silu_done[u], 1)
            act.sem_inc(acthi_done[u], 1)

        for g in range(NG):
            act.wait_ge(logitsT_done, g + 1)
            act.activation(lgT[:, GT * g:GT * (g + 1)], bank[5 + g % 2][0:NROUTE, :].rearrange("q (b s) -> q b s", b=GT), ACT.Copy).then_inc(logitsT_copied, 1)
        act.wait_ge(routing, ROUTED)
        act.activation(gate, gate, ACT.Tanh).then_inc(tanh_done, 1)

        def silu(g, j):
            u, n, m = j % 2, 7 * g + j // 2, CH[j]
            act.wait_ge(g_done[u], n + 1)
            act.wait_ge(su_done[u], n + 1)
            act.activation(silu_g[0:m, u], psG[u][0:m, :], ACT.Silu).then_inc(silu_done[u], 1)

        def high(g, j):
            u, n, m = j % 2, 7 * g + j // 2, CH[j]
            act.wait_ge(act_done[u], n + 2)
            act.wait_ge(down_done[u], n + 1)
            act.activation(act_hi[0:m, u], act_f[0:m, u], ACT.Copy).then_inc(acthi_done[u], 1)

        with act.Fori(0, NG) as g:
            for j in range(NCH):
                silu(g, j)
                high(g, j)

    @block.tensor
    def _(pe):
        pe.wait_ge(first_in, 4 * 16)
        for k in range(HEADS):
            mm = pe.matmul(psV[:, k * P:(k + 1) * P], whT[:, k], whT[:, k], start=True, stop=True)
        mm.then_inc(whwh_done, 1)
        pe.wait_ge(wh_ready, 1)

        def s_T(t, u):
            pe.wait_ge(ln.h_done[u], t + 1)
            pe.wait_ge(hT_copied[u], t)
            for c in range(DC):
                mm = pe.transpose(psT[u][:, c * P:(c + 1) * P], h[:, u, c * P:(c + 1) * P], ident[:])
            mm.then_inc(hT_done[u], 1)

        def s_v(t, u):
            pe.wait_ge(ctxT_in[u], 16 * (t + 1))
            pe.wait_ge(v_copied[1 - u], t + u)
            for k in range(HEADS):
                mm = pe.matmul(psV[:, k * P:(k + 1) * P], ctxT[:, u, k], wh[:, k], start=True, stop=True)
            mm.then_inc(v_done[u], 1)

        def s_r(t, u):
            pe.wait_ge(hT_copied[u], t + 1)
            pe.wait_ge(r_copied[1 - u], t + u)
            for k in range(HEADS):
                mm = pe.matmul(psR[:, k * P:(k + 1) * P], whwh[:, k], hT[:, u, k], start=True, stop=True)
            mm.then_inc(r_done[u], 1)

        def s_w(t, u):
            pe.wait_ge(w_copied[1 - u], t + u)
            for c in range(DC):
                mm = pe.matmul(psW[:, 0:D], hT[:, u, c], wg[:, c], start=(c == 0), stop=(c == DC - 1))
            mm.then_inc(w_done[u], 1)

        def s_score(t, u):
            pe.wait_ge(r_copied[u], t + 1)
            first = isinstance(t, int) and t == 0 and u == 0
            last = isinstance(t, int) and t == NB // 2 - 1 and u == 1
            for k in range(HEADS):
                mm = pe.matmul(psS[k][:, 0:P], ctxT[:, u, k], r[:, u, k], start=first, stop=last, skip_group_check=True)
            mm.then_inc(scored[u], 1)

        steps(pe, NB, [(0, s_T), (1, s_score), (0, s_v), (0, s_r), (0, s_w)], peel=4)

        def s_h2T(t, u):
            pe.wait_ge(ln.h_done[u], t + NB // 2 + 1)
            pe.wait_ge(h2lo_done[u], t)
            for c in range(DC):
                mm = pe.transpose(psHT[u][:, c * P:(c + 1) * P], h[:, u, c * P:(c + 1) * P], ident[:])
            mm.then_inc(h2T_done[u], 1)

        def s_wo(t, u):
            pe.wait_ge(prodT_copied[u], t + 1)
            pe.wait_ge(x1_done[1 - u], t + u)
            for c in range(DC):
                mm = pe.matmul(psD[:, 0:D], prodT[:, u, c], wo[:, c], start=(c == 0), stop=(c == DC - 1))
            mm.then_inc(delta_done[u], 1)

        def s_pT(t, u):
            pe.wait_ge(prod_done[u], t + 1)
            pe.wait_ge(prodT_copied[1 - u], t + u)
            for c in range(DC):
                mm = pe.transpose(psPT[:, c * P:(c + 1) * P], prod[:, u, c * P:(c + 1) * P], ident[:])
            mm.then_inc(prodT_done[u], 1)

        def s_o(t, u):
            pe.wait_ge(y_done[u], t)
            for k in range(HEADS):
                mm = pe.matmul(psO[u][:, k * HD:(k + 1) * HD], attT[:, k], entry(v[:], t, u)[:, k * HD:(k + 1) * HD],
                               start=True, stop=True)
            mm.then_inc(o_done[u], 1)

        for u in range(2):
            pe.wait_ge(v_copied[u], NB // 2)
            pe.wait_ge(w_copied[u], NB // 2)
        pe.wait_ge(att_done, 1)
        steps(pe, NB, [(4, s_pT), (0, s_o), (4, s_wo), (7, s_h2T)])

        pe.wait_ge(router_split, 2)
        for g in range(NG):
            for u in range(2):
                pe.wait_ge(h2lo_done[u], GT // 2 * (g + 1))
            if g >= 2:
                pe.wait_ge(logitsT_copied, g - 1)
            n = 0
            for c in range(DC):
                for wt, xt in ((router_hi, h2_hi), (router_hi, h2_lo), (router_lo, h2_hi)):
                    mm = pe.matmul(bank[5 + g % 2][:, :], wt[:, c], xt[:, GT * g:GT * (g + 1), c], start=(n == 0), stop=(n == 5))
                    n += 1
            mm.then_inc(logitsT_done, 1)
        pe.wait_ge(logitsT_copied, NG)
        for b in range(NB):
            mm = pe.transpose(bank[7][:, 16 * b:16 * b + NROUTE], lgT[:, b], ident[0:NROUTE, 0:NROUTE])
        mm.then_inc(logits_done, 1)
        for u in range(2):
            pe.sem_inc(down_done[u], 1)

        def up(g, j):
            u, n, m = j % 2, 7 * g + j // 2, CH[j]
            pe.wait_ge(act_done[u], n + 1)
            for ps, base, free, done in ((psG, 0, silu_done, g_done), (psU, DC * HID, su_done, u_done)):
                pe.wait_ge(free[u], n + 1)
                i = 0
                for c in range(DC):
                    cols = base + c * HID + j * P
                    for wt, xt in ((w_hi, h2_hi), (w_hi, h2_lo), (w_lo, h2_hi)):
                        mm = pe.matmul(ps[u][0:m, :], wt[:, cols:cols + m], tokens(xt, g, c), start=(i == 0), stop=(i == 5))
                        i += 1
                mm.then_inc(done[u], 1)

        def spread_gates(g, j):
            u, m = j % 2, CH[j]
            pe.matmul(psC[u][0:m, :], spread[:, j * P:j * P + m], gates[:].rearrange("q (g b) s -> q g (b s)", g=NG)[:, bass.ds(g, 1)].rearrange("q o n -> q (o n)"),
                      start=True, stop=True).then_inc(spread_done[u], 1)

        def down(g, j):
            u, n, m = j % 2, 7 * g + j // 2, CH[j]
            pe.wait_ge(actlo_done[u], n + 2)
            if j == 0:
                pe.wait_ge(x2_done, 2 * g + 1)
            cols = 2 * DC * HID + j * D
            for i in range(GT):
                for q, (at, wt) in enumerate(((act_hi, w_hi), (act_hi, w_lo), (act_lo, w_hi))):
                    mm = pe.matmul(psY[i // 2][:, (i % 2) * D:(i % 2 + 1) * D], at[0:m, u, i * P:(i + 1) * P], wt[0:m, cols:cols + D],
                                   start=(j == 0 and q == 0 and i % 2 == 0), stop=(j == NCH - 1 and q == 2 and i % 2 == 1),
                                   skip_group_check=True)
            mm.then_inc(down_done[u], 1)

        for u in range(2):
            pe.wait_ge(wlo_done[u], NB)
        up(0, 0)
        up(0, 1)
        pe.wait_ge(gate3_done, 1)
        pe.wait_ge(cast_in, 32)
        for b in range(NB):
            mm = pe.transpose(bank[4 + b // 8][0:3 * NROUTE, :].bitcast(BF16)[:, (b % 8) * P:(b % 8 + 1) * P], gate3[:, b], identb[:])
        mm.then_inc(gatesT_done, 1)
        pe.wait_ge(gatesT_copied, 2)

        spread_gates(0, 0)
        spread_gates(0, 1)
        with pe.Fori(0, NG - 1) as g:
            for j in range(2, NCH):
                up(g, j)
                spread_gates(g, j)
                down(g, j - 2)
            for j in range(2):
                up(g + 1, j)
                spread_gates(g + 1, j)
                down(g, NCH - 2 + j)
        for j in range(2, NCH):
            up(NG - 1, j)
            if j == 4:
                pe.wait_ge(exponents, 2)
                pe.wait_ge(wabs_done, NG + 1)
                pe.matmul(psC[0][:, 0:3], ones[:], wabs[:], start=True, stop=True).then_inc(wtotal_done, 1)
                pe.wait_ge(wscale_done, 2)
            spread_gates(NG - 1, j)
            down(NG - 1, j - 2)
        for j in range(2):
            down(NG - 1, NCH - 2 + j)


def last_layers(nc, a, out, core, bank, x, ident, half, late):
    sb, sem, sem2 = core.sb, core.sem, core.sem2
    ctxn, late_w, _, wscale, small, _ = late
    wq = late_w[:].bitcast(BF16)[:, :, 0:IC * D]
    h = sb("h_late", [P, 2, D])
    ln = Norm(core, "ln_late")
    lnq = Norm(core, "ln_quant")
    gphiw, thetaw, projb, gb, outb, lngamma, lnbeta, outw = small
    mean64 = sb("mean64", [LAT, P])
    gphi = sb("gphi", [P, 2, D])
    theta = sb("theta", [P, 2, D])
    gx = sb("gx", [P, 2, 2, LAT])
    negmax = sb("negmax", [P, 2, 2])
    prob = sb("prob", [P, 2, 2, D])
    probsum = sb("probsum", [P, 2, 2])
    probinv = sb("probinv", [P, 2, 2])
    probT = sb("probT", [P, 2, 2, D])
    tx = sb("tx", [LAT, 2, D])
    tstats = sb("tstats", [LAT, 2, 6])
    tmv = sb("tmv", [LAT, 2, 2])
    tall = sb("tall", [LAT, 2, 2])
    tneg = sb("tneg", [LAT, 2])
    tve = sb("tve", [LAT, 2])
    trstd = sb("trstd", [LAT, 2])
    ty = sb("ty", [LAT, 2, D])
    th = sb("th", [P, 2, D])
    xc = sb("xc", [P, 2, D])
    hmax = sb("hmax", [P, 2, 3])
    yscale = sb("yscale", [P, 2, 3])
    qf = sb("qf", [P, 2, D])
    xqT = sb("xqT", [P, 2, DC, P], BF16)
    silu2 = sb("silu2", [P, 2, INNER])
    gu = sb("gu", [P, 2, INNER])
    gus = sb("gus", [P, 2, 4])
    oscale = sb("oscale", [P, 2])
    hqT = sb("hqT", [P, 2, IC, P], BF16)
    x4 = sb("x4", [P, 2, D])
    roundc = sb("roundc", [P, 2])

    late_set = sem("late_set")
    proj_done = sem2("proj_done")
    proj_copied = sem2("proj_copied")
    gx_psum = sem2("gx_psum")
    gx_copied = sem2("gx_copied")
    score_done = sem2("score_done")
    max_done = sem2("max_done")
    exp_done = sem2("exp_done")
    inv_done = sem2("inv_done")
    prob_done = sem2("prob_done")
    probT_done = sem2("probT_done")
    probT_copied = sem2("probT_copied")
    pv_done = sem2("pv_done")
    tx_done = sem2("tx_done")
    tstats_done = sem2("tstats_done")
    tstep = sem2("tstep")
    tmean_done = sem2("tmean_done")
    tve_done = sem2("tve_done")
    trstd_done = sem2("trstd_done")
    ty_done = sem2("ty_done")
    th_done = sem2("th_done")
    out_done = sem2("out_done")
    xc_done = sem2("xc_done")
    x3_done = sem2("x3_done")
    hmax_done = sem2("hmax_done")
    qscale_done = sem2("qscale_done")
    qf_done = sem2("qf_done")
    xqT_done = sem2("xqT_done")
    xqT_copied = sem2("xqT_copied")
    gate_done = sem2("gate_done")
    up_done = sem2("up_done")
    silu2_done = sem2("silu2_done")
    gu_done = sem2("gu_done")
    hqT_done = sem2("hqT_done")
    hqT_copied = sem2("hqT_copied")
    gumax_done = sem2("gumax_done")
    guscale_done = sem2("guscale_done")
    guround_done = sem2("guround_done")
    down2_done = sem2("down2_done")
    x4_done = sem2("x4_done")
    stored = sem2("stored")

    psProj, psScore, psProbT, psTx, psOut, psGx, psMean = bank[0], bank[1:3], bank[3], bank[4], bank[5], bank[6], bank[7]
    psXq, psGate, psUp, psHq, psDown = bank[0], bank[1:3], bank[3:5], bank[5:7], bank[7]

    core.stack.callback(core.end)
    block = core.stack.enter_context(nc.Block())

    @block.sync
    def _(sp):
        def store(t, u):
            sp.wait_ge(x4_done[u], t + 1)
            sp.dma_start(out.rearrange("(t u) p d -> t u p d", u=2)[bass.ds(t, 1), u].rearrange("o p d -> p (o d)"), x4[:, u]).then_inc(stored[u], 16)

        steps(sp, NB, [(0, store)])
        for u in range(2):
            sp.wait_ge(stored[u], 16 * NB // 2)

    @block.vector
    def _(dve):
        dve.memset(mean64[:], 1.0 / LAT).then_inc(late_set, 1)
        dve.memset(th[LAT:P], 0.0).then_inc(late_set, 1)

        def c_stats(t, u):
            norm_stats(dve, ln, entry(x[:], t, u), t, u)

        def c_h(t, u):
            stats_landed(dve, ln, t + u, 1 - u)
            dve.wait_ge(proj_done[u], t)
            normalise(dve, ln, h[:, u], entry(x[:], t, u), t, u)

        def c_aggr(t, u):
            norm_aggr(dve, ln, t, u, LN_EPS)

        def c_max(t, u):
            dve.wait_ge(score_done[u], t + 1)
            dve.wait_ge(exp_done[u], t)
            dve.tensor_reduce(negmax[:, u], two(psScore[u], 512), AX.X, ALU.max, negate=True).then_inc(max_done[u], 1)

        def c_inv(t, u):
            dve.wait_ge(exp_done[u], t + 1)
            dve.wait_ge(prob_done[u], t)
            dve.reciprocal(probinv[:, u], probsum[:, u]).then_inc(inv_done[u], 1)

        def c_tstats(t, u):
            dve.wait_ge(tx_done[u], t + 1)
            dve.bn_stats(tstats[:, u], tx[:, u]).then_inc(tstats_done[u], 1)

        def c_var(t, u):
            if not isinstance(t, int):
                dve.wait_ge(tstats_done[1 - u], t + u + 1)
            dve.wait_ge(tmean_done[u], t + 1)
            dve.tensor_copy(tall[:, u], psMean[0:LAT, 0:2]).then_inc(tstep[u], 1)
            dve.wait_ge(tstep[u], 4 * t + 3)
            dve.scalar_tensor_tensor(out=tneg[:, u:u + 1], in0=tall[:, u, 0:1], scalar=tall[:, u, 0:1], in1=tall[:, u, 1:2],
                                     op0=ALU.mult, op1=ALU.subtract).then_inc(tstep[u], 1)
            dve.wait_ge(tstep[u], 4 * t + 4)
            dve.tensor_scalar(tve[:, u:u + 1], tneg[:, u:u + 1], -1.0, LN_EPS, ALU.mult, ALU.add).then_inc(tve_done[u], 1)

        def c_taggr(t, u):
            if isinstance(t, int):
                dve.wait_ge(tstats_done[u], t + 1)
            dve.bn_aggr(tmv[:, u], tstats[:, u]).then_inc(tstep[u], 1)
            dve.wait_ge(tstep[u], 4 * t + 1)
            dve.scalar_tensor_tensor(out=tmv[:, u, 1:2], in0=tmv[:, u, 0:1], scalar=tmv[:, u, 0:1], in1=tmv[:, u, 1:2],
                                     op0=ALU.mult, op1=ALU.add).then_inc(tstep[u], 1)

        def c_y1(t, u):
            dve.wait_ge(th_done[u], t)
            dve.wait_ge(tstep[u], 4 * t + 3)
            dve.scalar_tensor_tensor(out=ty[:, u], in0=tx[:, u], scalar=tall[:, u, 0:1], in1=lngamma[:],
                                     op0=ALU.subtract, op1=ALU.mult).then_inc(ty_done[u], 1)

        def c_y2(t, u):
            dve.wait_ge(ty_done[u], 2 * t + 1)
            dve.wait_ge(trstd_done[u], t + 1)
            dve.scalar_tensor_tensor(out=ty[:, u], in0=ty[:, u], scalar=trstd[:, u:u + 1], in1=lnbeta[:],
                                     op0=ALU.mult, op1=ALU.add).then_inc(ty_done[u], 1)

        def c_x3(t, u):
            dve.wait_ge(out_done[u], t + 1)
            dve.wait_ge(xc_done[u], t + 1)
            dve.scalar_tensor_tensor(out=entry(x[:], t, u), in0=psOut[:, 0:D], scalar=outb[:, 0:1], in1=xc[:, u],
                                     op0=ALU.add, op1=ALU.add).then_inc(x3_done[u], 1)

        steps(dve, NB, [(6, c_tstats), (7, c_var), (6, c_taggr), (3, c_max), (7, c_y1), (7, c_y2), (0, c_stats), (1, c_h), (0, c_aggr),
                        (3, c_inv), (8, c_x3)])

        def d_stats(t, u):
            norm_stats(dve, lnq, entry(x[:], t, u), t, u)

        def d_h(t, u):
            stats_landed(dve, lnq, t + u, 1 - u)
            dve.wait_ge(qf_done[u], t)
            normalise(dve, lnq, h[:, u], entry(x[:], t, u), t, u)

        def d_aggr(t, u):
            norm_aggr(dve, lnq, t, u, LN_EPS)

        def d_hmax(t, u):
            dve.wait_ge(lnq.h_done[u], t + 1)
            dve.tensor_reduce(hmax[:, u, 0:1], h[:, u], AX.X, ALU.max, apply_absolute_value=True).then_inc(hmax_done[u], 1)

        def d_hscale(t, u):
            dve.wait_ge(hmax_done[u], 3 * t + 1)
            dve.tensor_scalar(hmax[:, u, 1:2], hmax[:, u, 0:1], 1.0 / 127.0, Q_EPS, ALU.mult, ALU.add).then_inc(hmax_done[u], 1)
            dve.wait_ge(hmax_done[u], 3 * t + 2)
            dve.reciprocal(hmax[:, u, 2:3], hmax[:, u, 1:2]).then_inc(hmax_done[u], 1)
            dve.wait_ge(silu2_done[u], 2 * t)
            dve.tensor_scalar(yscale[:, u], wscale[:, 0:3], hmax[:, u, 1:2], None, ALU.mult).then_inc(qscale_done[u], 1)

        def d_gu(k):
            def stage(t, u):
                dve.wait_ge(silu2_done[u], 2 * t + 2 - k)
                dve.wait_ge(up_done[u], t + 1)
                dve.wait_ge(guround_done[u], t)
                dve.tensor_tensor(gu[:, u, k * 512:(k + 1) * 512], psUp[k][:, :], silu2[:, u, k * 512:(k + 1) * 512],
                                  ALU.mult).then_inc(gu_done[u], 1)
            return stage

        def d_gumax(t, u):
            dve.wait_ge(gu_done[u], 2 * t + 2)
            dve.tensor_reduce(gus[:, u, 0:1], gu[:, u], AX.X, ALU.max, apply_absolute_value=True).then_inc(gumax_done[u], 1)

        def d_guscale(t, u):
            dve.wait_ge(gumax_done[u], t + 1)
            dve.wait_ge(qscale_done[u], t + 1)
            dve.tensor_scalar(gus[:, u, 1:2], gus[:, u, 0:1], yscale[:, u, 2:3], Q_EPS, ALU.mult, ALU.add).then_inc(guscale_done[u], 1)
            dve.wait_ge(guscale_done[u], 4 * t + 1)
            dve.reciprocal(gus[:, u, 2:3], gus[:, u, 1:2]).then_inc(guscale_done[u], 1)
            dve.tensor_scalar(oscale[:, u:u + 1], gus[:, u, 1:2], wscale[:, 3:4], None, ALU.mult).then_inc(guscale_done[u], 1)
            dve.wait_ge(guscale_done[u], 4 * t + 3)
            dve.tensor_scalar(gus[:, u, 3:4], gus[:, u, 2:3], yscale[:, u, 1:2], None, ALU.mult).then_inc(guscale_done[u], 1)

        def d_x4(t, u):
            dve.wait_ge(down2_done[u], t + 1)
            dve.wait_ge(stored[u], 16 * t)
            dve.scalar_tensor_tensor(out=x4[:, u], in0=psDown[:, 0:D], scalar=oscale[:, u:u + 1], in1=entry(x[:], t, u),
                                     op0=ALU.mult, op1=ALU.add).then_inc(x4_done[u], 1)

        steps(dve, NB, [(0, d_stats), (1, d_h), (0, d_aggr), (3, d_gumax), (1, d_hmax), (3, d_guscale), (1, d_hscale), (2, d_gu(1)), (2, d_gu(0)), (4, d_x4)])

    @block.gpsimd
    def _(pool):
        pool.memset(roundc[:, 0:1], ROUND).then_inc(late_set, 1)
        pool.memset(roundc[:, 1:2], -ROUND).then_inc(late_set, 1)

        def c_rstd(t, u):
            norm_rstd(pool, ln, half, t, u)

        def c_prob(t, u):
            pool.wait_ge(inv_done[u], t + 1)
            pool.tensor_tensor(prob[:, u], prob[:, u], probinv[:, u].unsqueeze(2).to_broadcast([P, 2, D]), ALU.mult).then_inc(prob_done[u], 1)

        def c_xc(t, u):
            pool.wait_ge(x3_done[u], t)
            pool.tensor_tensor(xc[:, u], entry(x[:], t, u), entry(ctxn[:], t, u), ALU.add).then_inc(xc_done[u], 1)

        def c_trstd(t, u):
            pool.wait_ge(tve_done[u], t + 1)
            pool.tensor_tensor(trstd[:, u:u + 1], tve[:, u:u + 1], half[0:LAT, u:u + 1], ALU.pow).then_inc(trstd_done[u], 1)

        steps(pool, NB, [(0, c_rstd), (2, c_prob), (5, c_trstd), (5, c_xc)])

        def d_rstd(t, u):
            norm_rstd(pool, lnq, half, t, u)

        steps(pool, NB, [(0, d_rstd)])

    @block.scalar
    def _(act):

        def c_gphi(t, u):
            act.wait_ge(proj_done[u], t + 1)
            act.wait_ge(score_done[u], t)
            act.wait_ge(gx_psum[u], t)
            act.activation(gphi[:, u], psProj[:, 0:D], ACT.Identity, bias=projb[:, 1:2]).then_inc(proj_copied[u], 1)

        def c_theta(t, u):
            act.wait_ge(proj_done[u], t + 1)
            act.wait_ge(score_done[u], t)
            act.activation(theta[:, u], psProj[:, D:2 * D], ACT.Identity, bias=projb[:, 0:1]).then_inc(proj_copied[u], 1)

        def c_gx(t, u):
            act.wait_ge(gx_psum[u], t + 1)
            act.wait_ge(pv_done[u], t)
            act.activation(gx[:, u], two(psGx)[:, :, 0:LAT], ACT.Copy).then_inc(gx_copied[u], 1)

        def c_exp(t, u):
            act.wait_ge(max_done[u], t + 1)
            act.wait_ge(probT_done[u], t)
            act.wait_ge(inv_done[u], t)
            for k in range(2):
                op = act.activation(prob[:, u, k], psScore[u][:, k * D:(k + 1) * D], ACT.Exp, bias=negmax[:, u, k:k + 1],
                                    accum_out=probsum[:, u, k:k + 1])
            op.then_inc(exp_done[u], 1)

        def c_probT(t, u):
            act.wait_ge(probT_done[u], t + 1)
            act.wait_ge(pv_done[u], t)
            act.activation(probT[:, u], two(psProbT, 512), ACT.Copy).then_inc(probT_copied[u], 1)

        def c_tx(t, u):
            act.wait_ge(pv_done[u], t + 1)
            act.wait_ge(ty_done[u], 2 * t)
            act.wait_ge(tstats_done[u], t)
            act.activation(tx[:, u], psTx[0:LAT, 0:D], ACT.Identity, bias=gb[:, 0:1]).then_inc(tx_done[u], 1)

        def c_th(t, u):
            act.wait_ge(ty_done[u], 2 * t + 2)
            act.wait_ge(out_done[u], t)
            act.activation(th[0:LAT, u], ty[:, u], ACT.Relu).then_inc(th_done[u], 1)

        steps(act, NB, [(1, c_gphi), (2, c_exp), (4, c_tx), (6, c_th), (3, c_probT), (2, c_gx), (0, c_theta)])

        def d_silu(k):
            def stage(t, u):
                act.wait_ge(gate_done[u], t + 1)
                act.wait_ge(hqT_done[u], 2 * t)
                act.activation(silu2[:, u, k * 512:(k + 1) * 512], psGate[k][:, :], ACT.Silu, scale=yscale[:, u, 0:1]).then_inc(silu2_done[u], 1)
            return stage

        def d_round(t, u):
            act.wait_ge(guscale_done[u], 4 * t + 4)
            act.activation(silu2[:, u], gu[:, u], ACT.Identity, bias=roundc[:, 0:1], scale=gus[:, u, 3:4]).then_inc(guround_done[u], 1)

        def d_qf(t, u):
            act.wait_ge(qscale_done[u], t + 1)
            act.wait_ge(xqT_done[u], t)
            act.activation(qf[:, u], h[:, u], ACT.Identity, bias=roundc[:, 0:1], scale=hmax[:, u, 2:3]).then_inc(qf_done[u], 1)

        def d_xqT(t, u):
            act.wait_ge(xqT_done[u], t + 1)
            act.wait_ge(up_done[u], t)
            act.activation(xqT[:, u], two(psXq), ACT.Identity, bias=roundc[:, 1:2]).then_inc(xqT_copied[u], 1)

        def d_hqT(k):
            def stage(t, u):
                act.wait_ge(hqT_done[u], 2 * t + 2 - k)
                act.wait_ge(down2_done[u], t)
                act.activation(hqT[:, u, 4 * k:4 * (k + 1)], psHq[k][:, :].rearrange("p (c n) -> p c n", c=4), ACT.Identity,
                               bias=roundc[:, 1:2]).then_inc(hqT_copied[u], 1)
            return stage

        act.wait_ge(late_set, 4)
        steps(act, NB, [(3, d_hqT(1)), (3, d_hqT(0)), (1, d_silu(1)), (1, d_silu(0)), (2, d_round), (0, d_qf), (0, d_xqT)])

    @block.tensor
    def _(pe):
        pe.wait_ge(late_set, 4)


        def c_theta(t, u):
            pe.wait_ge(proj_copied[1 - u], 2 * (t + u))
            pe.matmul(psProj[:, D:2 * D], thetaw[:], entry(ctxn[:], t, u), start=True, stop=True)

        def c_gphi(t, u):
            pe.wait_ge(ln.h_done[u], t + 1)
            pe.matmul(psProj[:, 0:D], gphiw[:], h[:, u], start=True, stop=True).then_inc(proj_done[u], 1)

        def c_gx(t, u):
            pe.wait_ge(proj_copied[u], 2 * t + 2)
            pe.wait_ge(gx_copied[1 - u], t + u)
            for k in range(2):
                mm = pe.transpose(psGx[:, k * P:(k + 1) * P], gphi[:, u, k * P:(k + 1) * P], ident[:])
            mm.then_inc(gx_psum[u], 1)

        def c_score(t, u):
            pe.wait_ge(proj_copied[u], 2 * t + 2)
            pe.wait_ge(exp_done[u], t)
            for k in range(2):
                mm = pe.matmul(psScore[u][:, k * D:(k + 1) * D], theta[:, u, k * P:(k + 1) * P], gphi[:, u], start=True, stop=True)
            mm.then_inc(score_done[u], 1)

        def c_probT(t, u):
            pe.wait_ge(prob_done[u], t + 1)
            pe.wait_ge(probT_copied[1 - u], t + u)
            for sh in range(2):
                for th_ in range(2):
                    mm = pe.transpose(psProbT[:, sh * D + th_ * P:sh * D + (th_ + 1) * P], prob[:, u, th_, sh * P:(sh + 1) * P], ident[:])
            mm.then_inc(probT_done[u], 1)

        def c_pv(t, u):
            pe.wait_ge(probT_copied[u], t + 1)
            pe.wait_ge(gx_copied[u], t + 1)
            pe.wait_ge(tx_done[1 - u], t + u)
            for k in range(2):
                mm = pe.matmul(psTx[0:LAT, 0:D], gx[:, u, k], probT[:, u, k], start=(k == 0), stop=(k == 1))
            mm.then_inc(pv_done[u], 1)

        def c_mean(t, u):
            pe.wait_ge(tstep[u], 4 * t + 2)
            pe.wait_ge(tve_done[1 - u], t + u)
            pe.matmul(psMean[:, 0:2], mean64[:], tmv[:, u], start=True, stop=True).then_inc(tmean_done[u], 1)

        def c_out(t, u):
            pe.wait_ge(th_done[u], t + 1)
            pe.wait_ge(x3_done[1 - u], t + u)
            pe.matmul(psOut[:, 0:D], outw[:], th[:, u], start=True, stop=True).then_inc(out_done[u], 1)

        steps(pe, NB, [(4, c_pv), (3, c_probT), (0, c_theta), (5, c_mean), (0, c_gphi), (1, c_score), (1, c_gx), (6, c_out)])

        for u in range(2):
            pe.wait_ge(x3_done[u], NB // 2)

        def d_xqT(t, u):
            pe.wait_ge(qf_done[u], t + 1)
            pe.wait_ge(xqT_copied[1 - u], t + u)
            for c in range(DC):
                mm = pe.transpose(psXq[:, c * P:(c + 1) * P], qf[:, u, c * P:(c + 1) * P], ident[:])
            mm.then_inc(xqT_done[u], 1)

        def both(ps, i, u):
            for k in range(2):
                for c in range(DC):
                    mm = pe.matmul(ps[k][:, :], xqT[:, u, c], wq[:, i, c * INNER + k * 512:c * INNER + (k + 1) * 512],
                                   start=(c == 0), stop=(c == DC - 1))
            return mm

        def d_gate(t, u):
            pe.wait_ge(xqT_copied[u], t + 1)
            pe.wait_ge(silu2_done[1 - u], 2 * (t + u))
            both(psGate, 0, u).then_inc(gate_done[u], 1)

        def d_up(t, u):
            pe.wait_ge(gu_done[1 - u], 2 * (t + u))
            both(psUp, 1, u).then_inc(up_done[u], 1)

        def d_hqT(k):
            def stage(t, u):
                pe.wait_ge(guround_done[u], t + 1)
                pe.wait_ge(hqT_copied[1 - u], 2 * (t + u))
                for c in range(4):
                    n = (4 * k + c) * P
                    mm = pe.transpose(psHq[k][:, c * P:(c + 1) * P], silu2[:, u, n:n + P], ident[:])
                mm.then_inc(hqT_done[u], 1)
            return stage

        def d_down(t, u):
            pe.wait_ge(hqT_copied[u], 2 * t + 2)
            pe.wait_ge(x4_done[1 - u], t + u)
            for c in range(IC):
                mm = pe.matmul(psDown[:, 0:D], hqT[:, u, c], wq[:, 2, c * D:(c + 1) * D], start=(c == 0), stop=(c == IC - 1))
            mm.then_inc(down2_done[u], 1)

        steps(pe, NB, [(1, d_up), (3, d_down), (2, d_hqT(1)), (0, d_xqT), (2, d_hqT(0)), (0, d_gate)])


def kernel(x, ctx_2048, L0_xattn_Wh, L0_xattn_wg_w, L0_xattn_wo_w, L0_xattn_gn_gamma, L0_xattn_gn_beta,
           L0_ffn_gate_w, L0_ffn_w_gate, L0_ffn_w_up, L0_ffn_w_down, L0_ffn_shgate_w, L0_ffn_shw_gate,
           L0_ffn_shw_up, L0_ffn_shw_down, L1_xattn_theta_w, L1_xattn_theta_b, L1_xattn_phi_w,
           L1_xattn_phi_b, L1_xattn_g_w, L1_xattn_g_b, L1_xattn_ln_gamma, L1_xattn_ln_beta,
           L1_xattn_out_w, L1_xattn_out_b, L1_ffn_w_gate, L1_ffn_w_up, L1_ffn_w_down):
    import numpy as np
    import concourse.bacc as bacc
    from concourse.bass_utils import run_bass_kernel_spmd

    arr = np.asarray
    c = np.ascontiguousarray

    def rows(m):
        return c(m.reshape(-1, P, m.shape[1]).transpose(1, 0, 2))

    def side(experts, shared):
        return np.concatenate([arr(experts).transpose(1, 0, 2).reshape(D, -1), arr(shared)], 1)

    down = np.concatenate([arr(L0_ffn_w_down).reshape(-1, D), arr(L0_ffn_shw_down), np.zeros((NCH * P - HID, D), np.float32)], 0)
    gates = np.concatenate([arr(L0_ffn_gate_w), arr(L0_ffn_shgate_w)[None], np.zeros((P - NROUTE, D), np.float32)], 0)
    wh = arr(L0_xattn_Wh)
    none = np.zeros((P, P - LAT), np.float32)
    arrays = {
        "x": c(arr(x)), "ctx": c(arr(ctx_2048)),
        "ctxT": c(arr(ctx_2048).reshape(NB, P, HEADS, HD).transpose(3, 0, 2, 1)),
        "wh": c(wh.transpose(1, 0, 2)), "whT": c(wh.transpose(2, 0, 1)),
        "wg": rows(arr(L0_xattn_wg_w)), "wo": rows(arr(L0_xattn_wo_w)),
        "gamma": c(np.broadcast_to(arr(L0_xattn_gn_gamma), (P, D))),
        "beta": c(np.broadcast_to(arr(L0_xattn_gn_beta), (P, D))),
        "wpack": c(np.concatenate([rows(m).reshape(P, -1) for m in
                                   (side(L0_ffn_w_gate, L0_ffn_shw_gate), side(L0_ffn_w_up, L0_ffn_shw_up), down)], 1)),
        "router": rows(c(gates.T)),
        "thetaw": c(np.concatenate([none, arr(L1_xattn_theta_w).T], 1)),
        "gphiw": c(np.concatenate([arr(L1_xattn_g_w).T, arr(L1_xattn_phi_w).T], 1)),
        "outw": c(np.concatenate([arr(L1_xattn_out_w).T, none.T], 0)),
        "projb": c(np.stack([np.concatenate([none[0], arr(b)]) for b in (L1_xattn_theta_b, L1_xattn_phi_b)], 1)),
        "gb": c(arr(L1_xattn_g_b)[:, None]), "outb": c(arr(L1_xattn_out_b)[:, None]),
        "lngamma": c(arr(L1_xattn_ln_gamma)), "lnbeta": c(arr(L1_xattn_ln_beta)),
        "qgate": rows(arr(L1_ffn_w_gate).T), "qup": rows(arr(L1_ffn_w_up).T), "qdown": rows(arr(L1_ffn_w_down).T),
        **constants(),
    }
    nc = bacc.Bacc("TRN2", target_bir_lowering=False, num_devices=1)
    aps = {k: nc.dram_tensor(f"in_{k}", m.shape, mybir.dt.from_np(m.dtype), kind="ExternalInput").ap() for k, m in arrays.items()}
    out = nc.dram_tensor("out", (NB, P, D), F32, kind="ExternalOutput").ap()
    program(nc, aps, out)
    r = run_bass_kernel_spmd(nc, [{f"in_{k}": m for k, m in arrays.items()}], core_ids=[0])
    return r.results[0]["out"]


def constants():
    import numpy as np

    gamma = 1.0 - 2.0 ** (-5.0 - np.arange(HEADS))
    late = np.arange(P)[None, :] - np.arange(P)[:, None]
    mask = np.where(late[None] <= 0, gamma[:, None, None] ** late[None].astype(np.float64), 0.0)
    mask = mask / np.sqrt(mask.sum(-1))[:, None, :]
    spread = np.zeros((3, NROUTE, NCH * P), np.float32)
    for e in range(NE):
        spread[:, e, e * HE:(e + 1) * HE] = 1.0
    spread[:, NE, NE * HE:HID] = 1.0
    return {
        "ident": np.eye(P, dtype=np.float32),
        "decayT": np.ascontiguousarray((mask / np.sqrt(HD)).transpose(2, 0, 1).astype(np.float32)),
        "spread": spread.reshape(3 * NROUTE, NCH * P),
    }
```
